# Optimizing a Trainium2 kernel written in Bass

```python
import numpy as np
import jax
import jax.numpy as jnp

def _softmax(x, axis=-1):
    return jax.nn.softmax(x, axis=axis)

def _gelu(x):
    return jax.nn.gelu(x, approximate=True)

def _silu(x):
    return jax.nn.silu(x)

def _sigmoid(x):
    return jax.nn.sigmoid(x)

def _layernorm(x, axis=-1, eps=1e-05):
    m = jnp.mean(x, axis=axis, keepdims=True)
    v = jnp.var(x, axis=axis, keepdims=True)
    return (x - m) / jnp.sqrt(v + eps)

def _scatter_add(tgt, idx, src, axis=0):
    return tgt.at[idx].add(src)

def _segment_sum(src, seg, n):
    return jax.ops.segment_sum(src, seg, n)
kernel_name = 'mk_flamingo_gated_d2_seqx_r8_b68cca'

def setup_inputs(seed: int=0):
    np.random.seed(seed)
    _w = jnp.asarray

    def _rec_inputs():
        import jax
        import jax.numpy as jnp
        _rk = jax.random.key(seed)
        x = -0.0002928 + 1 * jax.random.normal(jax.random.fold_in(_rk, 1), (8, 128, 128), jnp.float32)
        _lenS = 128 - jax.random.randint(jax.random.fold_in(_rk, 7), (8,), 0, max(1, 128 // 4) + 1, jnp.int32)
        _lenS2 = 77 - jax.random.randint(jax.random.fold_in(_rk, 8), (8,), 0, max(1, 77 // 4) + 1, jnp.int32)
        _ctx_768P = jax.random.normal(jax.random.fold_in(_rk, 11), (8, 16, 96), jnp.float32)
        _ctx_768c = jax.random.dirichlet(jax.random.fold_in(_rk, 511), 0.3 * jnp.ones((16,), jnp.float32), (8, 77))
        _ctx_768t = jnp.einsum('bsk,bkd->bsd', _ctx_768c, _ctx_768P)
        _ctx_768t = _ctx_768t * jax.lax.rsqrt(jnp.mean(jnp.square(_ctx_768t)) + 1e-12) * 0.953939
        ctx_768 = 2.09791e-05 + 1.00001 * (_ctx_768t + 0.3 * jax.random.normal(jax.random.fold_in(_rk, 611), (8, 77, 96), jnp.float32))
        _g = jax.random.normal(jax.random.fold_in(_rk, 9001), (2, 2), jnp.float32)
        _g = jnp.sign(_g) * jnp.maximum(jnp.abs(_g), 1.0) + (_g == 0) * 1.0
        g_xattn = _g[0]
        g_ffn = _g[1]
        return (x, ctx_768, g_xattn, g_ffn)
    x, ctx_768, g_xattn, g_ffn = _rec_inputs()

    def _L0_xattn_setup():
        import jax, jax.numpy as jnp
        import numpy as np
        HEADS = 8
        DIM_HEAD = 128
        ATTN_MATRIX_SCALE = 1.5
        SCALE = DIM_HEAD ** (-0.5)

        def _split_heads(t):
            b, n, _ = t.shape
            t = t.reshape(b, n, HEADS, DIM_HEAD)
            return t.transpose(2, 0, 1, 3).reshape(HEADS, b * n, DIM_HEAD)
        key = jax.random.key(seed)
        ks = jax.random.split(key, 7)
        b, n, m = (2, 256, 256)
        qd, cd, inner = (128, 96, HEADS * DIM_HEAD)
        x = jax.random.normal(ks[0], (b, n, qd), dtype=jnp.float32)
        context = jax.random.normal(ks[1], (b, m, cd), dtype=jnp.float32)
        Wq = jax.random.normal(ks[2], (qd, inner), dtype=jnp.float32) * qd ** (-0.5)
        Wk = jax.random.normal(ks[3], (cd, inner), dtype=jnp.float32) * cd ** (-0.5)
        Wv = jax.random.normal(ks[4], (cd, inner), dtype=jnp.float32) * cd ** (-0.5)
        Wout = jax.random.normal(ks[5], (inner, qd), dtype=jnp.float32) * inner ** (-0.5)
        bout = jnp.zeros((qd,), dtype=jnp.float32)
        return {'x': x, 'context': context, 'Wq': Wq, 'Wk': Wk, 'Wv': Wv, 'Wout': Wout, 'bout': bout}
    _L0_xattn_all = _L0_xattn_setup()
    _L0_xattn_in = {k: v for k, v in _L0_xattn_all.items() if k in ('Wq', 'Wk', 'Wv', 'Wout', 'bout')}
    del _L0_xattn_all

    def _L0_ffn_setup():
        import math
        import jax, jax.numpy as jnp
        import numpy as np
        TOP_K = 2
        CAP_FACTOR = 1.25
        CLAMP = 10000.0
        key = jax.random.key(seed)
        k1, k2, k3, k4, k5 = jax.random.split(key, 5)
        B, S, D, F, E = (4, 256, 128, 512, 8)
        std = 0.02
        return {'x': jax.random.normal(k1, (B, S, D), dtype=jnp.float32), 'Wr': jax.random.normal(k2, (D, E), dtype=jnp.float32) * std, 'W1': jax.random.normal(k3, (E, D, F), dtype=jnp.float32) * std, 'W3': jax.random.normal(k4, (E, D, F), dtype=jnp.float32) * std, 'W2': jax.random.normal(k5, (E, F, D), dtype=jnp.float32) * std}
    _L0_ffn_all = _L0_ffn_setup()
    _L0_ffn_in = {k: v for k, v in _L0_ffn_all.items() if k in ('Wr', 'W1', 'W3', 'W2')}
    del _L0_ffn_all

    def _L1_xattn_setup():
        import jax, jax.numpy as jnp
        import numpy as np
        HEADS = 16
        DIM_HEAD = 64
        SCALE = DIM_HEAD ** (-0.5)
        QUERY_DIM = 128
        CONTEXT_DIM = 96
        INNER_DIM = HEADS * DIM_HEAD
        key = jax.random.key(seed)
        ks = jax.random.split(key, 7)
        B, Nq, Nk = (8, 512, 77)
        x = jax.random.normal(ks[0], (B, Nq, QUERY_DIM), dtype=jnp.float32)
        context = jax.random.normal(ks[1], (B, Nk, CONTEXT_DIM), dtype=jnp.float32)
        Wq = jax.random.normal(ks[2], (QUERY_DIM, INNER_DIM), dtype=jnp.float32) * QUERY_DIM ** (-0.5)
        Wk = jax.random.normal(ks[3], (CONTEXT_DIM, INNER_DIM), dtype=jnp.float32) * CONTEXT_DIM ** (-0.5)
        Wv = jax.random.normal(ks[4], (CONTEXT_DIM, INNER_DIM), dtype=jnp.float32) * CONTEXT_DIM ** (-0.5)
        Wo = jax.random.normal(ks[5], (INNER_DIM, QUERY_DIM), dtype=jnp.float32) * INNER_DIM ** (-0.5)
        bo = jnp.zeros((QUERY_DIM,), dtype=jnp.float32)
        return {'x': x, 'context': context, 'Wq': Wq, 'Wk': Wk, 'Wv': Wv, 'Wo': Wo, 'bo': bo}
    _L1_xattn_all = _L1_xattn_setup()
    _L1_xattn_in = {k: v for k, v in _L1_xattn_all.items() if k in ('Wq', 'Wk', 'Wv', 'Wo', 'bo')}
    del _L1_xattn_all

    def _L1_ffn_setup():
        import jax, jax.numpy as jnp
        import numpy as np
        B, S, H = (2, 128, 128)
        E, F = (8, 512)
        GATE_TEMP = 0.1
        key = jax.random.key(seed)
        ks = jax.random.split(key, 6)
        s_h = 1.0 / np.sqrt(H)
        s_f = 1.0 / np.sqrt(F)
        return {'hidden_states': jax.random.normal(ks[0], (B, S, H), dtype=jnp.float32), 'w_router': jax.random.normal(ks[1], (H, E), dtype=jnp.float32) * s_h, 'w_gating': jax.random.normal(ks[2], (H, E), dtype=jnp.float32) * s_h, 'w_gate': jax.random.normal(ks[3], (E, H, F), dtype=jnp.float32) * s_h, 'w_up': jax.random.normal(ks[4], (E, H, F), dtype=jnp.float32) * s_h, 'w_down': jax.random.normal(ks[5], (E, F, H), dtype=jnp.float32) * s_f}
    _L1_ffn_all = _L1_ffn_setup()
    _L1_ffn_in = {k: v for k, v in _L1_ffn_all.items() if k in ('w_router', 'w_gating', 'w_gate', 'w_up', 'w_down')}
    del _L1_ffn_all
    return {'x': x, 'ctx_768': ctx_768, 'g_xattn': g_xattn, 'g_ffn': g_ffn, 'L0_xattn_Wq': _L0_xattn_in['Wq'], 'L0_xattn_Wk': _L0_xattn_in['Wk'], 'L0_xattn_Wv': _L0_xattn_in['Wv'], 'L0_xattn_Wout': _L0_xattn_in['Wout'], 'L0_xattn_bout': _L0_xattn_in['bout'], 'L0_ffn_Wr': _L0_ffn_in['Wr'], 'L0_ffn_W1': _L0_ffn_in['W1'], 'L0_ffn_W3': _L0_ffn_in['W3'], 'L0_ffn_W2': _L0_ffn_in['W2'], 'L1_xattn_Wq': _L1_xattn_in['Wq'], 'L1_xattn_Wk': _L1_xattn_in['Wk'], 'L1_xattn_Wv': _L1_xattn_in['Wv'], 'L1_xattn_Wo': _L1_xattn_in['Wo'], 'L1_xattn_bo': _L1_xattn_in['bo'], 'L1_ffn_w_router': _L1_ffn_in['w_router'], 'L1_ffn_w_gating': _L1_ffn_in['w_gating'], 'L1_ffn_w_gate': _L1_ffn_in['w_gate'], 'L1_ffn_w_up': _L1_ffn_in['w_up'], 'L1_ffn_w_down': _L1_ffn_in['w_down']}

def reference(x, ctx_768, g_xattn, g_ffn, L0_xattn_Wq, L0_xattn_Wk, L0_xattn_Wv, L0_xattn_Wout, L0_xattn_bout, L0_ffn_Wr, L0_ffn_W1, L0_ffn_W3, L0_ffn_W2, L1_xattn_Wq, L1_xattn_Wk, L1_xattn_Wv, L1_xattn_Wo, L1_xattn_bo, L1_ffn_w_router, L1_ffn_w_gating, L1_ffn_w_gate, L1_ffn_w_up, L1_ffn_w_down):
    import jax
    import jax.numpy as jnp

    def _L0_xattn_ref(x, context, Wq, Wk, Wv, Wout, bout):
        import jax, jax.numpy as jnp
        import numpy as np
        HEADS = 8
        DIM_HEAD = 128
        ATTN_MATRIX_SCALE = 1.5
        SCALE = DIM_HEAD ** (-0.5)

        def _split_heads(t):
            b, n, _ = t.shape
            t = t.reshape(b, n, HEADS, DIM_HEAD)
            return t.transpose(2, 0, 1, 3).reshape(HEADS, b * n, DIM_HEAD)
        b, n, _ = x.shape
        qh = _split_heads(jnp.einsum('bnq,qi->bni', x, Wq))
        kh = _split_heads(jnp.einsum('bmc,ci->bmi', context, Wk))
        vh = _split_heads(jnp.einsum('bmc,ci->bmi', context, Wv))
        sim = jnp.einsum('hid,hjd->hij', qh, kh) * SCALE
        mean = jnp.mean(sim, axis=-1, keepdims=True)
        sim = (sim - mean) * ATTN_MATRIX_SCALE + mean
        attn = jax.nn.softmax(sim, axis=-1)
        out = jnp.einsum('hij,hjd->hid', attn, vh)
        out = out.reshape(HEADS, b, n, DIM_HEAD).transpose(1, 2, 0, 3)
        out = out.reshape(b, n, HEADS * DIM_HEAD)
        return jnp.einsum('bni,iq->bnq', out, Wout) + bout

    def _L0_ffn_ref(x, Wr, W1, W3, W2):
        import math
        import jax, jax.numpy as jnp
        import numpy as np
        TOP_K = 2
        CAP_FACTOR = 1.25
        CLAMP = 10000.0
        B, S, D = x.shape
        E = Wr.shape[1]
        K = TOP_K
        T = B * S
        cap = max(1, math.ceil(T * K * CAP_FACTOR / E))
        xf = x.reshape(T, D)
        logits = jnp.clip(xf @ Wr, -CLAMP, CLAMP)
        top_v, top_i = jax.lax.top_k(logits, K)
        m = jnp.max(top_v, axis=-1, keepdims=True)
        expv = jnp.exp(top_v - m)
        top_p = expv / (jnp.sum(expv, axis=-1, keepdims=True) + 1e-12)
        Sp = T * K
        experts = top_i.reshape(Sp)
        weights = top_p.reshape(Sp)
        tokens = jnp.repeat(jnp.arange(T), K)
        oh = experts[:, None] == jnp.arange(E)[None, :]
        pos = jnp.sum(jnp.cumsum(oh.astype(jnp.int32), axis=0) * oh, axis=-1) - 1
        kept = pos < cap
        pos_safe = jnp.where(kept, pos, cap)
        xe = jnp.zeros((E, cap + 1, D), x.dtype).at[experts, pos_safe].set(xf[tokens])[:, :cap]
        h = jax.nn.silu(jnp.einsum('ecd,edf->ecf', xe, W1)) * jnp.einsum('ecd,edf->ecf', xe, W3)
        ye = jnp.einsum('ecf,efd->ecd', h, W2)
        yp = ye[experts, jnp.minimum(pos_safe, cap - 1)]
        wk = weights * kept.astype(weights.dtype)
        out = jnp.zeros((T, D), x.dtype).at[tokens].add(wk[:, None] * yp)
        return out.reshape(B, S, D)

    def _L1_xattn_ref(x, context, Wq, Wk, Wv, Wo, bo):
        import jax, jax.numpy as jnp
        import numpy as np
        HEADS = 16
        DIM_HEAD = 64
        SCALE = DIM_HEAD ** (-0.5)
        QUERY_DIM = 128
        CONTEXT_DIM = 96
        INNER_DIM = HEADS * DIM_HEAD
        B, Nq, _ = x.shape
        Nk = context.shape[1]
        q = x @ Wq
        k = context @ Wk
        v = context @ Wv
        q = q.reshape(B, Nq, HEADS, DIM_HEAD).transpose(0, 2, 1, 3)
        k = k.reshape(B, Nk, HEADS, DIM_HEAD).transpose(0, 2, 1, 3)
        v = v.reshape(B, Nk, HEADS, DIM_HEAD).transpose(0, 2, 1, 3)
        sim = jnp.einsum('bhid,bhjd->bhij', q, k) * SCALE
        attn = jax.nn.softmax(sim, axis=-1)
        out = jnp.einsum('bhij,bhjd->bhid', attn, v)
        out = out.transpose(0, 2, 1, 3).reshape(B, Nq, INNER_DIM)
        return out @ Wo + bo

    def _L1_ffn_ref(hidden_states, w_router, w_gating, w_gate, w_up, w_down):
        import jax, jax.numpy as jnp
        import numpy as np
        B, S, H = (2, 128, 128)
        E, F = (8, 512)
        GATE_TEMP = 0.1
        x = hidden_states
        router_probs = jax.nn.softmax(jnp.einsum('bsh,he->bse', x, w_router), axis=-1)
        gate_weights = jax.nn.softmax(jnp.einsum('bsh,he->bse', x, w_gating) / GATE_TEMP, axis=-1)
        g = jnp.einsum('bsh,ehf->ebsf', x, w_gate)
        u = jnp.einsum('bsh,ehf->ebsf', x, w_up)
        h = jax.nn.silu(g) * u
        expert_out = jnp.einsum('ebsf,efh->ebsh', h, w_down)
        cw = router_probs * gate_weights
        cw = cw / (jnp.sum(cw, axis=-1, keepdims=True) + 1e-09)
        out = jnp.einsum('ebsh,bse->bsh', expert_out, cw)
        return out
    x = x + jnp.tanh(g_xattn[0]) * _L0_xattn_ref(_layernorm(x, axis=-1), ctx_768, L0_xattn_Wq, L0_xattn_Wk, L0_xattn_Wv, L0_xattn_Wout, L0_xattn_bout)
    x = x + jnp.tanh(g_ffn[0]) * _L0_ffn_ref(_layernorm(x, axis=-1), L0_ffn_Wr, L0_ffn_W1, L0_ffn_W3, L0_ffn_W2)
    x = x + jnp.tanh(g_xattn[1]) * _L1_xattn_ref(_layernorm(x, axis=-1), ctx_768, L1_xattn_Wq, L1_xattn_Wk, L1_xattn_Wv, L1_xattn_Wo, L1_xattn_bo)
    x = x + jnp.tanh(g_ffn[1]) * _L1_ffn_ref(_layernorm(x, axis=-1), L1_ffn_w_router, L1_ffn_w_gating, L1_ffn_w_gate, L1_ffn_w_up, L1_ffn_w_down)
    return x

_drawn_inputs = setup_inputs


def setup_inputs(seed=0):
    import zlib

    import numpy as np

    out = dict(_drawn_inputs(seed))
    spreads = {'g_ffn': (-1.0, 0.556), 'L0_xattn_bout': (0.0, 0.1), 'L1_xattn_bo': (0.0, 0.295)}
    factors = {'L0_ffn_Wr': 8.0, 'L0_ffn_W1': 7.239, 'L0_ffn_W3': 7.282, 'L0_ffn_W2': 7.225}
    for name, (base, spread) in spreads.items():
        noise = np.random.default_rng([zlib.crc32(name.encode()), seed]).standard_normal(out[name].shape)
        drawn = base * np.exp(spread * noise) if base else spread * noise
        out[name] = jnp.asarray(drawn.astype(out[name].dtype))
    for name, factor in factors.items():
        out[name] = (out[name] * factor).astype(out[name].dtype)
    return out
```

```python
from contextlib import ExitStack

import numpy as np

import concourse.bass as bass
from concourse import mybir

F32 = mybir.dt.float32
F32R = mybir.dt.float32r
BF16 = mybir.dt.bfloat16
U32 = mybir.dt.uint32
ALU = mybir.AluOpType
ACT = mybir.ActivationFunctionType
AX = mybir.AxisListType

P = 128
D = 128
C = 96
B, S, M = 8, 128, 77
T = B * S
TT = T // P
KEYS = B * M
KT = -(-KEYS // P)
KLAST = KEYS - (KT - 1) * P
H0, DH0 = 8, 128
H1, DH1 = 16, 64
E, F = 8, 512
FT = F // P
TOPK = 2
CAP = max(1, -(-T * TOPK * 5 // (4 * E)))
SLOTS = E * CAP
EPS = 1e-5
BANK = 512
SCALE0 = 1.5 * DH0 ** -0.5
SCALE1 = DH1 ** -0.5


def f32(ap):
    return ap.bitcast(F32)


class Split:

    def __init__(self, hi, lo):
        self.hi, self.lo = hi, lo

    def __getitem__(self, at):
        return Split(self.hi[at], self.lo[at])

    def view(self, pattern, **sizes):
        return Split(self.hi.rearrange(pattern, **sizes), self.lo.rearrange(pattern, **sizes))


def matmul3(pe, out, lhsT, rhs, start=True, stop=True):
    pe.matmul(out, lhsT.hi, rhs.hi, start=start, stop=False)
    pe.matmul(out, lhsT.hi, rhs.lo, start=False, stop=False)
    return pe.matmul(out, lhsT.lo, rhs.hi, start=False, stop=stop)


class Core:

    def __init__(self, nc, stack):
        self.nc, self.stack = nc, stack

    def scope(self, stack):
        return Core(self.nc, stack)

    def sb(self, name, shape, dt=F32):
        return self.stack.enter_context(self.nc.sbuf_tensor("sb_" + name, shape, dt))

    def split(self, name, shape):
        return Split(self.sb(name + "_hi", shape, F32R)[:], self.sb(name + "_lo", shape, F32R)[:])

    def sem(self, name):
        return self.stack.enter_context(self.nc.semaphore(name))


def wait(eng, sem, value):
    if not (isinstance(value, int) and value <= 0):
        eng.wait_ge(sem, value)


class Chain:

    def __init__(self, eng, sem):
        self.eng, self.sem, self.n = eng, sem, 0

    def __call__(self, instruction):
        self.n += 1
        instruction.then_inc(self.sem, 1)
        self.eng.wait_ge(self.sem, self.n)
        return instruction


def layernorm_stats(dve, step, x, stats, moments, variance_eps):
    for t in range(TT):
        last = dve.bn_stats(stats[:, t, :], x[:, t, :])
    step(last)
    for t in range(TT):
        last = dve.bn_aggr(moments[:, t, :], stats[:, t, :])
    step(last)
    return dve.tensor_scalar(variance_eps[:], moments[:, :, 1], EPS, None, ALU.add)


def layernorm_apply(dve, x, moments, rstd, xn):
    for t in range(TT):
        last = dve.tensor_scalar(xn[:, t, :], x[:, t, :], moments[:, t, 0:1], rstd[:, t:t + 1],
                                 ALU.subtract, ALU.mult)
    return last


def prepare0(core, g, io):
    nc = core.nc
    with ExitStack() as stack:
        c = core.scope(stack)
        wq = c.sb("wq0", [P, H0 * DH0])
        wk = c.sb("wk0", [C, H0 * DH0])
        wv = c.sb("wv0", [C, H0 * DH0])
        wout = c.sb("wout0", [P, H0, D])
        ctx_rows = c.sb("ctx_rows", [P, KT, C])
        wqT, wkT, wvT = (c.split(n, [P, H0, w]) for n, w in (("wq0T", D), ("wk0T", C), ("wv0T", C)))
        wout_s = c.split("wout0s", [P, H0, D])
        qk = c.split("qk0", [C, H0, D])
        vo = c.split("vo0", [C, H0 * D])
        xn = c.sb("xn_first", [P, TT, D])
        stats = c.sb("ln_stats0", [P, TT, 6])
        moments = c.sb("ln_moments0", [P, TT, 2])
        var_eps = c.sb("ln_var0", [P, TT])
        rstd = c.sb("ln_rstd0", [P, TT])
        gates_raw = c.sb("gates_raw", [P, 4])

        loaded = {n: c.sem("a_ld_" + n) for n in ("x", "ctx", "wq", "wk", "wv", "wout", "small")}
        ident_done, zero_done = c.sem("a_ident"), c.sem("a_zero")
        var_done, rstd_done, xn_done = c.sem("a_var"), c.sem("a_rstd"), c.sem("a_xn")
        pe_done, hi_done, lo_done = c.sem("a_pe"), c.sem("a_hi"), c.sem("a_lo")
        wout_hi, wout_lo, dve_step = c.sem("a_wouthi"), c.sem("a_woutlo"), c.sem("a_dve")

        CTX, WQ, WK, WV, QK, VO, XN = range(7)
        K0 = 7
        V0 = K0 + H0
        JOBS = V0 + KT

        def slot(j):
            return g.psum[:, 2 * (j % 4):2 * (j % 4) + 2, :].rearrange("p b n -> p (b n)")

        def evacuation(j):
            ps = slot(j)
            if j == CTX:
                return ps[0:C, 0:KEYS], g.ctxT, 1.0
            if j == WQ:
                return ps.rearrange("p (h n) -> p h n", n=P), wqT, 1.0
            if j in (WK, WV):
                return ps.rearrange("p (h n) -> p h n", n=P)[:, :, 0:C], (wkT, wvT)[j - WK], 1.0
            if j == QK:
                return ps[0:C, :].rearrange("p (h n) -> p h n", n=P), qk, SCALE0
            if j == VO:
                return ps[0:C, :], vo, 1.0
            if j == XN:
                return ps, g.xnT, 1.0
            if j < V0:
                half = ps.rearrange("p (b n) -> p b n", b=2)[:, :, 0:KEYS // 2]
                return half, g.keys0[:, j - K0, :].view("p (b n) -> p b n", b=2), 1.0
            kt = j - V0
            rows = P if kt < KT - 1 else KLAST
            return ps[0:rows, :], g.values0[0:rows, kt, :], 1.0

        block = stack.enter_context(nc.Block())

        @block.sync
        def _(sp):
            sp.dma_start(ctx_rows[:, 0:KT - 1, :],
                         io["ctx"][0:(KT - 1) * P, :].rearrange("(t p) c -> p t c", p=P)).then_inc(loaded["ctx"], 16)
            sp.dma_start(ctx_rows[0:KLAST, KT - 1, :], io["ctx"][(KT - 1) * P:KEYS, :]).then_inc(loaded["ctx"], 16)
            sp.dma_start(wq[:], io["L0_xattn_Wq"]).then_inc(loaded["wq"], 16)
            sp.dma_start(wk[:], io["L0_xattn_Wk"]).then_inc(loaded["wk"], 16)
            sp.wait_ge(zero_done, 1)
            for e in range(E):
                sp.dma_start(g.expert_in[e * CAP:(e + 1) * CAP, :].rearrange("(p r) d -> p (r d)", r=4),
                             g.zeros[0:CAP // 4, :]).then_inc(g.expert_in_zeroed, 16)

        @block.scalar
        def _(act):
            act.dma_start(g.x[:], io["x"].rearrange("(t p) d -> p t d", p=P)).then_inc(loaded["x"], 16)
            act.dma_start(wv[:], io["L0_xattn_Wv"]).then_inc(loaded["wv"], 16)
            act.dma_start(wout[:], io["L0_xattn_Wout"].rearrange("(h p) d -> p h d", p=P)).then_inc(loaded["wout"], 16)
            act.dma_start(g.bias0[:], io["L0_xattn_bout"].partition_broadcast(P)).then_inc(loaded["small"], 16)
            act.dma_start(g.bias1[:], io["L1_xattn_bo"].partition_broadcast(P)).then_inc(loaded["small"], 16)
            act.dma_start(gates_raw[:, 0:2], io["g_xattn"].partition_broadcast(P)).then_inc(loaded["small"], 16)
            act.dma_start(gates_raw[:, 2:4], io["g_ffn"].partition_broadcast(P)).then_inc(loaded["small"], 16)
            for j in range(JOBS):
                if j == QK:
                    act.wait_ge(loaded["wout"], 16)
                    act.copy(wout_s.hi, wout[:]).then_inc(wout_hi, 1)
                ps, to, factor = evacuation(j)
                act.wait_ge(pe_done, j + 1)
                act.activation(to.hi, ps, ACT.Copy, scale=factor).then_inc(hi_done, 1)
            act.wait_ge(loaded["small"], 64)
            act.activation(g.gates[:], gates_raw[:], ACT.Tanh).then_inc(hi_done, 1)

        @block.gpsimd
        def _(pool):
            step = Chain(pool, ident_done)
            step(pool.memset(g.ident[:], 0.0))
            step(pool.affine_select(out=g.ident[:], in_=g.ident[:], compare_op=ALU.not_equal, fill=1.0,
                                    base=0, pattern=[[-1, P]], channel_multiplier=1))
            pool.memset(g.zeros[:], 0.0).then_inc(zero_done, 1)
            pool.memset(g.minus_half[:], -0.5).then_inc(zero_done, 1)
            pool.wait_ge(zero_done, 2)
            pool.wait_ge(var_done, 1)
            pool.tensor_tensor(rstd[:], var_eps[:], g.minus_half[:], ALU.pow).then_inc(rstd_done, 1)

        @block.vector
        def _(dve):
            step = Chain(dve, dve_step)
            dve.wait_ge(loaded["x"], 16)
            layernorm_stats(dve, step, g.x, stats, moments, var_eps).then_inc(var_done, 1)
            for j in range(JOBS):
                if j == WV:
                    dve.wait_ge(rstd_done, 1)
                    layernorm_apply(dve, g.x, moments, rstd, xn).then_inc(xn_done, 1)
                if j == QK:
                    dve.wait_ge(wout_hi, 1)
                    dve.tensor_tensor(wout_s.lo, wout[:], f32(wout_s.hi), ALU.subtract).then_inc(wout_lo, 1)
                ps, to, factor = evacuation(j)
                dve.wait_ge(hi_done, j + 1)
                if factor == 1.0:
                    dve.tensor_tensor(to.lo, ps, f32(to.hi), ALU.subtract).then_inc(lo_done, 1)
                else:
                    dve.scalar_tensor_tensor(out=to.lo, in0=ps, scalar=factor, in1=f32(to.hi),
                                             op0=ALU.mult, op1=ALU.subtract).then_inc(lo_done, 1)

        @block.tensor
        def _(pe):
            pe.wait_ge(ident_done, 2)
            for j in range(JOBS):
                ps = slot(j)
                wait(pe, lo_done, j - 3)
                if j == CTX:
                    pe.wait_ge(loaded["ctx"], 32)
                    for kt in range(KT):
                        rows = P if kt < KT - 1 else KLAST
                        last = pe.transpose(ps[0:C, kt * P:kt * P + rows], ctx_rows[0:rows, kt, :],
                                            g.ident[0:rows, 0:rows])
                elif j in (WQ, WK, WV):
                    pe.wait_ge(loaded[("wq", "wk", "wv")[j - WQ]], 16)
                    w, rows = ((wq, D), (wk, C), (wv, C))[j - WQ]
                    for h in range(H0):
                        last = pe.transpose(ps[:, h * P:h * P + rows], w[:, h * DH0:(h + 1) * DH0],
                                            g.ident[0:rows, 0:rows])
                elif j == QK:
                    pe.wait_ge(lo_done, WK + 1)
                    for h in range(H0):
                        last = matmul3(pe, ps[0:C, h * D:(h + 1) * D], wkT[:, h, :], wqT[:, h, :])
                elif j == VO:
                    pe.wait_ge(lo_done, WV + 1)
                    pe.wait_ge(wout_lo, 1)
                    for h in range(H0):
                        last = matmul3(pe, ps[0:C, h * D:(h + 1) * D], wvT[:, h, :], wout_s[:, h, :])
                elif j == XN:
                    pe.wait_ge(xn_done, 1)
                    for t in range(TT):
                        last = pe.transpose(ps[:, t * P:(t + 1) * P], xn[:, t, :], g.ident[:])
                elif j < V0:
                    pe.wait_ge(lo_done, QK + 1)
                    for b in range(2):
                        n = KEYS // 2
                        last = matmul3(pe, ps[:, b * BANK:b * BANK + n], qk[:, j - K0, :],
                                       g.ctxT[:, b * n:(b + 1) * n])
                else:
                    pe.wait_ge(lo_done, VO + 1)
                    kt = j - V0
                    rows = P if kt < KT - 1 else KLAST
                    for b in range(2):
                        last = matmul3(pe, ps[0:rows, b * BANK:(b + 1) * BANK],
                                       g.ctxT[:, kt * P:kt * P + rows], vo[:, b * BANK:(b + 1) * BANK])
                last.then_inc(pe_done, 1)


def attention0(core, g):
    nc = core.nc
    with ExitStack() as stack:
        c = core.scope(stack)
        queries = [c.split(f"queries{i}", [D, P]) for i in range(2)]
        weights = [c.sb(f"weights{i}", [P, KT * P]) for i in range(2)]
        weightsT = [c.split(f"weights{i}T", [P, KT * P]) for i in range(2)]
        neg_max = c.sb("neg_max0", [P, 2])
        den = c.sb("den0", [P, 4])
        rden = c.sb("rden0", [P, 2])
        acc = [c.sb(f"acc{i}", [P, D]) for i in range(2)]

        queries_ready = c.sem("b_queries")
        scores_done, max_done, exp_done = c.sem("b_scores"), c.sem("b_max"), c.sem("b_exp")
        turned, hi_done, lo_done = c.sem("b_turned"), c.sem("b_hi"), c.sem("b_lo")
        pv_done, recip_done, acc_done = c.sem("b_pv"), c.sem("b_recip"), c.sem("b_acc")
        pad_done, dve_step = c.sem("b_pad"), c.sem("b_dve")

        UNITS = 2 * H0
        TURNS = TT // 2
        CHUNKS = [(0, 3), (3, KT)]
        half = KEYS // 2

        def scores(u):
            return g.psum[:, 2 * (u % 2):2 * (u % 2) + 2, 0:half]

        def turned_bank(i):
            return g.psum[:, 4 + i, :]

        def out_bank(u):
            return g.psum[:, 6 + u % 2, 0:D]

        def steps(engine_step, engine):
            for s in range(UNITS):
                engine_step(0, s)
            with engine.Fori(1, TURNS) as turn:
                for s in range(UNITS):
                    engine_step(turn, s)
            for s in range(2):
                engine_step(TURNS, s, drain=True)

        def unit(turn, s):
            return turn * UNITS + s

        def exists(turn, u):
            return not (isinstance(turn, int) and turn == 0 and u < 0)

        block = stack.enter_context(nc.Block())

        @block.gpsimd
        def _(pool):
            for i in range(2):
                pool.memset(weights[i][:, KEYS:KT * P], 0.0).then_inc(pad_done, 1)

            def step(turn, s, drain=False):
                if drain or s % H0:
                    return
                tile = turn * 2 + s // H0
                q = queries[s // H0]
                wait(pool, scores_done, (tile - 1) * H0)
                at = bass.ds(tile * P, P)
                pool.tensor_copy(q.hi, f32(g.xnT.hi[:, at])).then_inc(queries_ready, 1)
                pool.tensor_copy(q.lo, f32(g.xnT.lo[:, at])).then_inc(queries_ready, 1)

            steps(step, pool)

        @block.tensor
        def _(pe):
            def step(turn, s, drain=False):
                if not drain:
                    tile = turn * 2 + s // H0
                    if s % H0 == 0:
                        pe.wait_ge(queries_ready, tile * 2 + 2)
                    wait(pe, exp_done, unit(turn, s - 1))
                    for b in range(2):
                        last = matmul3(pe, scores(s)[:, b, :], queries[s // H0],
                                       g.keys0[:, s % H0, b * half:(b + 1) * half])
                    last.then_inc(scores_done, 1)
                if exists(turn, s - 1) and not (drain and s == 1):
                    u = s - 1
                    pe.wait_ge(exp_done, unit(turn, u + 1))
                    if s == 0 or s == 1:
                        pe.wait_ge(pad_done, 2)
                    for i, (a, b) in enumerate(CHUNKS):
                        wait(pe, lo_done, unit(turn, u - 1) * 2 + i + 1)
                        for kt in range(a, b):
                            last = pe.transpose(turned_bank(i)[:, (kt - a) * P:(kt - a + 1) * P],
                                                weights[u % 2][:, kt * P:(kt + 1) * P], g.ident[:])
                        last.then_inc(turned, 1)
                if exists(turn, s - 2):
                    u = s - 2
                    wait(pe, lo_done, unit(turn, u) * 2 + 2)
                    wait(pe, acc_done, unit(turn, u - 1))
                    h = u % H0
                    for kt in range(KT):
                        rows = P if kt < KT - 1 else KLAST
                        last = matmul3(pe, out_bank(u), weightsT[u % 2][0:rows, kt * P:(kt + 1) * P],
                                       g.values0[0:rows, kt, h * D:(h + 1) * D],
                                       start=kt == 0, stop=kt == KT - 1)
                    last.then_inc(pv_done, 1)

            steps(step, pe)

        @block.scalar
        def _(act):
            def step(turn, s, drain=False):
                if exists(turn, s - 1) and not (drain and s == 1):
                    u = s - 1
                    wait(act, pv_done, unit(turn, u - 1))
                    for i, (a, b) in enumerate(CHUNKS):
                        act.wait_ge(turned, unit(turn, u) * 2 + i + 1)
                        act.copy(weightsT[u % 2].hi[:, a * P:b * P],
                                 turned_bank(i)[:, 0:(b - a) * P]).then_inc(hi_done, 1)
                if not drain:
                    act.wait_ge(max_done, unit(turn, s + 1))
                    wait(act, turned, unit(turn, s - 1) * 2)
                    wait(act, recip_done, unit(turn, s - 3))
                    act.activation(weights[s % 2][:, 0:KEYS].rearrange("p (b n) -> p b n", b=2), scores(s),
                                   ACT.Exp, bias=neg_max[:, s % 2:s % 2 + 1],
                                   accum_out=den[:, s % 4:s % 4 + 1]).then_inc(exp_done, 1)

            steps(step, act)

        @block.vector
        def _(dve):
            def step(turn, s, drain=False):
                if not drain:
                    dve.wait_ge(scores_done, unit(turn, s + 1))
                    wait(dve, exp_done, unit(turn, s - 1))
                    dve.tensor_reduce(neg_max[:, s % 2:s % 2 + 1], scores(s), AX.XY, ALU.max,
                                      negate=True).then_inc(max_done, 1)
                if exists(turn, s - 1) and not (drain and s == 1):
                    u = s - 1
                    for i, (a, b) in enumerate(CHUNKS):
                        dve.wait_ge(hi_done, unit(turn, u) * 2 + i + 1)
                        dve.tensor_tensor(weightsT[u % 2].lo[:, a * P:b * P], turned_bank(i)[:, 0:(b - a) * P],
                                          f32(weightsT[u % 2].hi[:, a * P:b * P]), ALU.subtract).then_inc(lo_done, 1)
                    wait(dve, acc_done, unit(turn, u - 1))
                    dve.wait_ge(exp_done, unit(turn, u + 1))
                    dve.reciprocal(rden[:, u % 2:u % 2 + 1], den[:, u % 4:u % 4 + 1]).then_inc(recip_done, 1)
                if exists(turn, s - 2):
                    u = s - 2
                    h = u % H0
                    dve.wait_ge(pv_done, unit(turn, u + 1))
                    dve.wait_ge(recip_done, unit(turn, u + 1))
                    wait(dve, acc_done, unit(turn, u))
                    if h == H0 - 1:
                        tile = turn * 2 + (u // H0)
                        out = g.attended[:, bass.ds(tile * D, D)]
                    else:
                        out = acc[h % 2][:]
                    before = g.bias0[:] if h == 0 else acc[(h - 1) % 2][:]
                    dve.scalar_tensor_tensor(out=out, in0=out_bank(u), scalar=rden[:, u % 2:u % 2 + 1],
                                             in1=before, op0=ALU.mult, op1=ALU.add).then_inc(acc_done, 1)

            steps(step, dve)


def dispatch(core, g, io):
    nc = core.nc
    with ExitStack() as stack:
        c = core.scope(stack)
        wq, wk, wv = c.sb("wq1", [P, H1 * DH1]), c.sb("wk1", [C, H1 * DH1]), c.sb("wv1", [C, H1 * DH1])
        wr = c.sb("wr0", [D, E])
        wv_s = c.split("wv1s", [C, H1 * DH1])
        wqT, wkT = c.split("wq1T", [P, H1 // 2, D]), c.split("wk1T", [P, H1 // 2, C])
        qk = c.split("qk1", [C, 2, 2, H1 // 4, D])
        xn = c.sb("xn0", [P, TT, D])
        xnT = c.sb("xn0T", [D, T])
        stats, moments = c.sb("ln_stats1", [P, TT, 6]), c.sb("ln_moments1", [P, TT, 2])
        var_eps, rstd = c.sb("ln_var1", [P, TT]), c.sb("ln_rstd1", [P, TT])
        earlier = c.sb("earlier", [P, P], BF16)
        ones = c.sb("ones_bf", [P, P], BF16)
        descending = c.sb("descending", [P, TT, E])
        logits = c.sb("logits", [P, TT, E])
        masked = c.sb("masked", [P, TT, E])
        best = c.sb("best", [P, TOPK, TT])
        rank, topped = c.sb("rank", [P, TT, E]), c.sb("topped", [P, TOPK, TT])
        chosen = c.sb("chosen", [P, TOPK, TT, E])
        counted = c.sb("counted", [P, TT, E], BF16)
        places = c.sb("places", [P, TOPK, TT, E])
        pos, over = c.sb("pos", [P, TOPK, TT]), c.sb("over", [P, TOPK, TT])
        base, where_to = c.sb("slot_base", [P, TOPK, TT]), c.sb("where_to", [P, TOPK, TT])
        where_from = c.sb("where_from", [P, TOPK, TT])
        scatter_at = c.sb("scatter_at", [P, TOPK, TT], U32)
        lead, second, total = c.sb("lead", [P, TT]), c.sb("second", [P, TT]), c.sb("total", [P, TT])

        loaded = {n: c.sem("c_ld_" + n) for n in ("wq", "wk", "wv", "wr")}
        const_done, var_done, rstd_done, xn_done = (c.sem("c_" + n) for n in ("const", "var", "rstd", "xn"))
        turned, turned_out, logits_done = c.sem("c_turned"), c.sem("c_turnedout"), c.sem("c_logits")
        counted_done, pos_done, lead_done = c.sem("c_counted"), c.sem("c_pos"), c.sem("c_lead")
        second_done, at_done, scattered = c.sem("c_second"), c.sem("c_at"), c.sem("c_scattered")
        pe_done, hi_done, lo_done = c.sem("c_pe"), c.sem("c_hi"), c.sem("c_lo")
        wv_hi, wv_lo, dve_step = c.sem("c_wvhi"), c.sem("c_wvlo"), c.sem("c_dve")

        WQ, WK, QK = 0, 1, 2
        K1 = 4
        V1 = K1 + H1
        JOBS = V1 + B
        RING = 3
        half = KEYS // 2

        def slot(j):
            return g.psum[:, 2 * (j % RING):2 * (j % RING) + 2, :]

        def evacuation(j):
            ps = slot(j)
            flat = ps.rearrange("p b n -> p (b n)").rearrange("p (h n) -> p h n", n=P)
            if j == WQ:
                return flat, wqT, 1.0
            if j == WK:
                return flat[:, :, 0:C], wkT, 1.0
            if j < K1:
                return ps[0:C].rearrange("p o (i d) -> p o i d", d=D), qk[:, j - QK], SCALE1
            return ps[:, :, 0:half].rearrange("p n (b k) -> p n b k", k=M), \
                g.keys1[:, :, j - K1, :].view("p (n b) k -> p n b k", n=2), 1.0

        turned_ps = g.psum[:, 6:8, :].rearrange("p b n -> p (b n)")
        logits_ps = g.psum[:, 6, 0:TT * E].rearrange("p (t e) -> p t e", e=E)
        pos_ps = g.psum[:, 7, 0:TT * E].rearrange("p (t e) -> p t e", e=E)

        block = stack.enter_context(nc.Block())

        @block.sync
        def _(sp):
            sp.dma_start(wq[:], io["L1_xattn_Wq"]).then_inc(loaded["wq"], 16)
            sp.dma_start(wk[:], io["L1_xattn_Wk"]).then_inc(loaded["wk"], 16)
            sp.dma_start(wr[:], io["L0_ffn_Wr"]).then_inc(loaded["wr"], 16)
            sp.dma_start(wv[:], io["L1_xattn_Wv"]).then_inc(loaded["wv"], 16)

        @block.gpsimd
        def _(pool):
            step = Chain(pool, const_done)
            step(pool.memset(earlier[:], 1.0))
            step(pool.affine_select(out=earlier[:], in_=earlier[:], compare_op=ALU.is_gt, fill=0.0,
                                    base=0, pattern=[[1, P]], channel_multiplier=-1))
            step(pool.memset(ones[:], 1.0))
            step(pool.iota(descending[:], pattern=[[0, TT], [-1, E]], base=E, channel_multiplier=0,
                           allow_small_or_imprecise_dtypes=True))
            pool.wait_ge(var_done, 1)
            pool.tensor_tensor(rstd[:], var_eps[:], g.minus_half[:], ALU.pow).then_inc(rstd_done, 1)
            pool.wait_ge(g.expert_in_zeroed, 16 * E)
            pool.wait_ge(at_done, 1)
            for t in range(TT):
                for k in range(TOPK):
                    pool.indirect_dma_start(
                        out=g.expert_in, out_offset=bass.IndirectOffsetOnAxis(ap=scatter_at[:, k, t:t + 1], axis=0),
                        in_=xn[:, t, :], in_offset=None, bounds_check=SLOTS - 1,
                        oob_is_err=False).then_inc(scattered, 16)
            pool.wait_ge(scattered, 16 * TT * TOPK)

        @block.scalar
        def _(act):
            def evacuate(j):
                act.wait_ge(pe_done, j + 1)
                if j >= V1:
                    act.copy(g.values1[:, j - V1, :], slot(j)[0:M].rearrange("p b n -> p (b n)")).then_inc(hi_done, 1)
                    return
                ps, to, factor = evacuation(j)
                act.activation(to.hi, ps, ACT.Copy, scale=factor).then_inc(hi_done, 1)

            evacuate(WQ)
            evacuate(WK)
            act.wait_ge(turned, 1)
            act.copy(xnT[:], turned_ps).then_inc(turned_out, 1)
            evacuate(QK)
            act.wait_ge(lead_done, 1)
            act.activation(second[:], lead[:], ACT.Exp).then_inc(second_done, 1)
            act.wait_ge(loaded["wv"], 16)
            act.copy(wv_s.hi, wv[:]).then_inc(wv_hi, 1)
            for j in range(QK + 1, JOBS):
                evacuate(j)

        @block.vector
        def _(dve):
            step = Chain(dve, dve_step)

            def evacuate(j):
                ps, to, factor = evacuation(j)
                dve.wait_ge(hi_done, j + 1)
                if factor == 1.0:
                    dve.tensor_tensor(to.lo, ps, f32(to.hi), ALU.subtract).then_inc(lo_done, 1)
                elif j < K1:
                    for o in range(2):
                        last = dve.scalar_tensor_tensor(out=to.lo[:, o], in0=ps[:, o], scalar=factor,
                                                        in1=f32(to.hi[:, o]), op0=ALU.mult, op1=ALU.subtract)
                    last.then_inc(lo_done, 1)

            x2d = g.x[:].rearrange("p t d -> p (t d)")
            step(dve.scalar_tensor_tensor(out=x2d, in0=g.attended[:], scalar=g.gates[:, 0:1], in1=x2d,
                                          op0=ALU.mult, op1=ALU.add))
            layernorm_stats(dve, step, g.x, stats, moments, var_eps).then_inc(var_done, 1)
            evacuate(WQ)
            evacuate(WK)
            dve.wait_ge(rstd_done, 1)
            layernorm_apply(dve, g.x, moments, rstd, xn).then_inc(xn_done, 1)
            dve.wait_ge(logits_done, 1)
            step(dve.tensor_scalar(logits[:], logits_ps, 1e4, -1e4, ALU.min, ALU.max))
            dve.wait_ge(const_done, 4)
            for k in range(TOPK):
                scores = logits if k == 0 else masked
                step(dve.tensor_reduce(best[:, k, :], scores[:], AX.X, ALU.max))
                step(dve.tensor_tensor(rank[:], scores[:], best[:, k, :].unsqueeze(2).to_broadcast([P, TT, E]),
                                       ALU.is_equal))
                step(dve.tensor_tensor(rank[:], rank[:], descending[:], ALU.mult))
                step(dve.tensor_reduce(topped[:, k, :], rank[:], AX.X, ALU.max))
                step(dve.tensor_tensor(chosen[:, k], rank[:],
                                       topped[:, k, :].unsqueeze(2).to_broadcast([P, TT, E]), ALU.is_equal))
                if k == 0:
                    step(dve.scalar_tensor_tensor(
                        out=masked[:].rearrange("p t e -> p (t e)"),
                        in0=chosen[:, 0].rearrange("p t e -> p (t e)"), scalar=-4e4,
                        in1=logits[:].rearrange("p t e -> p (t e)"), op0=ALU.mult, op1=ALU.add))
            dve.tensor_tensor(counted[:], chosen[:, 0], chosen[:, 1], ALU.add).then_inc(counted_done, 1)
            dve.tensor_tensor(lead[:], best[:, 1, :], best[:, 0, :], ALU.subtract).then_inc(lead_done, 1)
            step(dve.tensor_scalar(base[:], topped[:], float(-CAP), float(CAP * E), ALU.mult, ALU.add))
            evacuate(QK)
            dve.wait_ge(pos_done, 1)
            for k in range(TOPK):
                last = dve.tensor_tensor(places[:, k], pos_ps, chosen[:, k], ALU.mult)
            step(last)
            step(dve.tensor_reduce(pos[:], places[:], AX.X, ALU.add))
            step(dve.tensor_scalar(over[:], pos[:], float(CAP), None, ALU.is_ge))
            step(dve.tensor_tensor(where_to[:], pos[:], base[:], ALU.add))
            over2, to2 = (v[:].rearrange("p k t -> p (k t)") for v in (over, where_to))
            step(dve.scalar_tensor_tensor(out=to2, in0=over2, scalar=float(1 << 16), in1=to2,
                                          op0=ALU.mult, op1=ALU.add))
            dve.tensor_copy(scatter_at[:], where_to[:]).then_inc(at_done, 1)
            step(dve.tensor_scalar(where_from[:], pos[:], float(CAP - 1), None, ALU.min))
            step(dve.tensor_tensor(where_from[:], where_from[:], base[:], ALU.add))
            step(dve.tensor_copy(g.gather_at[:], where_from[:]))
            dve.wait_ge(second_done, 1)
            step(dve.tensor_scalar(total[:], second[:], 1.0, 1e-12, ALU.add, ALU.add))
            step(dve.reciprocal(g.token_weights[:, 0, :], total[:]))
            step(dve.tensor_tensor(g.token_weights[:, 1, :], second[:], g.token_weights[:, 0, :], ALU.mult))
            step(dve.tensor_scalar(over[:], over[:], -1.0, 1.0, ALU.mult, ALU.add))
            step(dve.tensor_tensor(g.token_weights[:], g.token_weights[:], over[:], ALU.mult))
            step(dve.tensor_scalar(g.token_weights[:], g.token_weights[:], g.gates[:, 2:3], None, ALU.mult))
            dve.wait_ge(wv_hi, 1)
            dve.tensor_tensor(wv_s.lo, wv[:], f32(wv_s.hi), ALU.subtract).then_inc(wv_lo, 1)
            for j in range(QK + 1, V1):
                evacuate(j)

        @block.tensor
        def _(pe):
            def job(j):
                ps = slot(j)
                wait(pe, lo_done if j - RING < V1 else hi_done, j - RING + 1)
                if j in (WQ, WK):
                    pe.wait_ge(loaded[("wq", "wk")[j]], 16)
                    w, rows = ((wq, D), (wk, C))[j]
                    flat = ps.rearrange("p b n -> p (b n)")
                    for i in range(H1 // 2):
                        last = pe.transpose(flat[:, i * P:i * P + rows], w[:, i * P:(i + 1) * P],
                                            g.ident[0:rows, 0:rows])
                elif j < K1:
                    pe.wait_ge(lo_done, WK + 1)
                    for i in range(H1 // 4):
                        for odd in range(2):
                            at, pair = slice(odd * DH1, (odd + 1) * DH1), (j - QK) * (H1 // 4) + i
                            last = matmul3(pe, ps[0:C, odd, i * D:(i + 1) * D], wkT[at, pair, :], wqT[at, pair, :])
                elif j < V1:
                    h = j - K1
                    pe.wait_ge(lo_done, QK + 1 + h // (H1 // 2))
                    for b in range(2):
                        last = matmul3(pe, ps[:, b, 0:half], qk[:, h // 8, h % 2, h % 8 // 2, :],
                                       g.ctxT[:, b * half:(b + 1) * half])
                else:
                    b = j - V1
                    if j == V1:
                        pe.wait_ge(wv_lo, 1)
                    for i in range(2):
                        last = matmul3(pe, ps[0:M, i, :], g.ctxT[:, b * M:(b + 1) * M],
                                       wv_s[:, i * BANK:(i + 1) * BANK])
                last.then_inc(pe_done, 1)

            job(WQ)
            job(WK)
            pe.wait_ge(xn_done, 1)
            for t in range(TT):
                last = pe.transpose(turned_ps[:, t * P:(t + 1) * P], xn[:, t, :], g.ident[:])
            last.then_inc(turned, 1)
            pe.wait_ge(turned_out, 1)
            pe.wait_ge(loaded["wr"], 16)
            for t in range(TT):
                last = pe.matmul(logits_ps[:, t, :], xnT[:, t * P:(t + 1) * P], wr[:], start=True, stop=True)
            last.then_inc(logits_done, 1)
            job(QK)
            pe.wait_ge(counted_done, 1)
            last = pe.matmul(pos_ps, earlier[:], counted[:], start=True, stop=False)
            for t in range(TT - 1):
                last = pe.matmul(pos_ps[:, t + 1:TT, :], ones[:],
                                 counted[:, t, :].unsqueeze(1).to_broadcast([P, TT - 1 - t, E]),
                                 start=False, stop=t == TT - 2)
            last.then_inc(pos_done, 1)
            for j in range(QK + 1, JOBS):
                job(j)


def experts0(core, g, io):
    nc = core.nc
    with ExitStack() as stack:
        c = core.scope(stack)
        TILES = [(0, 112), (112, 216), (216, CAP)]
        NT = len(TILES)
        CREDIT = 16
        raw = [[c.sb(f"ew{i}_{n}", [P, F]) for n in range(3)] for i in range(2)]
        parts = [[c.split(f"ews{i}_{n}", [P, F]) for n in range(3)] for i in range(2)]
        rows = [c.sb(f"erows{i}", [P, NT, D]) for i in range(2)]
        tokensT = [c.split(f"etokT{i}", [D, CAP]) for i in range(2)]
        silu = [c.sb(f"esilu{i}", [P, CAP]) for i in range(2)]
        hidden = c.sb("ehidden", [P, CAP])
        hid = [c.split(f"ehid{i}", [P, FT, CAP]) for i in range(2)]
        result = [c.sb(f"eresult{i}", [P, NT, D]) for i in range(2)]

        w_loaded = [c.sem(f"d_wld{i}") for i in range(2)]
        r_loaded = [c.sem(f"d_rld{i}") for i in range(2)]
        w_hi, w_lo, stored = c.sem("d_whi"), c.sem("d_wlo"), [c.sem(f"d_stored{i}") for i in range(2)]
        turned, turned_hi, turned_lo = c.sem("d_turned"), c.sem("d_turnedhi"), c.sem("d_turnedlo")
        up_done, silu_done, mult_done = c.sem("d_up"), c.sem("d_silu"), c.sem("d_mult")
        hid_hi, hid_lo = c.sem("d_hidhi"), c.sem("d_hidlo")
        down_done, result_done, gathered, sum_step = c.sem("d_down"), c.sem("d_result"), c.sem("d_gath"), c.sem("d_sum")

        names = ("L0_ffn_W1", "L0_ffn_W3", "L0_ffn_W2")

        def turns(step, engine):
            for i in range(2):
                step(0, i)
            with engine.Fori(1, E // 2) as turn:
                for i in range(2):
                    step(turn, i)

        def up_bank(n, which):
            return g.psum[:, 2 * (n % 2) + which, 0:CAP]

        turned_ps = g.psum[:, 4, 0:CAP]

        def down_ps(i):
            return g.psum[:, 5 + i, 0:NT * D].rearrange("p (s d) -> p s d", d=D)

        block = stack.enter_context(nc.Block())

        @block.sync
        def _(sp):
            def step(turn, i):
                e = turn * 2 + i
                wait(sp, w_lo, e - 1)
                for n, name in enumerate(names):
                    w = io[name]
                    if n < 2:
                        src = w.rearrange("e d f -> (e d) f")[bass.ds(e * D, D), :]
                        sp.dma_start(raw[i][n][:], src).then_inc(w_loaded[i], 16)
                    else:
                        src = w.rearrange("e f d -> (e f) d")[bass.ds(e * F, F), :]
                        sp.dma_start(raw[i][n][:].rearrange("p (t d) -> p t d", d=D),
                                     src.rearrange("(t p) d -> p t d", p=P)).then_inc(w_loaded[i], 16)
                wait(sp, turned, e - 1)
                for s, (a, b) in enumerate(TILES):
                    sp.dma_start(rows[i][0:b - a, s, :],
                                 g.expert_in[bass.ds(e * CAP + a, b - a), :]).then_inc(r_loaded[i], 16)
                store(turn, i - 2)

            def store(turn, i):
                if isinstance(turn, int) and turn == 0 and i < 0:
                    return
                e = turn * 2 + i
                sp.wait_ge(result_done, e + 2)
                for s, (a, b) in enumerate(TILES):
                    sp.dma_start(g.expert_out[bass.ds(e * CAP + a, b - a), :],
                                 result[i % 2][0:b - a, s, :]).then_inc(stored[i % 2], 16)

            turns(step, sp)
            store(E // 2, -2)
            store(E // 2, -1)

        @block.gpsimd
        def _(pool):
            def step(turn, i):
                e = turn * 2 + i
                wait(pool, down_done, e - 1)
                for n in range(3):
                    pool.wait_ge(w_hi, e * 3 + n + 1)
                    last = pool.tensor_tensor(parts[i][n].lo, raw[i][n][:], f32(parts[i][n].hi), ALU.subtract)
                last.then_inc(w_lo, 1)

            turns(step, pool)
            for i in range(2):
                pool.wait_ge(stored[i], CREDIT + 16 * NT * (E // 2))
            for t in range(TT):
                for k in range(TOPK):
                    pool.indirect_dma_start(
                        out=g.gathered[:, t, k, :], out_offset=None, in_=g.expert_out,
                        in_offset=bass.IndirectOffsetOnAxis(ap=g.gather_at[:, k, t:t + 1], axis=0)
                    ).then_inc(gathered, 16)

        @block.scalar
        def _(act):
            def split_weights(turn, i):
                e = turn * 2 + i
                act.wait_ge(w_loaded[i % 2], (turn + (i // 2)) * 48 + 48)
                wait(act, down_done, e - 1)
                for n in range(3):
                    act.copy(parts[i % 2][n].hi, raw[i % 2][n][:]).then_inc(w_hi, 1)

            def tokens_hi(turn, i):
                act.wait_ge(turned, turn * 2 + i + 1)
                act.copy(tokensT[i % 2].hi, turned_ps).then_inc(turned_hi, 1)

            def store_result(turn, i):
                if isinstance(turn, int) and turn == 0 and i < 0:
                    return
                e = turn * 2 + i
                act.wait_ge(down_done, e + 1)
                wait(act, stored[i % 2], CREDIT + (turn + (i // 2)) * 16 * NT)
                for s, (a, b) in enumerate(TILES):
                    last = act.copy(result[i % 2][0:b - a, s, :], down_ps(i % 2)[0:b - a, s, :])
                last.then_inc(result_done, 1)

            def step(turn, i, ahead=True):
                e = turn * 2 + i
                for f in range(FT):
                    n = e * FT + f
                    act.wait_ge(up_done, n + 1)
                    wait(act, mult_done, n - 1)
                    act.activation(silu[f % 2][:], up_bank(f, 0), ACT.Silu).then_inc(silu_done, 1)
                    if f == 1:
                        store_result(turn, i - 1)
                        if ahead:
                            split_weights(turn, i + 1)
                            tokens_hi(turn, i + 1)

            for i in range(2):
                act.sem_inc(stored[i], CREDIT)
            split_weights(0, 0)
            tokens_hi(0, 0)
            for i in range(2):
                step(0, i)
            with act.Fori(1, E // 2 - 1) as turn:
                for i in range(2):
                    step(turn, i)
            step(E // 2 - 1, 0)
            step(E // 2 - 1, 1, ahead=False)
            store_result(E // 2, -1)

        @block.vector
        def _(dve):
            def tokens_lo(turn, i):
                dve.wait_ge(turned_hi, turn * 2 + i + 1)
                dve.tensor_tensor(tokensT[i % 2].lo, turned_ps, f32(tokensT[i % 2].hi),
                                  ALU.subtract).then_inc(turned_lo, 1)

            def step(turn, i, ahead=True):
                e = turn * 2 + i
                wait(dve, down_done, e - 1)
                for f in range(FT):
                    n = e * FT + f
                    dve.wait_ge(silu_done, n + 1)
                    wait(dve, hid_lo, n)
                    dve.tensor_tensor(hidden[:], silu[f % 2][:], up_bank(f, 1), ALU.mult).then_inc(mult_done, 1)
                    dve.wait_ge(mult_done, n + 1)
                    dve.tensor_copy(hid[i].hi[:, f, :], hidden[:]).then_inc(hid_hi, 1)
                    dve.wait_ge(hid_hi, n + 1)
                    dve.tensor_tensor(hid[i].lo[:, f, :], hidden[:], f32(hid[i].hi[:, f, :]),
                                      ALU.subtract).then_inc(hid_lo, 1)
                    if f == 1 and ahead:
                        tokens_lo(turn, i + 1)

            tokens_lo(0, 0)
            for i in range(2):
                step(0, i)
            with dve.Fori(1, E // 2 - 1) as turn:
                for i in range(2):
                    step(turn, i)
            step(E // 2 - 1, 0)
            step(E // 2 - 1, 1, ahead=False)
            chain = Chain(dve, sum_step)
            dve.wait_ge(gathered, 16 * TOPK * TT)
            for k in range(TOPK):
                for t in range(TT):
                    last = dve.scalar_tensor_tensor(out=g.x[:, t, :], in0=g.gathered[:, t, k, :],
                                                    scalar=g.token_weights[:, k, t:t + 1], in1=g.x[:, t, :],
                                                    op0=ALU.mult, op1=ALU.add)
                chain(last)

        @block.tensor
        def _(pe):
            def transposes(turn, i):
                e = turn * 2 + i
                pe.wait_ge(r_loaded[i % 2], (turn + i // 2) * 16 * NT + 16 * NT)
                wait(pe, turned_lo, e)
                wait(pe, up_done, (e - 1) * FT)
                for s, (a, b) in enumerate(TILES):
                    last = pe.transpose(turned_ps[:, a:b], rows[i % 2][0:b - a, s, :], g.ident[0:b - a, 0:b - a])
                last.then_inc(turned, 1)

            def down(turn, i):
                if isinstance(turn, int) and turn == 0 and i < 0:
                    return
                e = turn * 2 + i
                pe.wait_ge(hid_lo, e * FT + FT)
                wait(pe, result_done, e)
                w = parts[i % 2][2].view("p (t d) -> p t d", d=D)
                for s, (a, b) in enumerate(TILES):
                    for f in range(FT):
                        last = matmul3(pe, down_ps(i % 2)[0:b - a, s, :], hid[i % 2][:, f, a:b], w[:, f, :],
                                       start=f == 0, stop=f == FT - 1)
                last.then_inc(down_done, 1)

            def step(turn, i, ahead=True):
                e = turn * 2 + i
                pe.wait_ge(w_lo, e + 1)
                pe.wait_ge(turned_lo, e + 1)
                for f in range(FT):
                    n = e * FT + f
                    wait(pe, mult_done, n - 1)
                    for which in range(2):
                        last = matmul3(pe, up_bank(f, which), parts[i][which][:, f * P:(f + 1) * P], tokensT[i])
                    last.then_inc(up_done, 1)
                    if f == 1:
                        down(turn, i - 1)
                        if ahead:
                            transposes(turn, i + 1)

            pe.sem_inc(result_done, 1)
            transposes(0, 0)
            for i in range(2):
                step(0, i)
            with pe.Fori(1, E // 2 - 1) as turn:
                for i in range(2):
                    step(turn, i)
            step(E // 2 - 1, 0)
            step(E // 2 - 1, 1, ahead=False)
            down(E // 2, -1)


def attention1(core, g, io):
    nc = core.nc
    with ExitStack() as stack:
        c = core.scope(stack)
        N1 = H1 * M
        INNER = H1 * DH1
        HC = 4
        PC = H1 // HC
        OC = 2
        OB = INNER // P // OC
        wo = c.split("wo1", [P, INNER // P, D])
        xnT = c.split("xn1T", [D, T])
        moments = c.sb("ln_moments2", [P, TT, 2])
        var_eps, rstd = c.sb("ln_var2", [P, TT]), c.sb("ln_rstd2", [P, TT])

        with ExitStack() as head_stack:
            h = core.scope(head_stack)
            wo_raw = h.sb("wo1_raw", [P, INNER // P, D])
            xn = h.sb("xn1", [P, TT, D])
            stats = h.sb("ln_stats2", [P, TT, 6])
            gated_bias = h.sb("gated_bias", [P, D])
            wo_loaded, var_done, rstd_done = h.sem("e_wold"), h.sem("e_var"), h.sem("e_rstd")
            xn_done, turned, hi_done, dve_step = h.sem("e_xn"), h.sem("e_turned0"), h.sem("e_hi0"), h.sem("e_dve0")
            wo_hi = h.sem("e_wohi")
            turned_ps = g.psum[:, 0:2, :].rearrange("p b n -> p (b n)")
            block = head_stack.enter_context(nc.Block())

            @block.sync
            def _(sp):
                sp.dma_start(wo_raw[:], io["L1_xattn_Wo"].rearrange("(t p) d -> p t d", p=P)).then_inc(wo_loaded, 16)

            @block.gpsimd
            def _(pool):
                pool.wait_ge(var_done, 1)
                pool.tensor_tensor(rstd[:], var_eps[:], g.minus_half[:], ALU.pow).then_inc(rstd_done, 1)

            @block.scalar
            def _(act):
                act.wait_ge(wo_loaded, 16)
                act.copy(wo.hi, wo_raw[:]).then_inc(wo_hi, 1)
                act.wait_ge(turned, 1)
                act.copy(xnT.hi, turned_ps).then_inc(hi_done, 1)

            @block.vector
            def _(dve):
                step = Chain(dve, dve_step)
                layernorm_stats(dve, step, g.x, stats, moments, var_eps).then_inc(var_done, 1)
                step(dve.tensor_scalar(gated_bias[:], g.bias1[:], g.gates[:, 1:2], None, ALU.mult))
                dve.wait_ge(rstd_done, 1)
                last = layernorm_apply(dve, g.x, moments, rstd, xn)
                last.then_inc(xn_done, 1)
                dve.wait_ge(xn_done, 1)
                dve.tensor_tensor(g.x[:], g.x[:], gated_bias[:].unsqueeze(1).to_broadcast([P, TT, D]), ALU.add)
                dve.wait_ge(wo_hi, 1)
                dve.tensor_tensor(wo.lo, wo_raw[:], f32(wo.hi), ALU.subtract)
                dve.wait_ge(hi_done, 1)
                dve.tensor_tensor(xnT.lo, turned_ps, f32(xnT.hi), ALU.subtract)

            @block.tensor
            def _(pe):
                pe.wait_ge(xn_done, 1)
                for t in range(TT):
                    last = pe.transpose(turned_ps[:, t * P:(t + 1) * P], xn[:, t, :], g.ident[:])
                last.then_inc(turned, 1)

        queries = [c.split(f"queries1_{i}", [D, P]) for i in range(2)]
        values = [c.split(f"values1_{i}", [M, INNER]) for i in range(2)]
        maximum = c.sb("max1", [P, H1])
        den, rden = c.sb("den1", [P, H1]), c.sb("rden1", [P, H1])
        weights = [c.sb(f"weights1_{i}", [P, H1, M]) for i in range(2)]
        partsT = [c.split(f"parts1T{i}", [P, HC * P]) for i in range(2)]
        outT = c.split("out1T", [P, OC, OB * P])
        heads_out = c.sb("heads_out", [P, INNER])

        queries_ready, v_hi, v_lo = c.sem("e_q"), c.sem("e_vhi"), c.sem("e_vlo")
        scores_done, max_done, sub_done, exp_done = (c.sem("e_" + n) for n in ("scores", "max", "sub", "exp"))
        den_done, rden_done, norm_done = c.sem("e_den"), c.sem("e_rden"), c.sem("e_norm")
        turned, hi_done, lo_done = c.sem("e_turned"), c.sem("e_hi"), c.sem("e_lo")
        pv_done, out_done = c.sem("e_pv"), c.sem("e_out")
        oturned, ohi_done, olo_done = c.sem("e_oturned"), c.sem("e_ohi"), c.sem("e_olo")
        wo_done, x_done = c.sem("e_wo"), c.sem("e_x")

        GROUPS = [(0, 0, 6), (1, 6, 12), (2, 12, 16)]

        def scores_views(per_key):
            yield g.psum[:, 0:2, 0:6 * M].rearrange("p b (h k) -> p b h k", k=M), slice(0, 12)
            yield g.psum[:, 2:3, 0:4 * M].rearrange("p b (h k) -> p b h k", k=M), slice(12, 16)

        def chunk_bank(i):
            return g.psum[:, 3 + i % 2, :]

        outs = g.psum[:, 5:7, :].rearrange("p b n -> p (b n)")
        final = g.psum[:, 7, 0:D]

        def before(turn, b):
            return isinstance(turn, int) and turn == 0 and b < 0

        def turns(step, engine):
            for i in range(2):
                step(0, i)
            with engine.Fori(1, B // 2) as turn:
                for i in range(2):
                    step(turn, i)
            for i in range(2):
                step(B // 2, i, drain=True)

        block = stack.enter_context(nc.Block())

        @block.gpsimd
        def _(pool):
            def step(turn, i, drain=False):
                b = turn * 2 + i
                if drain:
                    return
                pool.wait_ge(v_hi, b + 1)
                pool.tensor_tensor(values[i].lo, g.values1[:, bass.ds(b, 1), :].rearrange("p o n -> p (o n)"),
                                   f32(values[i].hi), ALU.subtract).then_inc(v_lo, 1)
                pool.wait_ge(rden_done, b + 1)
                pool.tensor_tensor(weights[i][:], weights[i][:], rden[:].unsqueeze(2).to_broadcast([P, H1, M]),
                                   ALU.mult).then_inc(norm_done, 1)

            turns(step, pool)

        @block.scalar
        def _(act):
            def step(turn, i, drain=False):
                b = turn * 2 + i
                if not before(turn, i - 2):
                    for o in range(OC):
                        act.wait_ge(oturned, (b - 2) * OC + o + 1)
                        wait(act, wo_done, b - 1)
                        act.copy(outT.hi[:, o, :], chunk_bank(o)).then_inc(ohi_done, 1)
                if not drain:
                    act.wait_ge(sub_done, b + 1)
                    act.activation(weights[i][:], weights[i][:], ACT.Exp).then_inc(exp_done, 1)
                if not before(turn, i - 1) and not (drain and i == 1):
                    for p in range(PC):
                        n = (b - 1) * PC + p
                        act.wait_ge(turned, n + 1)
                        wait(act, pv_done, n - 1)
                        act.copy(partsT[p % 2].hi[0:M, :], chunk_bank(p)[0:M, :]).then_inc(hi_done, 1)
                    act.wait_ge(pv_done, b * PC)
                    wait(act, oturned, (b - 1) * OC)
                    act.copy(heads_out[:], outs).then_inc(out_done, 1)

            turns(step, act)

        @block.vector
        def _(dve):
            def step(turn, i, drain=False):
                b = turn * 2 + i
                if not drain:
                    wait(dve, scores_done, b - 1)
                    at = bass.ds(b * P, P)
                    dve.tensor_copy(queries[i].hi, f32(xnT.hi[:, at])).then_inc(queries_ready, 1)
                    dve.tensor_copy(queries[i].lo, f32(xnT.lo[:, at])).then_inc(queries_ready, 1)
                    wait(dve, pv_done, (b - 1) * PC)
                    dve.tensor_copy(values[i].hi, g.values1[:, bass.ds(b, 1), :].rearrange("p o n -> p (o n)")
                                    ).then_inc(v_hi, 1)
                if not before(turn, i - 2):
                    for o in range(OC):
                        dve.wait_ge(ohi_done, (b - 2) * OC + o + 1)
                        dve.tensor_tensor(outT.lo[:, o, :], chunk_bank(o), f32(outT.hi[:, o, :]),
                                          ALU.subtract).then_inc(olo_done, 1)
                if not drain:
                    dve.wait_ge(scores_done, b + 1)
                    wait(dve, sub_done, b)
                    for ps, hs in scores_views(M):
                        last = dve.tensor_reduce(maximum[:, hs].rearrange("p (b h) -> p b h", b=ps.shape[1]),
                                                 ps, AX.X, ALU.max)
                    last.then_inc(max_done, 1)
                    dve.wait_ge(max_done, b + 1)
                    wait(dve, turned, (b - 1) * PC)
                    for ps, hs in scores_views(M):
                        nb = ps.shape[1]
                        last = dve.tensor_tensor(
                            weights[i][:, hs, :].rearrange("p (b h) k -> p b h k", b=nb), ps,
                            maximum[:, hs].rearrange("p (b h) -> p b h", b=nb).unsqueeze(3)
                            .to_broadcast([P, nb, ps.shape[2], M]), ALU.subtract)
                    last.then_inc(sub_done, 1)
                if not before(turn, i - 1) and not (drain and i == 1):
                    for p in range(PC):
                        n = (b - 1) * PC + p
                        dve.wait_ge(hi_done, n + 1)
                        dve.tensor_tensor(partsT[p % 2].lo[0:M, :], chunk_bank(p)[0:M, :],
                                          f32(partsT[p % 2].hi[0:M, :]), ALU.subtract).then_inc(lo_done, 1)
                if not drain:
                    dve.wait_ge(exp_done, b + 1)
                    dve.tensor_reduce(den[:], weights[i][:], AX.X, ALU.add).then_inc(den_done, 1)
                    dve.wait_ge(den_done, b + 1)
                    wait(dve, norm_done, b)
                    dve.reciprocal(rden[:], den[:]).then_inc(rden_done, 1)
                if not before(turn, i - 2):
                    dve.wait_ge(wo_done, b)
                    rows = g.x[:, bass.ds(b - 2, 1), :].rearrange("p o d -> p (o d)")
                    dve.scalar_tensor_tensor(out=rows, in0=final, scalar=g.gates[:, 1:2], in1=rows,
                                             op0=ALU.mult, op1=ALU.add).then_inc(x_done, 1)

            turns(step, dve)

        @block.tensor
        def _(pe):
            def step(turn, i, drain=False):
                b = turn * 2 + i
                weights_turn = not before(turn, i - 1) and not (drain and i == 1)

                def turn_weights(p):
                    if p == 0:
                        pe.wait_ge(norm_done, b)
                        wait(pe, olo_done, (b - 1) * OC)
                    if p < 2:
                        wait(pe, lo_done, (b - 1) * PC - 2 + p + 1)
                    else:
                        pe.wait_ge(lo_done, (b - 1) * PC + p - 1)
                    for q in range(HC):
                        last = pe.transpose(chunk_bank(p)[0:M, q * P:(q + 1) * P],
                                            weights[(i - 1) % 2][:, p * HC + q, :], g.ident[:])
                    last.then_inc(turned, 1)

                def multiply_values(p):
                    n = (b - 1) * PC + p
                    pe.wait_ge(lo_done, n + 1)
                    if p == 0:
                        pe.wait_ge(v_lo, b)
                        wait(pe, out_done, b - 1)
                    for q in range(HC):
                        hd = p * HC + q
                        last = matmul3(pe, outs[:, hd * DH1:(hd + 1) * DH1], partsT[p % 2][0:M, q * P:(q + 1) * P],
                                       values[(i - 1) % 2][:, hd * DH1:(hd + 1) * DH1])
                    last.then_inc(pv_done, 1)

                if not drain:
                    pe.wait_ge(queries_ready, b * 2 + 2)
                    wait(pe, sub_done, b)
                    for bank, a, z in GROUPS:
                        last = matmul3(pe, g.psum[:, bank, 0:(z - a) * M], queries[i],
                                       g.keys1[:, bass.ds(b, 1), a:z, :].view("p o h k -> p (o h k)"))
                    last.then_inc(scores_done, 1)
                if not before(turn, i - 2):
                    pe.wait_ge(out_done, b - 1)
                    pe.wait_ge(lo_done, (b - 1) * PC)
                    for o in range(OC):
                        for q in range(OB):
                            at = (o * OB + q) * P
                            last = pe.transpose(chunk_bank(o)[:, q * P:(q + 1) * P], heads_out[:, at:at + P], g.ident[:])
                        last.then_inc(oturned, 1)
                if weights_turn:
                    turn_weights(0)
                    turn_weights(1)
                if not before(turn, i - 2):
                    pe.wait_ge(olo_done, (b - 1) * OC)
                    wait(pe, x_done, b - 1)
                    for n in range(OC * OB):
                        last = matmul3(pe, final, outT[:, n // OB, (n % OB) * P:(n % OB + 1) * P], wo[:, n, :],
                                       start=n == 0, stop=n == OC * OB - 1)
                    last.then_inc(wo_done, 1)
                if weights_turn:
                    multiply_values(0)
                    turn_weights(2)
                    multiply_values(1)
                    turn_weights(3)
                    multiply_values(2)
                    multiply_values(3)

            pe.sem_inc(wo_done, 1)
            pe.sem_inc(x_done, 1)
            turns(step, pe)


def experts1(core, g, io, out):
    nc = core.nc
    with ExitStack() as stack:
        c = core.scope(stack)
        HALF = T // 2
        UNITS = FT * 2
        xnT = c.split("xn2T", [D, T])
        mix = c.sb("mix", [P, E, TT])
        raw = [[c.sb(f"fw{i}_{n}", [P, F]) for n in range(3)] for i in range(2)]
        w_loaded = [c.sem(f"f_wld{i}") for i in range(2)]
        names = ("L1_ffn_w_gate", "L1_ffn_w_up", "L1_ffn_w_down")

        def load_weights(sp, e, i):
            for n, name in enumerate(names):
                w = io[name]
                if n < 2:
                    src = w.rearrange("e d f -> (e d) f")[bass.ds(e * D, D), :]
                    sp.dma_start(raw[i][n][:], src).then_inc(w_loaded[i], 16)
                else:
                    src = w.rearrange("e f d -> (e f) d")[bass.ds(e * F, F), :]
                    sp.dma_start(raw[i][n][:].rearrange("p (t d) -> p t d", d=D),
                                 src.rearrange("(t p) d -> p t d", p=P)).then_inc(w_loaded[i], 16)

        with ExitStack() as head_stack:
            h = core.scope(head_stack)
            routers = h.sb("routers", [D, 2, E])
            xn, xnT_raw = h.sb("xn2", [P, TT, D]), h.sb("xn2T_raw", [D, T])
            stats, moments = h.sb("ln_stats3", [P, TT, 6]), h.sb("ln_moments3", [P, TT, 2])
            var_eps, rstd = h.sb("ln_var3", [P, TT]), h.sb("ln_rstd3", [P, TT])
            top = h.sb("top", [P, TT, 2])
            probs = h.sb("probs", [P, TT, 2, E])
            sums, rsums = h.sb("sums", [P, TT, 2]), h.sb("rsums", [P, TT, 2])
            both, bsum, rbsum = h.sb("both", [P, TT, E]), h.sb("bsum", [P, TT]), h.sb("rbsum", [P, TT])
            r_loaded, var_done, rstd_done = h.sem("f_rld"), h.sem("f_var"), h.sem("f_rstd")
            xn_done, turned, raw_done, hi_done = (h.sem("f_" + n) for n in ("xn", "turned", "raw", "hi"))
            logits_done, shifted, exp_done, dve_step = (h.sem("f_" + n) for n in ("logits", "shifted", "exp", "dve"))
            turned_ps = g.psum[:, 0:2, :].rearrange("p b n -> p (b n)")
            logits_ps = g.psum[:, 2, 0:TT * 2 * E].rearrange("p (t r e) -> p t r e", r=2, e=E)
            block = head_stack.enter_context(nc.Block())

            @block.sync
            def _(sp):
                sp.dma_start(routers[:, 0, :], io["L1_ffn_w_router"]).then_inc(r_loaded, 16)
                sp.dma_start(routers[:, 1, :], io["L1_ffn_w_gating"]).then_inc(r_loaded, 16)
                for i in range(2):
                    load_weights(sp, i, i)

            @block.gpsimd
            def _(pool):
                pool.wait_ge(var_done, 1)
                pool.tensor_tensor(rstd[:], var_eps[:], g.minus_half[:], ALU.pow).then_inc(rstd_done, 1)

            @block.scalar
            def _(act):
                act.wait_ge(turned, 1)
                act.copy(xnT_raw[:], turned_ps).then_inc(raw_done, 1)
                act.copy(xnT.hi, turned_ps).then_inc(hi_done, 1)
                act.wait_ge(shifted, 1)
                act.activation(probs[:, :, 0, :], probs[:, :, 0, :], ACT.Exp)
                act.activation(probs[:, :, 1, :], probs[:, :, 1, :], ACT.Exp, scale=10.0).then_inc(exp_done, 1)

            @block.vector
            def _(dve):
                step = Chain(dve, dve_step)
                layernorm_stats(dve, step, g.x, stats, moments, var_eps).then_inc(var_done, 1)
                dve.wait_ge(rstd_done, 1)
                layernorm_apply(dve, g.x, moments, rstd, xn).then_inc(xn_done, 1)
                dve.wait_ge(logits_done, 1)
                step(dve.tensor_reduce(top[:], logits_ps, AX.X, ALU.max))
                dve.tensor_tensor(probs[:], logits_ps, top[:].unsqueeze(3).to_broadcast([P, TT, 2, E]),
                                  ALU.subtract).then_inc(shifted, 1)
                dve.wait_ge(hi_done, 1)
                dve.tensor_tensor(xnT.lo, turned_ps, f32(xnT.hi), ALU.subtract)
                dve.wait_ge(exp_done, 1)
                step(dve.tensor_reduce(sums[:], probs[:], AX.X, ALU.add))
                step(dve.reciprocal(rsums[:], sums[:]))
                step(dve.tensor_tensor(probs[:], probs[:], rsums[:].unsqueeze(3).to_broadcast([P, TT, 2, E]), ALU.mult))
                step(dve.tensor_tensor(both[:], probs[:, :, 0, :], probs[:, :, 1, :], ALU.mult))
                step(dve.tensor_reduce(bsum[:], both[:], AX.X, ALU.add))
                step(dve.tensor_scalar(bsum[:], bsum[:], 1e-9, None, ALU.add))
                step(dve.reciprocal(rbsum[:], bsum[:]))
                step(dve.tensor_scalar(rbsum[:], rbsum[:], g.gates[:, 3:4], None, ALU.mult))
                step(dve.tensor_tensor(mix[:].rearrange("p e t -> p t e"), both[:],
                                       rbsum[:].unsqueeze(2).to_broadcast([P, TT, E]), ALU.mult))

            @block.tensor
            def _(pe):
                pe.wait_ge(xn_done, 1)
                for t in range(TT):
                    last = pe.transpose(turned_ps[:, t * P:(t + 1) * P], xn[:, t, :], g.ident[:])
                last.then_inc(turned, 1)
                pe.wait_ge(raw_done, 1)
                pe.wait_ge(r_loaded, 32)
                for t in range(TT):
                    last = pe.matmul(logits_ps[:, t].rearrange("p r e -> p (r e)"), xnT_raw[:, t * P:(t + 1) * P],
                                     routers[:].rearrange("p r e -> p (r e)"), start=True, stop=True)
                last.then_inc(logits_done, 1)

        parts = [[c.split(f"fws{i}_{n}", [P, F]) for n in range(3)] for i in range(2)]
        silu = [c.sb(f"fsilu{i}", [P, HALF]) for i in range(2)]
        hidden = [c.sb(f"fhidden{i}", [P, HALF]) for i in range(2)]
        hid = [c.split(f"fhid{i}", [P, FT, T]) for i in range(2)]
        w_hi, w_lo = c.sem("f_whi"), c.sem("f_wlo")
        up_done, silu_done, mult_done = c.sem("f_up"), c.sem("f_silu"), c.sem("f_mult")
        hid_hi, hid_lo = c.sem("f_hidhi"), c.sem("f_hidlo")
        down_done, sum_done, stored = c.sem("f_down"), c.sem("f_sum"), c.sem("f_stored")
        DC = 2
        DT = TT // DC

        def up_bank(n, which):
            return g.psum[:, 2 * (n % 2) + which, :]

        def down_ps(d):
            return g.psum[:, 4 + d, :].rearrange("p (t d) -> p t d", d=D)

        def turns(step, engine):
            for i in range(2):
                step(0, i)
            with engine.Fori(1, E // 2 - 1) as turn:
                for i in range(2):
                    step(turn, i)
            for i in range(2):
                step(E // 2 - 1, i)
            step(E // 2, 0, drain=True)

        def before(turn, i):
            return isinstance(turn, int) and turn == 0 and i < 0

        def ahead(turn, i):
            return not (isinstance(turn, int) and turn * 2 + i + 1 >= E)

        block = stack.enter_context(nc.Block())

        @block.sync
        def _(sp):
            def step(turn, i, drain=False):
                if drain or (isinstance(turn, int) and turn == 0):
                    return
                e = turn * 2 + i
                sp.wait_ge(w_lo, e - 1)
                load_weights(sp, e, i)

            turns(step, sp)
            for t in range(TT):
                if t % DT == 0:
                    sp.wait_ge(sum_done, (E - 1) * DC + t // DT + 1)
                sp.dma_start(out[t * P:(t + 1) * P, :], g.x[:, t, :]).then_inc(stored, 16)
            sp.wait_ge(stored, 16 * TT)

        @block.gpsimd
        def _(pool):
            def step(turn, i, drain=False):
                if drain:
                    return
                e = turn * 2 + i
                wait(pool, down_done, (e - 1) * DC)
                for n in range(3):
                    pool.wait_ge(w_hi, e * 3 + n + 1)
                    last = pool.tensor_tensor(parts[i][n].lo, raw[i][n][:], f32(parts[i][n].hi), ALU.subtract)
                last.then_inc(w_lo, 1)

            turns(step, pool)

        @block.scalar
        def _(act):
            def split_weights(turn, i):
                e = turn * 2 + i
                act.wait_ge(w_loaded[i % 2], (turn + i // 2) * 48 + 48)
                wait(act, down_done, (e - 1) * DC)
                for n in range(3):
                    act.copy(parts[i % 2][n].hi, raw[i % 2][n][:]).then_inc(w_hi, 1)

            def step(turn, i, drain=False):
                if drain:
                    return
                e = turn * 2 + i
                for u in range(UNITS):
                    n = e * UNITS + u
                    act.wait_ge(up_done, n + 1)
                    wait(act, mult_done, n - 1)
                    act.activation(silu[u % 2][:], up_bank(u, 0), ACT.Silu).then_inc(silu_done, 1)
                    act.wait_ge(mult_done, n + 1)
                    act.copy(hid[i].hi[:, u // 2, (u % 2) * HALF:(u % 2 + 1) * HALF],
                             hidden[u % 2][:]).then_inc(hid_hi, 1)
                    if u == 4 and ahead(turn, i):
                        split_weights(turn, i + 1)

            split_weights(0, 0)
            turns(step, act)

        @block.vector
        def _(dve):
            def step(turn, i, drain=False):
                e = turn * 2 + i

                def add(d):
                    dve.wait_ge(down_done, (e - 1) * DC + d + 1)
                    wait(dve, sum_done, (e - 2) * DC + d + 1)
                    for t in range(DT):
                        at = d * DT + t
                        last = dve.scalar_tensor_tensor(
                            out=g.x[:, at, :], in0=down_ps(d)[:, t, :],
                            scalar=mix[:].rearrange("p e t -> p (e t)")[:, bass.ds((e - 1) * TT + at, 1)],
                            in1=g.x[:, at, :], op0=ALU.mult, op1=ALU.add)
                    last.then_inc(sum_done, 1)

                for u in range(UNITS):
                    n = e * UNITS + u
                    if not drain:
                        dve.wait_ge(silu_done, n + 1)
                        wait(dve, hid_lo, n - 1)
                        if u == 0:
                            wait(dve, down_done, (e - 1) * DC)
                        dve.tensor_tensor(hidden[u % 2][:], silu[u % 2][:], up_bank(u, 1), ALU.mult).then_inc(mult_done, 1)
                        dve.wait_ge(hid_hi, n + 1)
                        at = slice((u % 2) * HALF, (u % 2 + 1) * HALF)
                        dve.tensor_tensor(hid[i].lo[:, u // 2, at], hidden[u % 2][:], f32(hid[i].hi[:, u // 2, at]),
                                          ALU.subtract).then_inc(hid_lo, 1)
                    if u in (3, 5) and not before(turn, i - 1):
                        add((u - 3) // 2)

            turns(step, dve)

        @block.tensor
        def _(pe):
            def step(turn, i, drain=False):
                e = turn * 2 + i

                def down(d):
                    pe.wait_ge(hid_lo, e * UNITS)
                    wait(pe, sum_done, (e - 2) * DC + d + 1)
                    w = parts[(i - 1) % 2][2].view("p (t d) -> p t d", d=D)
                    for t in range(DT):
                        at = (d * DT + t) * P
                        for f in range(FT):
                            last = matmul3(pe, down_ps(d)[:, t, :], hid[(i - 1) % 2][:, f, at:at + P], w[:, f, :],
                                           start=f == 0, stop=f == FT - 1)
                    last.then_inc(down_done, 1)

                if not drain:
                    pe.wait_ge(w_lo, e + 1)
                for u in range(UNITS):
                    n = e * UNITS + u
                    if not drain:
                        wait(pe, mult_done, n - 1)
                        for which in range(2):
                            f, at = u // 2, (u % 2) * HALF
                            last = matmul3(pe, up_bank(u, which), parts[i][which][:, f * P:(f + 1) * P],
                                           xnT[:, at:at + HALF])
                        last.then_inc(up_done, 1)
                    if u in (1, 3) and not before(turn, i - 1):
                        down((u - 1) // 2)

            turns(step, pe)


def alloc(core, nc):
    class Shared:
        pass

    g = Shared()
    g.psum = core.stack.enter_context(nc.psum_tensor("ps_all", [P, 8, BANK], F32))
    g.x = core.sb("x", [P, TT, D])
    g.attended = core.sb("attended", [P, TT * D])
    g.ident = core.sb("ident", [P, P])
    g.zeros = core.sb("zeros", [P, 4 * D])
    g.minus_half = core.sb("minus_half", [P, TT])
    g.bias0 = core.sb("bias0", [P, D])
    g.bias1 = core.sb("bias1", [P, D])
    g.gates = core.sb("gates", [P, 4])
    g.gather_at = core.sb("gather_at", [P, TOPK, TT], U32)
    g.token_weights = core.sb("token_weights", [P, TOPK, TT])
    g.ctxT = core.split("ctxT", [C, KEYS])
    g.expert_in = nc.dram_tensor("expert_in", [SLOTS, D], F32, kind="Internal").ap()
    g.expert_out = nc.dram_tensor("expert_out", [SLOTS, D], F32, kind="Internal").ap()
    g.expert_in_zeroed = core.sem("expert_in_zeroed")
    return g


def flamingo(nc, io, out, until=None):
    io = dict(io)
    io["x"] = io["x"].rearrange("b s d -> (b s) d")
    io["ctx"] = io["ctx_768"].rearrange("b m c -> (b m) c")
    with ExitStack() as stack:
        core = Core(nc, stack)
        g = alloc(core, nc)
        with ExitStack() as layer0:
            c0 = core.scope(layer0)
            g.xnT = c0.split("xnT", [D, T])
            g.keys0 = c0.split("keys0", [D, H0, KEYS])
            g.values0 = c0.split("values0", [P, KT, H0 * D])
            prepare0(core, g, io)
            attention0(core, g)
        if until == "attention0":
            dump(core, g.attended[:], out)
            return
        with ExitStack() as layer1:
            c1 = core.scope(layer1)
            g.keys1 = c1.split("keys1", [D, B, H1, M])
            g.values1 = c1.sb("values1", [M, B, H1 * DH1])
            dispatch(core, g, io)
            if until == "dispatch":
                dump(core, g.expert_in, out)
                return
            with ExitStack() as only:
                g.gathered = core.scope(only).sb("gathered", [P, TT, TOPK, D])
                experts0(core, g, io)
            if until == "experts0":
                dump(core, g.x[:].rearrange("p t d -> p (t d)"), out)
                return
            attention1(core, g, io)
            if until == "attention1":
                dump(core, g.x[:].rearrange("p t d -> p (t d)"), out)
                return
        experts1(core, g, io, out.rearrange("b s d -> (b s) d"))


def dump(core, ap, out):
    with core.nc.semaphore("dump") as s, core.nc.Block() as block:
        @block.sync
        def _(sp):
            sp.dma_start(out, ap).then_inc(s, 16)
            sp.wait_ge(s, 16)


_INS = ["x", "ctx_768", "g_xattn", "g_ffn",
        "L0_xattn_Wq", "L0_xattn_Wk", "L0_xattn_Wv", "L0_xattn_Wout", "L0_xattn_bout",
        "L0_ffn_Wr", "L0_ffn_W1", "L0_ffn_W3", "L0_ffn_W2",
        "L1_xattn_Wq", "L1_xattn_Wk", "L1_xattn_Wv", "L1_xattn_Wo", "L1_xattn_bo",
        "L1_ffn_w_router", "L1_ffn_w_gating", "L1_ffn_w_gate", "L1_ffn_w_up", "L1_ffn_w_down"]


def kernel(**inputs):
    import concourse.bacc as _bacc
    from concourse.bass_utils import run_bass_kernel_spmd as _run

    nc = _bacc.Bacc("TRN2", target_bir_lowering=False, num_devices=1)
    arrays, io = {}, {}
    for name in _INS:
        a = np.ascontiguousarray(inputs[name])
        arrays[f"in_{name}_dram"] = a
        io[name] = nc.dram_tensor(f"in_{name}_dram", a.shape, mybir.dt.from_np(a.dtype), kind="ExternalInput").ap()
    out = nc.dram_tensor("out_dram", (B, S, D), F32, kind="ExternalOutput").ap()
    flamingo(nc, io, out)
    r = _run(nc, [arrays], core_ids=[0])
    return r.results[0]["out_dram"]
```

```python
from contextlib import ExitStack

import numpy as np

import concourse.bass as bass
from concourse import mybir

F32 = mybir.dt.float32
F32R = mybir.dt.float32r
BF16 = mybir.dt.bfloat16
U32 = mybir.dt.uint32
ALU = mybir.AluOpType
ACT = mybir.ActivationFunctionType
AX = mybir.AxisListType

P = 128
D = 128
C = 96
B, S, M = 8, 128, 77
T = B * S
TT = T // P
KEYS = B * M
KT = -(-KEYS // P)
KLAST = KEYS - (KT - 1) * P
H0, DH0 = 8, 128
H1, DH1 = 16, 64
E, F = 8, 512
FT = F // P
TOPK = 2
CAP = max(1, -(-T * TOPK * 5 // (4 * E)))
SLOTS = E * CAP
EPS = 1e-5
BANK = 512
SCALE0 = 1.5 * DH0 ** -0.5
SCALE1 = DH1 ** -0.5


def f32(ap):
    return ap.bitcast(F32)


class Split:

    def __init__(self, hi, lo):
        self.hi, self.lo = hi, lo

    def __getitem__(self, at):
        return Split(self.hi[at], self.lo[at])

    def view(self, pattern, **sizes):
        return Split(self.hi.rearrange(pattern, **sizes), self.lo.rearrange(pattern, **sizes))


def matmul3(pe, out, lhsT, rhs, start=True, stop=True):
    pe.matmul(out, lhsT.hi, rhs.hi, start=start, stop=False)
    pe.matmul(out, lhsT.hi, rhs.lo, start=False, stop=False)
    return pe.matmul(out, lhsT.lo, rhs.hi, start=False, stop=stop)


class Core:

    def __init__(self, nc, stack):
        self.nc, self.stack = nc, stack

    def scope(self, stack):
        return Core(self.nc, stack)

    def sb(self, name, shape, dt=F32):
        return self.stack.enter_context(self.nc.sbuf_tensor("sb_" + name, shape, dt))

    def split(self, name, shape):
        return Split(self.sb(name + "_hi", shape, F32R)[:], self.sb(name + "_lo", shape, F32R)[:])

    def sem(self, name):
        return self.stack.enter_context(self.nc.semaphore(name))


def wait(eng, sem, value):
    if not (isinstance(value, int) and value <= 0):
        eng.wait_ge(sem, value)


class Chain:

    def __init__(self, eng, sem):
        self.eng, self.sem, self.n = eng, sem, 0

    def __call__(self, instruction):
        self.n += 1
        instruction.then_inc(self.sem, 1)
        self.eng.wait_ge(self.sem, self.n)
        return instruction


def layernorm_stats(dve, step, x, stats, moments, variance_eps):
    for t in range(TT):
        last = dve.bn_stats(stats[:, t, :], x[:, t, :])
    step(last)
    for t in range(TT):
        last = dve.bn_aggr(moments[:, t, :], stats[:, t, :])
    step(last)
    return dve.tensor_scalar(variance_eps[:], moments[:, :, 1], EPS, None, ALU.add)


def layernorm_apply(dve, x, moments, rstd, xn):
    for t in range(TT):
        last = dve.tensor_scalar(xn[:, t, :], x[:, t, :], moments[:, t, 0:1], rstd[:, t:t + 1],
                                 ALU.subtract, ALU.mult)
    return last


def prepare0(core, g, io):
    nc = core.nc
    with ExitStack() as stack:
        c = core.scope(stack)
        wq = c.sb("wq0", [P, H0 * DH0])
        wk = c.sb("wk0", [C, H0 * DH0])
        wv = c.sb("wv0", [C, H0 * DH0])
        wout = c.sb("wout0", [P, H0, D])
        ctx_rows = c.sb("ctx_rows", [P, KT, C])
        wqT, wkT, wvT = (c.split(n, [P, H0, w]) for n, w in (("wq0T", D), ("wk0T", C), ("wv0T", C)))
        wout_s = c.split("wout0s", [P, H0, D])
        qk = c.split("qk0", [C, H0, D])
        vo = c.split("vo0", [C, H0 * D])
        xn = c.sb("xn_first", [P, TT, D])
        stats = c.sb("ln_stats0", [P, TT, 6])
        moments = c.sb("ln_moments0", [P, TT, 2])
        var_eps = c.sb("ln_var0", [P, TT])
        rstd = c.sb("ln_rstd0", [P, TT])
        gates_raw = c.sb("gates_raw", [P, 4])

        loaded = {n: c.sem("a_ld_" + n) for n in ("x", "ctx", "wq", "wk", "wv", "wout", "small")}
        ident_done, zero_done = c.sem("a_ident"), c.sem("a_zero")
        var_done, rstd_done, xn_done = c.sem("a_var"), c.sem("a_rstd"), c.sem("a_xn")
        pe_done, hi_done, lo_done = c.sem("a_pe"), c.sem("a_hi"), c.sem("a_lo")
        wout_hi, wout_lo, dve_step = c.sem("a_wouthi"), c.sem("a_woutlo"), c.sem("a_dve")

        CTX, WQ, WK, WV, QK, VO, XN = range(7)
        K0 = 7
        V0 = K0 + H0
        JOBS = V0 + KT

        def slot(j):
            return g.psum[:, 2 * (j % 4):2 * (j % 4) + 2, :].rearrange("p b n -> p (b n)")

        def evacuation(j):
            ps = slot(j)
            if j == CTX:
                return ps[0:C, 0:KEYS], g.ctxT, 1.0
            if j == WQ:
                return ps.rearrange("p (h n) -> p h n", n=P), wqT, 1.0
            if j in (WK, WV):
                return ps.rearrange("p (h n) -> p h n", n=P)[:, :, 0:C], (wkT, wvT)[j - WK], 1.0
            if j == QK:
                return ps[0:C, :].rearrange("p (h n) -> p h n", n=P), qk, SCALE0
            if j == VO:
                return ps[0:C, :], vo, 1.0
            if j == XN:
                return ps, g.xnT, 1.0
            if j < V0:
                half = ps.rearrange("p (b n) -> p b n", b=2)[:, :, 0:KEYS // 2]
                return half, g.keys0[:, j - K0, :].view("p (b n) -> p b n", b=2), 1.0
            kt = j - V0
            rows = P if kt < KT - 1 else KLAST
            return ps[0:rows, :], g.values0[0:rows, kt, :], 1.0

        block = stack.enter_context(nc.Block())

        @block.sync
        def _(sp):
            sp.dma_start(ctx_rows[:, 0:KT - 1, :],
                         io["ctx"][0:(KT - 1) * P, :].rearrange("(t p) c -> p t c", p=P)).then_inc(loaded["ctx"], 16)
            sp.dma_start(ctx_rows[0:KLAST, KT - 1, :], io["ctx"][(KT - 1) * P:KEYS, :]).then_inc(loaded["ctx"], 16)
            sp.dma_start(wq[:], io["L0_xattn_Wq"]).then_inc(loaded["wq"], 16)
            sp.dma_start(wk[:], io["L0_xattn_Wk"]).then_inc(loaded["wk"], 16)
            sp.wait_ge(zero_done, 1)
            for e in range(E):
                sp.dma_start(g.expert_in[e * CAP:(e + 1) * CAP, :].rearrange("(p r) d -> p (r d)", r=4),
                             g.zeros[0:CAP // 4, :]).then_inc(g.expert_in_zeroed, 16)

        @block.scalar
        def _(act):
            act.dma_start(g.x[:], io["x"].rearrange("(t p) d -> p t d", p=P)).then_inc(loaded["x"], 16)
            act.dma_start(wv[:], io["L0_xattn_Wv"]).then_inc(loaded["wv"], 16)
            act.dma_start(wout[:], io["L0_xattn_Wout"].rearrange("(h p) d -> p h d", p=P)).then_inc(loaded["wout"], 16)
            act.dma_start(g.bias0[:], io["L0_xattn_bout"].partition_broadcast(P)).then_inc(loaded["small"], 16)
            act.dma_start(g.bias1[:], io["L1_xattn_bo"].partition_broadcast(P)).then_inc(loaded["small"], 16)
            act.dma_start(gates_raw[:, 0:2], io["g_xattn"].partition_broadcast(P)).then_inc(loaded["small"], 16)
            act.dma_start(gates_raw[:, 2:4], io["g_ffn"].partition_broadcast(P)).then_inc(loaded["small"], 16)
            for j in range(JOBS):
                if j == QK:
                    act.wait_ge(loaded["wout"], 16)
                    act.copy(wout_s.hi, wout[:]).then_inc(wout_hi, 1)
                ps, to, factor = evacuation(j)
                act.wait_ge(pe_done, j + 1)
                act.activation(to.hi, ps, ACT.Copy, scale=factor).then_inc(hi_done, 1)
            act.wait_ge(loaded["small"], 64)
            act.activation(g.gates[:], gates_raw[:], ACT.Tanh).then_inc(hi_done, 1)

        @block.gpsimd
        def _(pool):
            step = Chain(pool, ident_done)
            step(pool.memset(g.ident[:], 0.0))
            step(pool.affine_select(out=g.ident[:], in_=g.ident[:], compare_op=ALU.not_equal, fill=1.0,
                                    base=0, pattern=[[-1, P]], channel_multiplier=1))
            pool.memset(g.zeros[:], 0.0).then_inc(zero_done, 1)
            pool.memset(g.minus_half[:], -0.5).then_inc(zero_done, 1)
            pool.wait_ge(zero_done, 2)
            pool.wait_ge(var_done, 1)
            pool.tensor_tensor(rstd[:], var_eps[:], g.minus_half[:], ALU.pow).then_inc(rstd_done, 1)

        @block.vector
        def _(dve):
            step = Chain(dve, dve_step)
            dve.wait_ge(loaded["x"], 16)
            layernorm_stats(dve, step, g.x, stats, moments, var_eps).then_inc(var_done, 1)
            for j in range(JOBS):
                if j == WV:
                    dve.wait_ge(rstd_done, 1)
                    layernorm_apply(dve, g.x, moments, rstd, xn).then_inc(xn_done, 1)
                if j == QK:
                    dve.wait_ge(wout_hi, 1)
                    dve.tensor_tensor(wout_s.lo, wout[:], f32(wout_s.hi), ALU.subtract).then_inc(wout_lo, 1)
                ps, to, factor = evacuation(j)
                dve.wait_ge(hi_done, j + 1)
                if factor == 1.0:
                    dve.tensor_tensor(to.lo, ps, f32(to.hi), ALU.subtract).then_inc(lo_done, 1)
                else:
                    dve.scalar_tensor_tensor(out=to.lo, in0=ps, scalar=factor, in1=f32(to.hi),
                                             op0=ALU.mult, op1=ALU.subtract).then_inc(lo_done, 1)

        @block.tensor
        def _(pe):
            pe.wait_ge(ident_done, 2)
            for j in range(JOBS):
                ps = slot(j)
                wait(pe, lo_done, j - 3)
                if j == CTX:
                    pe.wait_ge(loaded["ctx"], 32)
                    for kt in range(KT):
                        rows = P if kt < KT - 1 else KLAST
                        last = pe.transpose(ps[0:C, kt * P:kt * P + rows], ctx_rows[0:rows, kt, :],
                                            g.ident[0:rows, 0:rows])
                elif j in (WQ, WK, WV):
                    pe.wait_ge(loaded[("wq", "wk", "wv")[j - WQ]], 16)
                    w, rows = ((wq, D), (wk, C), (wv, C))[j - WQ]
                    for h in range(H0):
                        last = pe.transpose(ps[:, h * P:h * P + rows], w[:, h * DH0:(h + 1) * DH0],
                                            g.ident[0:rows, 0:rows])
                elif j == QK:
                    pe.wait_ge(lo_done, WK + 1)
                    for h in range(H0):
                        last = matmul3(pe, ps[0:C, h * D:(h + 1) * D], wkT[:, h, :], wqT[:, h, :])
                elif j == VO:
                    pe.wait_ge(lo_done, WV + 1)
                    pe.wait_ge(wout_lo, 1)
                    for h in range(H0):
                        last = matmul3(pe, ps[0:C, h * D:(h + 1) * D], wvT[:, h, :], wout_s[:, h, :])
                elif j == XN:
                    pe.wait_ge(xn_done, 1)
                    for t in range(TT):
                        last = pe.transpose(ps[:, t * P:(t + 1) * P], xn[:, t, :], g.ident[:])
                elif j < V0:
                    pe.wait_ge(lo_done, QK + 1)
                    for b in range(2):
                        n = KEYS // 2
                        last = matmul3(pe, ps[:, b * BANK:b * BANK + n], qk[:, j - K0, :],
                                       g.ctxT[:, b * n:(b + 1) * n])
                else:
                    pe.wait_ge(lo_done, VO + 1)
                    kt = j - V0
                    rows = P if kt < KT - 1 else KLAST
                    for b in range(2):
                        last = matmul3(pe, ps[0:rows, b * BANK:(b + 1) * BANK],
                                       g.ctxT[:, kt * P:kt * P + rows], vo[:, b * BANK:(b + 1) * BANK])
                last.then_inc(pe_done, 1)


def attention0(core, g):
    nc = core.nc
    with ExitStack() as stack:
        c = core.scope(stack)
        queries = [c.split(f"queries{i}", [D, P]) for i in range(2)]
        weights = [c.sb(f"weights{i}", [P, KT * P]) for i in range(4)]
        weightsT = [c.split(f"weights{i}T", [P, KT, 2, P]) for i in range(2)]
        neg_max = c.sb("neg_max0", [P, 2])
        den, rden = c.sb("den0", [P, 4]), c.sb("rden0", [P, 4])
        outT = c.sb("outT", [D, 2 * P])

        queries_ready, pad_done = c.sem("b_queries"), c.sem("b_pad")
        scores_done, max_done, exp_done = c.sem("b_scores"), c.sem("b_max"), c.sem("b_exp")
        recip_done, norm_done = c.sem("b_recip"), c.sem("b_norm")
        turned, hi_done, lo_done = c.sem("b_turned"), c.sem("b_hi"), c.sem("b_lo")
        pv_done, out_done, back_done, attended_done = (c.sem("b_" + n) for n in ("pv", "out", "back", "attended"))

        UNITS = 2 * H0
        TURNS = TT // 2
        CHUNKS = [(0, 3), (3, KT)]
        DRAIN = 6
        half = KEYS // 2

        def scores(u):
            return g.psum[:, 2 * (u % 2):2 * (u % 2) + 2, 0:half]

        def turned_bank(i):
            return g.psum[:, 4 + i, :]

        out_ps = g.psum[:, 6, 0:2 * P]
        back_ps = g.psum[:, 7, 0:2 * D]

        def steps(engine_step, engine):
            for s in range(UNITS):
                engine_step(0, s)
            with engine.Fori(1, TURNS) as turn:
                for s in range(UNITS):
                    engine_step(turn, s)
            for s in range(DRAIN):
                engine_step(TURNS, s)

        def unit(turn, s):
            return turn * UNITS + s

        def exists(turn, u):
            return not isinstance(turn, int) or 0 <= turn * UNITS + u < TURNS * UNITS

        block = stack.enter_context(nc.Block())

        @block.gpsimd
        def _(pool):
            for i in range(4):
                pool.memset(weights[i][:, KEYS:KT * P], 0.0).then_inc(pad_done, 1)

            def step(turn, s):
                if s < 2 and exists(turn, s):
                    wait(pool, scores_done, unit(turn, s - 1))
                    at = bass.ds((turn * 2 + s) * P, P)
                    pool.tensor_copy(queries[s].hi, f32(g.xnT.hi[:, at])).then_inc(queries_ready, 1)
                    pool.tensor_copy(queries[s].lo, f32(g.xnT.lo[:, at])).then_inc(queries_ready, 1)
                if exists(turn, s - 2):
                    u = s - 2
                    w = weights[u % 4][:, 0:KEYS]
                    pool.wait_ge(recip_done, unit(turn, u + 1))
                    pool.tensor_tensor(w, w, rden[:, u % 4:u % 4 + 1].to_broadcast([P, KEYS]),
                                       ALU.mult).then_inc(norm_done, 1)

            steps(step, pool)

        @block.tensor
        def _(pe):
            def values_product(turn, u, a, b):
                h = (u // 2) % H0
                for kt in range(a, b):
                    rows = P if kt < KT - 1 else KLAST
                    last = matmul3(pe, out_ps, g.values0[0:rows, kt, h * D:(h + 1) * D],
                                   weightsT[h % 2][0:rows, kt].view("p t q -> p (t q)"),
                                   start=h == 0 and kt == 0, stop=h == H0 - 1 and kt == KT - 1)
                return last

            def step(turn, s):
                if exists(turn, s):
                    if s < 2:
                        pe.wait_ge(queries_ready, turn * 4 + 2 * s + 2)
                    wait(pe, exp_done, unit(turn, s - 1))
                    for b in range(2):
                        last = matmul3(pe, scores(s)[:, b, :], queries[s % 2],
                                       g.keys0[:, s // 2, b * half:(b + 1) * half])
                    last.then_inc(scores_done, 1)
                if exists(turn, s - 2):
                    u = s - 2
                    pe.wait_ge(norm_done, unit(turn, u + 1))
                    if isinstance(turn, int) and unit(turn, u) < 4:
                        pe.wait_ge(pad_done, 4)
                    for i, (a, b) in enumerate(CHUNKS):
                        wait(pe, lo_done, unit(turn, u - 1) * 2 + i + 1)
                        for kt in range(a, b):
                            last = pe.transpose(turned_bank(i)[:, (kt - a) * P:(kt - a + 1) * P],
                                                weights[u % 4][:, kt * P:(kt + 1) * P], g.ident[:])
                        last.then_inc(turned, 1)
                if s == 4 and exists(turn, s - 5):
                    pe.wait_ge(out_done, turn)
                    for t in range(2):
                        last = pe.transpose(back_ps[:, t * D:(t + 1) * D], outT[:, t * P:(t + 1) * P], g.ident[:])
                    last.then_inc(back_done, 1)
                if s % 2 == 0 and exists(turn, s - 4):
                    pe.wait_ge(lo_done, unit(turn, s - 3) * 2 + 1)
                    if s == 4:
                        wait(pe, out_done, turn)
                    values_product(turn, s - 4, *CHUNKS[0])
                if s % 2 == 1 and exists(turn, s - 5):
                    pe.wait_ge(lo_done, unit(turn, s - 4) * 2 + 2)
                    values_product(turn, s - 5, *CHUNKS[1]).then_inc(pv_done, 1)

            steps(step, pe)

        @block.scalar
        def _(act):
            def step(turn, s):
                if s == 4 and exists(turn, s - 5):
                    act.wait_ge(pv_done, turn * H0)
                    act.copy(outT[:], out_ps).then_inc(out_done, 1)
                if exists(turn, s - 2):
                    u = s - 2
                    if u % 2 == 0:
                        wait(act, pv_done, turn * H0 + u // 2 - 1)
                    for i, (a, b) in enumerate(CHUNKS):
                        act.wait_ge(turned, unit(turn, u) * 2 + i + 1)
                        act.copy(weightsT[(u // 2) % 2].hi[:, a:b, u % 2, :],
                                 turned_bank(i)[:, 0:(b - a) * P].rearrange("p (k q) -> p k q", q=P)).then_inc(hi_done, 1)
                if exists(turn, s):
                    act.wait_ge(max_done, unit(turn, s + 1))
                    wait(act, turned, unit(turn, s - 3) * 2)
                    wait(act, recip_done, unit(turn, s - 3))
                    act.activation(weights[s % 4][:, 0:KEYS].rearrange("p (b n) -> p b n", b=2), scores(s),
                                   ACT.Exp, bias=neg_max[:, s % 2:s % 2 + 1],
                                   accum_out=den[:, s % 4:s % 4 + 1]).then_inc(exp_done, 1)

            steps(step, act)

        @block.vector
        def _(dve):
            def step(turn, s):
                if exists(turn, s):
                    dve.wait_ge(scores_done, unit(turn, s + 1))
                    wait(dve, exp_done, unit(turn, s - 1))
                    dve.tensor_reduce(neg_max[:, s % 2:s % 2 + 1], scores(s), AX.XY, ALU.max,
                                      negate=True).then_inc(max_done, 1)
                if exists(turn, s - 2):
                    u = s - 2
                    for i, (a, b) in enumerate(CHUNKS):
                        dve.wait_ge(hi_done, unit(turn, u) * 2 + i + 1)
                        dve.tensor_tensor(weightsT[(u // 2) % 2].lo[:, a:b, u % 2, :],
                                          turned_bank(i)[:, 0:(b - a) * P].rearrange("p (k q) -> p k q", q=P),
                                          f32(weightsT[(u // 2) % 2].hi[:, a:b, u % 2, :]),
                                          ALU.subtract).then_inc(lo_done, 1)
                if exists(turn, s):
                    wait(dve, norm_done, unit(turn, s - 3))
                    dve.wait_ge(exp_done, unit(turn, s + 1))
                    dve.reciprocal(rden[:, s % 4:s % 4 + 1], den[:, s % 4:s % 4 + 1]).then_inc(recip_done, 1)
                if s == 5 and exists(turn, s - 6):
                    dve.wait_ge(back_done, turn)
                    dve.tensor_tensor(g.attended[:, bass.ds((turn - 1) * 2 * D, 2 * D)].rearrange("p (t d) -> p t d", d=D),
                                      back_ps.rearrange("p (t d) -> p t d", d=D),
                                      g.bias0[:].unsqueeze(1).to_broadcast([P, 2, D]), ALU.add).then_inc(attended_done, 1)

            steps(step, dve)


LAYER0_EXPERTS = ("L0_ffn_W1", "L0_ffn_W3", "L0_ffn_W2")
LAYER1_EXPERTS = ("L1_ffn_w_gate", "L1_ffn_w_up", "L1_ffn_w_down")


def load_expert(sp, io, names, e, raw, loaded):
    for n, name in enumerate(names):
        w = io[name]
        if n < 2:
            src = w.rearrange("e d f -> (e d) f")[bass.ds(e * D, D), :]
            sp.dma_start(raw[n][:], src).then_inc(loaded, 16)
        else:
            src = w.rearrange("e f d -> (e f) d")[bass.ds(e * F, F), :]
            sp.dma_start(raw[n][:].rearrange("p (t d) -> p t d", d=D),
                         src.rearrange("(t p) d -> p t d", p=P)).then_inc(loaded, 16)


def dispatch(core, g, io):
    nc = core.nc
    with ExitStack() as stack:
        c = core.scope(stack)
        wq, wk = c.sb("wq1", [P, H1 * DH1]), c.sb("wk1", [C, H1 * DH1])
        wr = c.sb("wr0", [D, E])
        wqT, wkT = c.split("wq1T", [P, H1 // 2, D]), c.split("wk1T", [P, H1 // 2, C])
        qk = c.split("qk1", [C, 2, 2, H1 // 4, D])
        xn = c.sb("xn0", [P, TT, D])
        xnT = c.sb("xn0T", [D, T])
        stats, moments = c.sb("ln_stats1", [P, TT, 6]), c.sb("ln_moments1", [P, TT, 2])
        var_eps, rstd = c.sb("ln_var1", [P, TT]), c.sb("ln_rstd1", [P, TT])
        earlier = c.sb("earlier", [P, P], BF16)
        ones = c.sb("ones_bf", [P, P], BF16)
        descending = c.sb("descending", [P, TT, E])
        logits = c.sb("logits", [P, TT, E])
        masked = c.sb("masked", [P, TT, E])
        best = c.sb("best", [P, TOPK, TT])
        rank, topped = c.sb("rank", [P, TT, E]), c.sb("topped", [P, TOPK, TT])
        chosen = c.sb("chosen", [P, TOPK, TT, E])
        counted = c.sb("counted", [P, TT, E], BF16)
        places = c.sb("places", [P, TOPK, TT, E])
        pos, over = c.sb("pos", [P, TOPK, TT]), c.sb("over", [P, TOPK, TT])
        base, where_to = c.sb("slot_base", [P, TOPK, TT]), c.sb("where_to", [P, TOPK, TT])
        where_from = c.sb("where_from", [P, TOPK, TT])
        scatter_at = c.sb("scatter_at", [P, TOPK, TT], U32)
        lead, second, total = c.sb("lead", [P, TT]), c.sb("second", [P, TT]), c.sb("total", [P, TT])

        loaded = {n: c.sem("c_ld_" + n) for n in ("wq", "wk", "wr")}
        const_done, var_done, rstd_done, xn_done = (c.sem("c_" + n) for n in ("const", "var", "rstd", "xn"))
        turned, turned_out, logits_done = c.sem("c_turned"), c.sem("c_turnedout"), c.sem("c_logits")
        counted_done, pos_done, lead_done = c.sem("c_counted"), c.sem("c_pos"), c.sem("c_lead")
        second_done, at_done, scattered = c.sem("c_second"), c.sem("c_at"), c.sem("c_scattered")
        pe_done, hi_done, lo_done = c.sem("c_pe"), c.sem("c_hi"), c.sem("c_lo")
        dve_step = c.sem("c_dve")

        WQ, WK, QK = 0, 1, 2
        K1 = 4
        JOBS = K1 + H1
        RING = 3
        half = KEYS // 2

        def slot(j):
            return g.psum[:, 2 * (j % RING):2 * (j % RING) + 2, :]

        def evacuation(j):
            ps = slot(j)
            flat = ps.rearrange("p b n -> p (b n)").rearrange("p (h n) -> p h n", n=P)
            if j == WQ:
                return flat, wqT, 1.0
            if j == WK:
                return flat[:, :, 0:C], wkT, 1.0
            if j < K1:
                return ps[0:C].rearrange("p o (i d) -> p o i d", d=D), qk[:, j - QK], SCALE1
            return ps[:, :, 0:half].rearrange("p n (b k) -> p n b k", k=M), \
                g.keys1[:, :, j - K1, :].view("p (n b) k -> p n b k", n=2), 1.0

        turned_ps = g.psum[:, 6:8, :].rearrange("p b n -> p (b n)")
        logits_ps = g.psum[:, 6, 0:TT * E].rearrange("p (t e) -> p t e", e=E)
        pos_ps = g.psum[:, 7, 0:TT * E].rearrange("p (t e) -> p t e", e=E)

        block = stack.enter_context(nc.Block())

        @block.sync
        def _(sp):
            sp.dma_start(wq[:], io["L1_xattn_Wq"]).then_inc(loaded["wq"], 16)
            sp.dma_start(wk[:], io["L1_xattn_Wk"]).then_inc(loaded["wk"], 16)
            sp.dma_start(wr[:], io["L0_ffn_Wr"]).then_inc(loaded["wr"], 16)
            sp.dma_start(g.wv1[:], io["L1_xattn_Wv"]).then_inc(g.value_weights_loaded, 16)
            sp.dma_start(g.wo1[:], io["L1_xattn_Wo"].rearrange("(t p) d -> p t d", p=P)
                         ).then_inc(g.value_weights_loaded, 16)
            for i in range(2):
                load_expert(sp, io, LAYER0_EXPERTS, i, g.expert_w[i], g.expert_w_loaded[i])

        @block.gpsimd
        def _(pool):
            step = Chain(pool, const_done)
            step(pool.memset(earlier[:], 1.0))
            step(pool.affine_select(out=earlier[:], in_=earlier[:], compare_op=ALU.is_gt, fill=0.0,
                                    base=0, pattern=[[1, P]], channel_multiplier=-1))
            step(pool.memset(ones[:], 1.0))
            step(pool.iota(descending[:], pattern=[[0, TT], [-1, E]], base=E, channel_multiplier=0,
                           allow_small_or_imprecise_dtypes=True))
            pool.wait_ge(var_done, 1)
            pool.tensor_tensor(rstd[:], var_eps[:], g.minus_half[:], ALU.pow).then_inc(rstd_done, 1)
            pool.wait_ge(g.expert_in_zeroed, 16 * E)
            pool.wait_ge(at_done, 1)
            for t in range(TT):
                for k in range(TOPK):
                    pool.indirect_dma_start(
                        out=g.expert_in, out_offset=bass.IndirectOffsetOnAxis(ap=scatter_at[:, k, t:t + 1], axis=0),
                        in_=xn[:, t, :], in_offset=None, bounds_check=SLOTS - 1,
                        oob_is_err=False).then_inc(scattered, 16)
            pool.wait_ge(scattered, 16 * TT * TOPK)

        @block.scalar
        def _(act):
            def evacuate(j):
                act.wait_ge(pe_done, j + 1)
                ps, to, factor = evacuation(j)
                act.activation(to.hi, ps, ACT.Copy, scale=factor).then_inc(hi_done, 1)

            evacuate(WQ)
            evacuate(WK)
            act.wait_ge(turned, 1)
            act.copy(xnT[:], turned_ps).then_inc(turned_out, 1)
            evacuate(QK)
            act.wait_ge(lead_done, 1)
            act.activation(second[:], lead[:], ACT.Exp).then_inc(second_done, 1)
            for j in range(QK + 1, JOBS):
                evacuate(j)

        @block.vector
        def _(dve):
            step = Chain(dve, dve_step)

            def evacuate(j):
                ps, to, factor = evacuation(j)
                dve.wait_ge(hi_done, j + 1)
                if factor == 1.0:
                    dve.tensor_tensor(to.lo, ps, f32(to.hi), ALU.subtract).then_inc(lo_done, 1)
                elif j < K1:
                    for o in range(2):
                        last = dve.scalar_tensor_tensor(out=to.lo[:, o], in0=ps[:, o], scalar=factor,
                                                        in1=f32(to.hi[:, o]), op0=ALU.mult, op1=ALU.subtract)
                    last.then_inc(lo_done, 1)

            x2d = g.x[:].rearrange("p t d -> p (t d)")
            step(dve.scalar_tensor_tensor(out=x2d, in0=g.attended[:], scalar=g.gates[:, 0:1], in1=x2d,
                                          op0=ALU.mult, op1=ALU.add))
            layernorm_stats(dve, step, g.x, stats, moments, var_eps).then_inc(var_done, 1)
            evacuate(WQ)
            evacuate(WK)
            dve.wait_ge(rstd_done, 1)
            layernorm_apply(dve, g.x, moments, rstd, xn).then_inc(xn_done, 1)
            dve.wait_ge(logits_done, 1)
            step(dve.tensor_scalar(logits[:], logits_ps, 1e4, -1e4, ALU.min, ALU.max))
            dve.wait_ge(const_done, 4)
            for k in range(TOPK):
                scores = logits if k == 0 else masked
                step(dve.tensor_reduce(best[:, k, :], scores[:], AX.X, ALU.max))
                step(dve.tensor_tensor(rank[:], scores[:], best[:, k, :].unsqueeze(2).to_broadcast([P, TT, E]),
                                       ALU.is_equal))
                step(dve.tensor_tensor(rank[:], rank[:], descending[:], ALU.mult))
                step(dve.tensor_reduce(topped[:, k, :], rank[:], AX.X, ALU.max))
                step(dve.tensor_tensor(chosen[:, k], rank[:],
                                       topped[:, k, :].unsqueeze(2).to_broadcast([P, TT, E]), ALU.is_equal))
                if k == 0:
                    step(dve.scalar_tensor_tensor(
                        out=masked[:].rearrange("p t e -> p (t e)"),
                        in0=chosen[:, 0].rearrange("p t e -> p (t e)"), scalar=-4e4,
                        in1=logits[:].rearrange("p t e -> p (t e)"), op0=ALU.mult, op1=ALU.add))
            dve.tensor_tensor(counted[:], chosen[:, 0], chosen[:, 1], ALU.add).then_inc(counted_done, 1)
            dve.tensor_tensor(lead[:], best[:, 1, :], best[:, 0, :], ALU.subtract).then_inc(lead_done, 1)
            step(dve.tensor_scalar(base[:], topped[:], float(-CAP), float(CAP * E), ALU.mult, ALU.add))
            evacuate(QK)
            dve.wait_ge(pos_done, 1)
            for k in range(TOPK):
                last = dve.tensor_tensor(places[:, k], pos_ps, chosen[:, k], ALU.mult)
            step(last)
            step(dve.tensor_reduce(pos[:], places[:], AX.X, ALU.add))
            step(dve.tensor_scalar(over[:], pos[:], float(CAP), None, ALU.is_ge))
            step(dve.tensor_tensor(where_to[:], pos[:], base[:], ALU.add))
            over2, to2 = (v[:].rearrange("p k t -> p (k t)") for v in (over, where_to))
            step(dve.scalar_tensor_tensor(out=to2, in0=over2, scalar=float(1 << 16), in1=to2,
                                          op0=ALU.mult, op1=ALU.add))
            dve.tensor_copy(scatter_at[:], where_to[:]).then_inc(at_done, 1)
            step(dve.tensor_scalar(where_from[:], pos[:], float(CAP - 1), None, ALU.min))
            step(dve.tensor_tensor(where_from[:], where_from[:], base[:], ALU.add))
            step(dve.tensor_copy(g.gather_at[:], where_from[:]))
            dve.wait_ge(second_done, 1)
            step(dve.tensor_scalar(total[:], second[:], 1.0, 1e-12, ALU.add, ALU.add))
            step(dve.reciprocal(g.token_weights[:, 0, :], total[:]))
            step(dve.tensor_tensor(g.token_weights[:, 1, :], second[:], g.token_weights[:, 0, :], ALU.mult))
            step(dve.tensor_scalar(over[:], over[:], -1.0, 1.0, ALU.mult, ALU.add))
            step(dve.tensor_tensor(g.token_weights[:], g.token_weights[:], over[:], ALU.mult))
            step(dve.tensor_scalar(g.token_weights[:], g.token_weights[:], g.gates[:, 2:3], None, ALU.mult))
            for j in range(QK + 1, JOBS):
                evacuate(j)

        @block.tensor
        def _(pe):
            def job(j):
                ps = slot(j)
                wait(pe, lo_done, j - RING + 1)
                if j in (WQ, WK):
                    pe.wait_ge(loaded[("wq", "wk")[j]], 16)
                    w, rows = ((wq, D), (wk, C))[j]
                    flat = ps.rearrange("p b n -> p (b n)")
                    for i in range(H1 // 2):
                        last = pe.transpose(flat[:, i * P:i * P + rows], w[:, i * P:(i + 1) * P],
                                            g.ident[0:rows, 0:rows])
                elif j < K1:
                    pe.wait_ge(lo_done, WK + 1)
                    for i in range(H1 // 4):
                        for odd in range(2):
                            at, pair = slice(odd * DH1, (odd + 1) * DH1), (j - QK) * (H1 // 4) + i
                            last = matmul3(pe, ps[0:C, odd, i * D:(i + 1) * D], wkT[at, pair, :], wqT[at, pair, :])
                else:
                    h = j - K1
                    pe.wait_ge(lo_done, QK + 1 + h // (H1 // 2))
                    for b in range(2):
                        last = matmul3(pe, ps[:, b, 0:half], qk[:, h // 8, h % 2, h % 8 // 2, :],
                                       g.ctxT[:, b * half:(b + 1) * half])
                last.then_inc(pe_done, 1)

            job(WQ)
            job(WK)
            pe.wait_ge(xn_done, 1)
            for t in range(TT):
                last = pe.transpose(turned_ps[:, t * P:(t + 1) * P], xn[:, t, :], g.ident[:])
            last.then_inc(turned, 1)
            pe.wait_ge(turned_out, 1)
            pe.wait_ge(loaded["wr"], 16)
            for t in range(TT):
                last = pe.matmul(logits_ps[:, t, :], xnT[:, t * P:(t + 1) * P], wr[:], start=True, stop=True)
            last.then_inc(logits_done, 1)
            job(QK)
            pe.wait_ge(counted_done, 1)
            last = pe.matmul(pos_ps, earlier[:], counted[:], start=True, stop=False)
            for t in range(TT - 1):
                last = pe.matmul(pos_ps[:, t + 1:TT, :], ones[:],
                                 counted[:, t, :].unsqueeze(1).to_broadcast([P, TT - 1 - t, E]),
                                 start=False, stop=t == TT - 2)
            last.then_inc(pos_done, 1)
            for j in range(QK + 1, JOBS):
                job(j)


def experts0(core, g, io):
    nc = core.nc
    with ExitStack() as stack:
        c = core.scope(stack)
        TILES = [(0, 112), (112, 216), (216, CAP)]
        NT = len(TILES)
        CREDIT = 16
        parts = [[c.split(f"ews{i}_{n}", [P, F]) for n in range(3)] for i in range(2)]
        rows = [c.sb(f"erows{i}", [P, NT, D]) for i in range(2)]
        tokensT = [c.split(f"etokT{i}", [D, CAP]) for i in range(2)]
        silu = [c.sb(f"esilu{i}", [P, CAP]) for i in range(2)]
        hidden = c.sb("ehidden", [P, CAP])
        hid = [c.split(f"ehid{i}", [P, FT, CAP]) for i in range(2)]
        down_out = c.sb("edownT", [D, CAP])
        result = [c.sb(f"eresult{i}", [P, NT, D]) for i in range(2)]

        raw, w_loaded = g.expert_w, g.expert_w_loaded
        r_loaded = [c.sem(f"d_rld{i}") for i in range(2)]
        up_w_hi, up_w_lo, down_w_hi, down_w_lo = (c.sem("d_" + n) for n in ("uwhi", "uwlo", "dwhi", "dwlo"))
        stored = [c.sem(f"d_stored{i}") for i in range(2)]
        turned, turned_hi, turned_lo = c.sem("d_turned"), c.sem("d_turnedhi"), c.sem("d_turnedlo")
        up_done, silu_done, mult_done = c.sem("d_up"), c.sem("d_silu"), c.sem("d_mult")
        hid_hi, hid_lo = c.sem("d_hidhi"), c.sem("d_hidlo")
        down_done, result_done = c.sem("d_down"), c.sem("d_result")
        down_copied, back_done = c.sem("d_downout"), c.sem("d_back")

        def turns(step, engine):
            for i in range(2):
                step(0, i)
            with engine.Fori(1, E // 2) as turn:
                for i in range(2):
                    step(turn, i)

        def move_slots(queue, dram, e, tile, sem, to_dram):
            first, like = TILES[0][1], TILES[1][1] - TILES[1][0]
            for src, dst in ((dram[bass.ds(e * CAP, first), :], tile[0:first, 0, :]),
                             (dram[bass.ds(e * CAP + first, 2 * like), :].rearrange("(s p) d -> p s d", s=2),
                              tile[0:like, 1:3, :])):
                if to_dram:
                    src, dst = dst, src
                queue.dma_start(dst, src).then_inc(sem, 16)

        def up_bank(n, which):
            return g.psum[:, 2 * (n % 2) + which, 0:CAP]

        turned_ps = g.psum[:, 4, 0:CAP]

        down_ps = g.psum[:, 5, 0:CAP]
        back_ps = g.psum[:, 6, 0:NT * D].rearrange("p (s d) -> p s d", d=D)

        def before(turn, i):
            return isinstance(turn, int) and turn == 0 and i < 0

        block = stack.enter_context(nc.Block())

        @block.sync
        def _(sp):
            def step(turn, i):
                e = turn * 2 + i
                wait(sp, up_w_lo, e - 1)
                wait(sp, down_w_lo, e - 1)
                if not (isinstance(turn, int) and turn == 0):
                    load_expert(sp, io, LAYER0_EXPERTS, e, raw[i], w_loaded[i])
                wait(sp, turned, e - 1)
                move_slots(sp, g.expert_in, e, rows[i], r_loaded[i], False)

            turns(step, sp)

        @block.gpsimd
        def _(pool):
            def low(i, n):
                return pool.tensor_tensor(parts[i][n].lo, raw[i][n][:], f32(parts[i][n].hi), ALU.subtract)

            def step(turn, i):
                e = turn * 2 + i
                wait(pool, up_done, (e - 1) * FT)
                for n in range(2):
                    pool.wait_ge(up_w_hi, e * 2 + n + 1)
                    last = low(i, n)
                last.then_inc(up_w_lo, 1)
                wait(pool, down_done, e - 1)
                pool.wait_ge(down_w_hi, e + 1)
                low(i, 2).then_inc(down_w_lo, 1)

            turns(step, pool)

        @block.scalar
        def _(act):
            def split_weight(turn, i, n):
                e = turn * 2 + i
                if n == 0:
                    act.wait_ge(w_loaded[i % 2], (turn + (i // 2)) * 48 + 48)
                    wait(act, up_done, (e - 1) * FT)
                if n == 2:
                    wait(act, down_done, e - 1)
                act.copy(parts[i % 2][n].hi, raw[i % 2][n][:]).then_inc(down_w_hi if n == 2 else up_w_hi, 1)

            def tokens_hi(turn, i):
                act.wait_ge(turned, turn * 2 + i + 1)
                act.copy(tokensT[i % 2].hi, turned_ps).then_inc(turned_hi, 1)

            def store(turn, i):
                act.wait_ge(result_done, turn * 2 + i + 2)
                move_slots(act, g.expert_out, turn * 2 + i, result[i % 2], stored[i % 2], True)

            def copy_down(turn, i):
                if before(turn, i):
                    return
                e = turn * 2 + i
                act.wait_ge(down_done, e + 1)
                wait(act, back_done, e)
                act.copy(down_out[:], down_ps).then_inc(down_copied, 1)

            def step(turn, i, ahead=True):
                e = turn * 2 + i
                for f in range(FT):
                    n = e * FT + f
                    act.wait_ge(up_done, n + 1)
                    wait(act, mult_done, n - 1)
                    act.activation(silu[f % 2][:], up_bank(f, 0), ACT.Silu).then_inc(silu_done, 1)
                    if f == 2:
                        copy_down(turn, i - 1)
                    if ahead and f < 3:
                        split_weight(turn, i + 1, f)
                    if f == 3 and not (isinstance(turn, int) and turn == 0):
                        store(turn, i - 2)
                    if ahead and f == 2:
                        tokens_hi(turn, i + 1)

            for n in range(3):
                split_weight(0, 0, n)
            tokens_hi(0, 0)
            for i in range(2):
                step(0, i)
            with act.Fori(1, E // 2 - 1) as turn:
                for i in range(2):
                    step(turn, i)
            step(E // 2 - 1, 0)
            step(E // 2 - 1, 1, ahead=False)
            copy_down(E // 2, -1)
            for i in range(2):
                store(E // 2, i - 2)
            for i in range(2):
                act.wait_ge(stored[i], CREDIT + 32 * (E // 2))

        @block.vector
        def _(dve):
            def tokens_lo(turn, i):
                dve.wait_ge(turned_hi, turn * 2 + i + 1)
                dve.tensor_tensor(tokensT[i % 2].lo, turned_ps, f32(tokensT[i % 2].hi),
                                  ALU.subtract).then_inc(turned_lo, 1)

            def copy_result(turn, i):
                if before(turn, i):
                    return
                e = turn * 2 + i
                dve.wait_ge(back_done, e + 1)
                wait(dve, stored[i % 2], CREDIT + (turn + (i // 2)) * 32)
                for s, (a, b) in enumerate(TILES):
                    last = dve.tensor_copy(result[i % 2][0:b - a, s, :], back_ps[0:b - a, s, :])
                last.then_inc(result_done, 1)

            def step(turn, i, ahead=True):
                e = turn * 2 + i
                wait(dve, down_done, e - 1)
                for f in range(FT):
                    n = e * FT + f
                    dve.wait_ge(silu_done, n + 1)
                    wait(dve, hid_lo, n)
                    dve.tensor_tensor(hidden[:], silu[f % 2][:], up_bank(f, 1), ALU.mult).then_inc(mult_done, 1)
                    dve.wait_ge(mult_done, n + 1)
                    dve.tensor_copy(hid[i].hi[:, f, :], hidden[:]).then_inc(hid_hi, 1)
                    dve.wait_ge(hid_hi, n + 1)
                    dve.tensor_tensor(hid[i].lo[:, f, :], hidden[:], f32(hid[i].hi[:, f, :]),
                                      ALU.subtract).then_inc(hid_lo, 1)
                    if f == 2 and ahead:
                        tokens_lo(turn, i + 1)
                    if f == 0:
                        copy_result(turn, i - 2) if not isinstance(turn, int) or turn * 2 + i >= 2 else None

            for i in range(2):
                dve.sem_inc(stored[i], CREDIT)
            tokens_lo(0, 0)
            for i in range(2):
                step(0, i)
            with dve.Fori(1, E // 2 - 1) as turn:
                for i in range(2):
                    step(turn, i)
            step(E // 2 - 1, 0)
            step(E // 2 - 1, 1, ahead=False)
            copy_result(E // 2, -2)
            copy_result(E // 2, -1)

        @block.tensor
        def _(pe):
            def transposes(turn, i):
                e = turn * 2 + i
                pe.wait_ge(r_loaded[i % 2], (turn + i // 2) * 32 + 32)
                wait(pe, turned_lo, e)
                wait(pe, up_done, (e - 1) * FT)
                for s, (a, b) in enumerate(TILES):
                    last = pe.transpose(turned_ps[:, a:b], rows[i % 2][0:b - a, s, :], g.ident[0:b - a, 0:b - a])
                last.then_inc(turned, 1)

            def down(turn, i):
                if before(turn, i):
                    return
                e = turn * 2 + i
                pe.wait_ge(hid_lo, e * FT + FT)
                pe.wait_ge(down_w_lo, e + 1)
                wait(pe, down_copied, e)
                for f in range(FT):
                    last = matmul3(pe, down_ps, parts[i % 2][2][:, f * D:(f + 1) * D], hid[i % 2][:, f, :],
                                   start=f == 0, stop=f == FT - 1)
                last.then_inc(down_done, 1)

            def back(turn, i):
                if before(turn, i):
                    return
                e = turn * 2 + i
                pe.wait_ge(down_copied, e + 1)
                wait(pe, result_done, e + 1)
                for s, (a, b) in enumerate(TILES):
                    last = pe.transpose(back_ps[0:b - a, s, :], down_out[:, a:b], g.ident[:])
                last.then_inc(back_done, 1)

            def step(turn, i, ahead=True):
                e = turn * 2 + i
                pe.wait_ge(up_w_lo, e + 1)
                pe.wait_ge(turned_lo, e + 1)
                for f in range(FT):
                    n = e * FT + f
                    wait(pe, mult_done, n - 1)
                    for which in range(2):
                        last = matmul3(pe, up_bank(f, which), parts[i][which][:, f * P:(f + 1) * P], tokensT[i])
                    last.then_inc(up_done, 1)
                    if f == 1:
                        down(turn, i - 1)
                        if ahead:
                            transposes(turn, i + 1)
                    if f == 3:
                        back(turn, i - 1)

            pe.sem_inc(result_done, 1)
            transposes(0, 0)
            for i in range(2):
                step(0, i)
            with pe.Fori(1, E // 2 - 1) as turn:
                for i in range(2):
                    step(turn, i)
            step(E // 2 - 1, 0)
            step(E // 2 - 1, 1, ahead=False)
            down(E // 2, -1)
            back(E // 2, -1)


def combine(core, g):
    nc = core.nc
    with ExitStack() as stack:
        c = core.scope(stack)
        gathered = c.sb("gathered", [P, TT, TOPK, D])
        wvT, wo = c.split("wv1T", [P, H1 // 2, C]), c.split("wo1s", [P, H1 // 2, D])
        vo = c.split("vo1", [C, H1, D])
        staged = [c.sb(f"vstage{i}", [M, H1 // 2, D]) for i in range(4)]
        got, sum_step = c.sem("v_gathered"), c.sem("v_sum")
        wo_hi, wo_lo = c.sem("v_wohi"), c.sem("v_wolo")
        pe_done, hi_done, lo_done = c.sem("v_pe"), c.sem("v_hi"), c.sem("v_lo")
        copied = [c.sem(f"v_copied{i}") for i in range(4)]
        stored = [c.sem(f"v_stored{i}") for i in range(4)]
        value_done = c.sem("v_values")

        WV, VO, V0 = 0, 1, 3
        JOBS = V0 + 2 * B
        RING = 4

        def slot(j):
            return g.psum[:, 2 * (j % RING):2 * (j % RING) + 2, :].rearrange("p b n -> p (b n)")

        def evacuation(j):
            if j == WV:
                return slot(j).rearrange("p (h n) -> p h n", n=P)[:, :, 0:C], wvT
            i = j - VO
            return slot(j)[0:C].rearrange("p (o h d) -> p o h d", o=2, d=D), \
                vo.view("p (o h) d -> p o h d", o=2)[:, :, 4 * i:4 * i + 4, :]

        block = stack.enter_context(nc.Block())

        @block.gpsimd
        def _(pool):
            for t in range(TT):
                for k in range(TOPK):
                    pool.indirect_dma_start(
                        out=gathered[:, t, k, :], out_offset=None, in_=g.expert_out,
                        in_offset=bass.IndirectOffsetOnAxis(ap=g.gather_at[:, k, t:t + 1], axis=0)
                    ).then_inc(got, 16)

        @block.sync
        def _(sp):
            for n in range(2 * B):
                b, odd = n // 2, n % 2
                sp.wait_ge(copied[n % 4], n // 4 + 1)
                sp.dma_start(g.values1[b].rearrange("(h o k) d -> o k h d", o=2, k=M)[odd],
                             staged[n % 4][:]).then_inc(stored[n % 4], 16)
            for i in range(4):
                sp.wait_ge(stored[i], 16 * 2 * B // 4)

        def value_copy(eng, copy, n):
            eng.wait_ge(pe_done, V0 + n + 1)
            wait(eng, stored[n % 4], 16 * (n // 4))
            copy(staged[n % 4][:], slot(V0 + n)[0:M].rearrange("p (h d) -> p h d", d=D)).then_inc(copied[n % 4], 1)

        @block.scalar
        def _(act):
            act.wait_ge(g.value_weights_loaded, 32)
            act.copy(wo.hi, g.wo1[:]).then_inc(wo_hi, 1)
            for j in range(V0):
                act.wait_ge(pe_done, j + 1)
                ps, to = evacuation(j)
                act.copy(to.hi, ps).then_inc(hi_done, 1)
            for n in range(0, 2 * B, 2):
                value_copy(act, act.copy, n)

        @block.vector
        def _(dve):
            dve.wait_ge(wo_hi, 1)
            dve.tensor_tensor(wo.lo, g.wo1[:], f32(wo.hi), ALU.subtract).then_inc(wo_lo, 1)
            for j in range(V0):
                ps, to = evacuation(j)
                dve.wait_ge(hi_done, j + 1)
                dve.tensor_tensor(to.lo, ps, f32(to.hi), ALU.subtract).then_inc(lo_done, 1)
            for n in range(1, 2 * B, 2):
                value_copy(dve, dve.tensor_copy, n)
            chain = Chain(dve, sum_step)
            dve.wait_ge(got, 16 * TOPK * TT)
            for k in range(TOPK):
                for t in range(TT):
                    last = dve.scalar_tensor_tensor(out=g.x[:, t, :], in0=gathered[:, t, k, :],
                                                    scalar=g.token_weights[:, k, t:t + 1], in1=g.x[:, t, :],
                                                    op0=ALU.mult, op1=ALU.add)
                chain(last)

        @block.tensor
        def _(pe):
            pe.wait_ge(g.value_weights_loaded, 32)
            for j in range(JOBS):
                ps = slot(j)
                if j == VO or j == V0:
                    pe.wait_ge(lo_done, j)
                    pe.wait_ge(wo_lo, 1)
                if j >= V0 + RING:
                    n = j - V0 - RING
                    pe.wait_ge(copied[n % 4], n // 4 + 1)
                if j == WV:
                    for i in range(H1 // 2):
                        last = pe.transpose(ps[:, i * P:i * P + C], g.wv1[:, i * P:(i + 1) * P], g.ident[0:C, 0:C])
                elif j < V0:
                    for i in range(4):
                        for odd in range(2):
                            at, pair = slice(odd * DH1, (odd + 1) * DH1), 4 * (j - VO) + i
                            last = matmul3(pe, ps[0:C, odd * BANK + i * D:odd * BANK + (i + 1) * D],
                                           wvT[at, pair, :], wo[at, pair, :])
                else:
                    b, odd = (j - V0) // 2, (j - V0) % 2
                    for i in range(2):
                        first = odd * (H1 // 2) + 4 * i
                        last = matmul3(pe, ps[0:M, i * BANK:(i + 1) * BANK], g.ctxT[:, b * M:(b + 1) * M],
                                       vo[:, first:first + 4, :].view("p h d -> p (h d)"))
                last.then_inc(pe_done, 1)


def attention1(core, g, io):
    nc = core.nc
    with ExitStack() as stack:
        c = core.scope(stack)
        N1 = H1 * M
        NT = -(-N1 // P)
        LAST = N1 - (NT - 1) * P
        CHUNKS = [(0, 4), (4, 8), (8, NT)]
        xnT = c.split("xn1T", [D, T])
        raw_values = [c.sb(f"vraw{i}", [P, NT, D]) for i in range(2)]
        values_loaded = [c.sem(f"e_vld{i}") for i in range(2)]
        pad_done = c.sem("e_pad")

        def load_values(sp, b, i):
            rows = g.values1.rearrange("b n d -> (b n) d")[bass.ds(b * N1, N1), :]
            sp.dma_start(raw_values[i][:, 0:NT - 1, :],
                         rows[0:(NT - 1) * P, :].rearrange("(t p) d -> p t d", p=P)).then_inc(values_loaded[i], 16)
            sp.dma_start(raw_values[i][0:LAST, NT - 1, :], rows[(NT - 1) * P:N1, :]).then_inc(values_loaded[i], 16)

        with ExitStack() as head_stack:
            h = core.scope(head_stack)
            xn = h.sb("xn1", [P, TT, D])
            stats, moments = h.sb("ln_stats2", [P, TT, 6]), h.sb("ln_moments2", [P, TT, 2])
            var_eps, rstd = h.sb("ln_var2", [P, TT]), h.sb("ln_rstd2", [P, TT])
            gated_bias = h.sb("gated_bias", [P, D])
            var_done, rstd_done = h.sem("e_var"), h.sem("e_rstd")
            xn_done, turned, hi_done, dve_step = h.sem("e_xn"), h.sem("e_turned0"), h.sem("e_hi0"), h.sem("e_dve0")
            turned_ps = g.psum[:, 0:2, :].rearrange("p b n -> p (b n)")
            block = head_stack.enter_context(nc.Block())

            @block.sync
            def _(sp):
                sp.wait_ge(pad_done, 2)
                for i in range(2):
                    load_values(sp, i, i)
                for i in range(2):
                    load_expert(sp, io, LAYER1_EXPERTS, i, g.expert_w[i], g.expert1_w_loaded[i])

            @block.gpsimd
            def _(pool):
                for i in range(2):
                    pool.memset(raw_values[i][:, NT - 1, :], 0.0).then_inc(pad_done, 1)
                pool.wait_ge(var_done, 1)
                pool.tensor_tensor(rstd[:], var_eps[:], g.minus_half[:], ALU.pow).then_inc(rstd_done, 1)

            @block.scalar
            def _(act):
                act.wait_ge(turned, 1)
                act.copy(xnT.hi, turned_ps).then_inc(hi_done, 1)

            @block.vector
            def _(dve):
                step = Chain(dve, dve_step)
                layernorm_stats(dve, step, g.x, stats, moments, var_eps).then_inc(var_done, 1)
                step(dve.tensor_scalar(gated_bias[:], g.bias1[:], g.gates[:, 1:2], None, ALU.mult))
                dve.wait_ge(rstd_done, 1)
                last = layernorm_apply(dve, g.x, moments, rstd, xn)
                last.then_inc(xn_done, 1)
                dve.wait_ge(xn_done, 1)
                dve.tensor_tensor(g.x[:], g.x[:], gated_bias[:].unsqueeze(1).to_broadcast([P, TT, D]), ALU.add)
                dve.wait_ge(hi_done, 1)
                dve.tensor_tensor(xnT.lo, turned_ps, f32(xnT.hi), ALU.subtract)

            @block.tensor
            def _(pe):
                pe.wait_ge(xn_done, 1)
                for t in range(TT):
                    last = pe.transpose(turned_ps[:, t * P:(t + 1) * P], xn[:, t, :], g.ident[:])
                last.then_inc(turned, 1)

        queries = [c.split(f"queries1_{i}", [D, P]) for i in range(2)]
        values = [c.split(f"values1_{i}", [P, NT, D]) for i in range(2)]
        maximum = c.sb("max1", [P, H1])
        den, rden = c.sb("den1", [P, H1]), c.sb("rden1", [P, H1])
        weights = [c.sb(f"weights1_{i}", [P, NT * P]) for i in range(2)]
        by_head = [w[:, 0:N1].rearrange("p (h k) -> p h k", k=M) for w in weights]
        weightsT = c.split("turned1", [P, NT * P])

        queries_ready, v_hi, v_lo = c.sem("e_q"), c.sem("e_vhi"), c.sem("e_vlo")
        scores_done, max_done, sub_done, exp_done = (c.sem("e_" + n) for n in ("scores", "max", "sub", "exp"))
        den_done, rden_done, norm_done = c.sem("e_den"), c.sem("e_rden"), c.sem("e_norm")
        turned, hi_done, lo_done = c.sem("e_turned"), c.sem("e_hi"), c.sem("e_lo")
        pv_done, x_done = c.sem("e_pv"), c.sem("e_x")

        GROUPS = [(0, 0, 6), (1, 6, 12), (2, 12, 16)]
        NC = len(CHUNKS)

        def scores_views():
            yield g.psum[:, 0:2, 0:6 * M].rearrange("p b (h k) -> p b h k", k=M), slice(0, 12)
            yield g.psum[:, 2:3, 0:4 * M].rearrange("p b (h k) -> p b h k", k=M), slice(12, 16)

        def chunk(p):
            a, z = CHUNKS[p]
            return g.psum[:, 3 + p, 0:(z - a) * P]

        def output(i):
            return g.psum[:, 6 + i, 0:D]

        def turns(step, engine):
            for i in range(2):
                step(0, i, True, False)
            with engine.Fori(1, B // 2) as turn:
                for i in range(2):
                    step(turn, i, True, True)
            for i in range(2):
                step(B // 2, i, False, True)

        block = stack.enter_context(nc.Block())

        @block.sync
        def _(sp):
            def step(turn, i, new, old):
                if new and old:
                    b = turn * 2 + i
                    sp.wait_ge(v_lo, b - 1)
                    load_values(sp, b, i)

            turns(step, sp)

        @block.gpsimd
        def _(pool):
            for i in range(2):
                pool.memset(weights[i][:, N1:NT * P], 0.0).then_inc(pad_done, 1)

            def step(turn, i, new, old):
                if not new:
                    return
                b = turn * 2 + i
                pool.wait_ge(v_hi, b + 1)
                pool.tensor_tensor(values[i].lo, raw_values[i][:], f32(values[i].hi), ALU.subtract).then_inc(v_lo, 1)
                pool.wait_ge(rden_done, b + 1)
                pool.tensor_tensor(by_head[i], by_head[i], rden[:].unsqueeze(2).to_broadcast([P, H1, M]),
                                   ALU.mult).then_inc(norm_done, 1)

            turns(step, pool)

        @block.scalar
        def _(act):
            def step(turn, i, new, old):
                b = turn * 2 + i
                if old:
                    wait(act, pv_done, b - 1)
                    for p, (a, z) in enumerate(CHUNKS):
                        act.wait_ge(turned, (b - 2) * NC + p + 1)
                        act.copy(weightsT.hi[:, a * P:z * P], chunk(p)).then_inc(hi_done, 1)
                if new:
                    act.wait_ge(sub_done, b + 1)
                    act.activation(by_head[i], by_head[i], ACT.Exp).then_inc(exp_done, 1)
                    act.wait_ge(values_loaded[i], turn * 32 + 32)
                    if old:
                        act.wait_ge(pv_done, b)
                    act.copy(values[i].hi, raw_values[i][:]).then_inc(v_hi, 1)

            act.sem_inc(pv_done, 1)
            turns(step, act)

        @block.vector
        def _(dve):
            def normalise(b, i):
                dve.wait_ge(exp_done, b + 1)
                dve.tensor_reduce(den[:], by_head[i % 2], AX.X, ALU.add).then_inc(den_done, 1)
                dve.wait_ge(den_done, b + 1)
                wait(dve, norm_done, b)
                dve.reciprocal(rden[:], den[:]).then_inc(rden_done, 1)

            def step(turn, i, new, old):
                b = turn * 2 + i
                if new:
                    wait(dve, scores_done, b - 1)
                    at = bass.ds(b * P, P)
                    dve.tensor_copy(queries[i].hi, f32(xnT.hi[:, at])).then_inc(queries_ready, 1)
                    dve.tensor_copy(queries[i].lo, f32(xnT.lo[:, at])).then_inc(queries_ready, 1)
                if old:
                    for p, (a, z) in enumerate(CHUNKS):
                        dve.wait_ge(hi_done, (b - 2) * NC + p + 1)
                        dve.tensor_tensor(weightsT.lo[:, a * P:z * P], chunk(p), f32(weightsT.hi[:, a * P:z * P]),
                                          ALU.subtract).then_inc(lo_done, 1)
                if not (isinstance(turn, int) and b == 0) and not (old and not new and i == 1):
                    normalise(b - 1, i - 1)
                if new:
                    dve.wait_ge(scores_done, b + 1)
                    wait(dve, sub_done, b)
                    for ps, hs in scores_views():
                        last = dve.tensor_reduce(maximum[:, hs].rearrange("p (b h) -> p b h", b=ps.shape[1]),
                                                 ps, AX.X, ALU.max)
                    last.then_inc(max_done, 1)
                    dve.wait_ge(max_done, b + 1)
                    wait(dve, turned, (b - 1) * NC)
                    for ps, hs in scores_views():
                        nb = ps.shape[1]
                        last = dve.tensor_tensor(
                            by_head[i][:, hs, :].rearrange("p (b h) k -> p b h k", b=nb), ps,
                            maximum[:, hs].rearrange("p (b h) -> p b h", b=nb).unsqueeze(3)
                            .to_broadcast([P, nb, ps.shape[2], M]), ALU.subtract)
                    last.then_inc(sub_done, 1)
                if old:
                    dve.wait_ge(pv_done, b)
                    rows = g.x[:, bass.ds(b - 2, 1), :].rearrange("p o d -> p (o d)")
                    dve.scalar_tensor_tensor(out=rows, in0=output(i), scalar=g.gates[:, 1:2], in1=rows,
                                             op0=ALU.mult, op1=ALU.add).then_inc(x_done, 1)

            turns(step, dve)

        @block.tensor
        def _(pe):
            def step(turn, i, new, old):
                b = turn * 2 + i
                if old:
                    pe.wait_ge(norm_done, b - 1)
                    for p, (a, z) in enumerate(CHUNKS):
                        for t in range(a, z):
                            last = pe.transpose(chunk(p)[:, (t - a) * P:(t - a + 1) * P],
                                                weights[i][:, t * P:(t + 1) * P], g.ident[:])
                        last.then_inc(turned, 1)
                if new:
                    pe.wait_ge(queries_ready, b * 2 + 2)
                    wait(pe, sub_done, b)
                    for bank, a, z in GROUPS:
                        last = matmul3(pe, g.psum[:, bank, 0:(z - a) * M], queries[i],
                                       g.keys1[:, bass.ds(b, 1), a:z, :].view("p o h k -> p (o h k)"))
                    last.then_inc(scores_done, 1)
                if old:
                    pe.wait_ge(v_lo, b - 1)
                    wait(pe, x_done, b - 1)
                    for p, (a, z) in enumerate(CHUNKS):
                        pe.wait_ge(lo_done, (b - 2) * NC + p + 1)
                        for t in range(a, z):
                            rows = P if t < NT - 1 else LAST
                            last = matmul3(pe, output(i), weightsT[0:rows, t * P:(t + 1) * P],
                                           values[i][0:rows, t, :], start=t == 0, stop=t == NT - 1)
                    last.then_inc(pv_done, 1)

            pe.sem_inc(x_done, 2)
            pe.wait_ge(pad_done, 4)
            turns(step, pe)


def experts1(core, g, io, out):
    nc = core.nc
    with ExitStack() as stack:
        c = core.scope(stack)
        HALF = T // 2
        UNITS = FT * 2
        xnT = c.split("xn2T", [D, T])
        mix = c.sb("mix", [P, E, TT])
        mix_s = c.split("mixs", [P, E * TT])
        raw, w_loaded = g.expert_w, g.expert1_w_loaded

        with ExitStack() as head_stack:
            h = core.scope(head_stack)
            routers = h.sb("routers", [D, 2, E])
            xn, xnT_raw = h.sb("xn2", [P, TT, D]), h.sb("xn2T_raw", [D, T])
            stats, moments = h.sb("ln_stats3", [P, TT, 6]), h.sb("ln_moments3", [P, TT, 2])
            var_eps, rstd = h.sb("ln_var3", [P, TT]), h.sb("ln_rstd3", [P, TT])
            top = h.sb("top", [P, TT, 2])
            probs = h.sb("probs", [P, TT, 2, E])
            sums, rsums = h.sb("sums", [P, TT, 2]), h.sb("rsums", [P, TT, 2])
            both, bsum, rbsum = h.sb("both", [P, TT, E]), h.sb("bsum", [P, TT]), h.sb("rbsum", [P, TT])
            r_loaded, var_done, rstd_done = h.sem("f_rld"), h.sem("f_var"), h.sem("f_rstd")
            xn_done, turned, raw_done, hi_done = (h.sem("f_" + n) for n in ("xn", "turned", "raw", "hi"))
            logits_done, shifted, exp_done, dve_step = (h.sem("f_" + n) for n in ("logits", "shifted", "exp", "dve"))
            turned_ps = g.psum[:, 0:2, :].rearrange("p b n -> p (b n)")
            logits_ps = g.psum[:, 2, 0:TT * 2 * E].rearrange("p (t r e) -> p t r e", r=2, e=E)
            block = head_stack.enter_context(nc.Block())

            @block.sync
            def _(sp):
                sp.dma_start(routers[:, 0, :], io["L1_ffn_w_router"]).then_inc(r_loaded, 16)
                sp.dma_start(routers[:, 1, :], io["L1_ffn_w_gating"]).then_inc(r_loaded, 16)

            @block.gpsimd
            def _(pool):
                pool.wait_ge(var_done, 1)
                pool.tensor_tensor(rstd[:], var_eps[:], g.minus_half[:], ALU.pow).then_inc(rstd_done, 1)

            @block.scalar
            def _(act):
                act.wait_ge(turned, 1)
                act.copy(xnT_raw[:], turned_ps).then_inc(raw_done, 1)
                act.copy(xnT.hi, turned_ps).then_inc(hi_done, 1)
                act.wait_ge(shifted, 1)
                act.activation(probs[:, :, 0, :], probs[:, :, 0, :], ACT.Exp)
                act.activation(probs[:, :, 1, :], probs[:, :, 1, :], ACT.Exp, scale=10.0).then_inc(exp_done, 1)

            @block.vector
            def _(dve):
                step = Chain(dve, dve_step)
                layernorm_stats(dve, step, g.x, stats, moments, var_eps).then_inc(var_done, 1)
                dve.wait_ge(rstd_done, 1)
                layernorm_apply(dve, g.x, moments, rstd, xn).then_inc(xn_done, 1)
                dve.wait_ge(logits_done, 1)
                step(dve.tensor_reduce(top[:], logits_ps, AX.X, ALU.max))
                dve.tensor_tensor(probs[:], logits_ps, top[:].unsqueeze(3).to_broadcast([P, TT, 2, E]),
                                  ALU.subtract).then_inc(shifted, 1)
                dve.wait_ge(hi_done, 1)
                dve.tensor_tensor(xnT.lo, turned_ps, f32(xnT.hi), ALU.subtract)
                dve.wait_ge(exp_done, 1)
                step(dve.tensor_reduce(sums[:], probs[:], AX.X, ALU.add))
                step(dve.reciprocal(rsums[:], sums[:]))
                step(dve.tensor_tensor(probs[:], probs[:], rsums[:].unsqueeze(3).to_broadcast([P, TT, 2, E]), ALU.mult))
                step(dve.tensor_tensor(both[:], probs[:, :, 0, :], probs[:, :, 1, :], ALU.mult))
                step(dve.tensor_reduce(bsum[:], both[:], AX.X, ALU.add))
                step(dve.tensor_scalar(bsum[:], bsum[:], 1e-9, None, ALU.add))
                step(dve.reciprocal(rbsum[:], bsum[:]))
                step(dve.tensor_scalar(rbsum[:], rbsum[:], g.gates[:, 3:4], None, ALU.mult))
                step(dve.tensor_tensor(mix[:].rearrange("p e t -> p t e"), both[:],
                                       rbsum[:].unsqueeze(2).to_broadcast([P, TT, E]), ALU.mult))
                flat = mix[:].rearrange("p e t -> p (e t)")
                step(dve.tensor_copy(mix_s.hi, flat))
                dve.tensor_tensor(mix_s.lo, flat, f32(mix_s.hi), ALU.subtract)

            @block.tensor
            def _(pe):
                pe.wait_ge(xn_done, 1)
                for t in range(TT):
                    last = pe.transpose(turned_ps[:, t * P:(t + 1) * P], xn[:, t, :], g.ident[:])
                last.then_inc(turned, 1)
                pe.wait_ge(raw_done, 1)
                pe.wait_ge(r_loaded, 32)
                for t in range(TT):
                    last = pe.matmul(logits_ps[:, t].rearrange("p r e -> p (r e)"), xnT_raw[:, t * P:(t + 1) * P],
                                     routers[:].rearrange("p r e -> p (r e)"), start=True, stop=True)
                last.then_inc(logits_done, 1)

        parts = [[c.split(f"fws{i}_{n}", [P, F]) for n in range(3)] for i in range(2)]
        silu = [c.sb(f"fsilu{i}", [P, HALF]) for i in range(2)]
        hidden = [c.sb(f"fhidden{i}", [P, HALF]) for i in range(2)]
        hid = [c.split(f"fhid{i}", [P, FT, T]) for i in range(2)]
        ones = c.sb("fones", [P, P], F32R)
        diagonal = c.split("diagonal", [P, TT, P])
        spread = c.sb("spread", [P, T])
        mixed = [c.sb(f"mixed{i}", [D, HALF]) for i in range(2)]
        total = c.sb("total_out", [D, T])
        up_w_hi, up_w_lo, down_w_hi, down_w_lo = (c.sem("f_" + n) for n in ("uwhi", "uwlo", "dwhi", "dwlo"))
        const_done = c.sem("f_const")
        up_done, silu_done, mult_done = c.sem("f_up"), c.sem("f_silu"), c.sem("f_mult")
        hid_hi, hid_lo = c.sem("f_hidhi"), c.sem("f_hidlo")
        diag_done, spread_done, spread_out = c.sem("f_diag"), c.sem("f_spread"), c.sem("f_spreadout")
        down_done, mixed_done, sum_done = c.sem("f_down"), c.sem("f_mixed"), c.sem("f_sum")
        back_done, x_done, stored = c.sem("f_back"), c.sem("f_x"), c.sem("f_stored")

        def up_bank(n, which):
            return g.psum[:, 2 * (n % 2) + which, :]

        def down_bank(d):
            return g.psum[:, 4 + d, :]

        spread_ps = g.psum[:, 6:8, :]

        def half(d):
            return slice(d * HALF, (d + 1) * HALF)

        def turns(step, engine):
            for i in range(2):
                step(0, i)
            with engine.Fori(1, E // 2 - 1) as turn:
                for i in range(2):
                    step(turn, i)
            for i in range(2):
                step(E // 2 - 1, i)
            step(E // 2, 0, drain=True)

        def before(turn, i):
            return isinstance(turn, int) and turn == 0 and i < 0

        def ahead(turn, i):
            return not (isinstance(turn, int) and turn * 2 + i + 1 >= E)

        block = stack.enter_context(nc.Block())

        @block.sync
        def _(sp):
            def step(turn, i, drain=False):
                if drain or (isinstance(turn, int) and turn == 0):
                    return
                e = turn * 2 + i
                sp.wait_ge(up_w_lo, e - 1)
                sp.wait_ge(down_w_lo, e - 1)
                load_expert(sp, io, LAYER1_EXPERTS, e, raw[i], w_loaded[i])

            turns(step, sp)
            for d in range(2):
                sp.wait_ge(x_done, d + 1)
                sp.dma_start(out[d * HALF:(d + 1) * HALF, :].rearrange("(t p) d -> p t d", p=P),
                             g.x[:, d * TT // 2:(d + 1) * TT // 2, :]).then_inc(stored, 16)
            sp.wait_ge(stored, 32)

        @block.gpsimd
        def _(pool):
            def low(i, n):
                return pool.tensor_tensor(parts[i % 2][n].lo, raw[i % 2][n][:], f32(parts[i % 2][n].hi),
                                          ALU.subtract)

            def split_up(turn, i):
                e = turn * 2 + i
                wait(pool, up_done, (e - 1) * UNITS)
                for n in range(2):
                    pool.wait_ge(up_w_hi, e * 2 + n + 1)
                    last = low(i, n)
                last.then_inc(up_w_lo, 1)

            def split_down(turn, i):
                e = turn * 2 + i
                wait(pool, down_done, (e - 1) * 2)
                pool.wait_ge(down_w_hi, e + 1)
                low(i, 2).then_inc(down_w_lo, 1)

            def step(turn, i, drain=False):
                e = turn * 2 + i
                if not drain and ahead(turn, i):
                    split_up(turn, i + 1)
                if not drain:
                    wait(pool, spread_done, e)
                    for part, of in ((diagonal.hi, mix_s.hi), (diagonal.lo, mix_s.lo)):
                        last = pool.tensor_tensor(
                            part, g.ident[:].unsqueeze(1).to_broadcast([P, TT, P]),
                            f32(of[:, bass.ds(e * TT, TT)]).unsqueeze(2).to_broadcast([P, TT, P]), ALU.mult)
                    last.then_inc(diag_done, 1)
                if not before(turn, i - 1):
                    for d in range(2):
                        pool.wait_ge(mixed_done, (e - 1) * 2 + d + 1)
                        wait(pool, sum_done, (e - 2) * 2 + d + 1)
                        pool.tensor_tensor(total[:, half(d)], total[:, half(d)], mixed[d][:],
                                           ALU.add).then_inc(sum_done, 1)
                if not drain and ahead(turn, i):
                    split_down(turn, i + 1)

            pool.memset(total[:], 0.0).then_inc(const_done, 1)
            pool.memset(ones[:].bitcast(F32), 1.0).then_inc(const_done, 1)
            pool.wait_ge(const_done, 1)
            split_up(0, 0)
            split_down(0, 0)
            turns(step, pool)

        @block.scalar
        def _(act):
            def split_weight(turn, i, n):
                e = turn * 2 + i
                if n == 0:
                    act.wait_ge(w_loaded[i % 2], (turn + i // 2) * 48 + 48)
                    wait(act, up_done, (e - 1) * UNITS)
                if n == 2:
                    wait(act, down_done, (e - 1) * 2)
                act.copy(parts[i % 2][n].hi, raw[i % 2][n][:]).then_inc(down_w_hi if n == 2 else up_w_hi, 1)

            def hidden_high(turn, i, u):
                act.wait_ge(mult_done, (turn * 2 + i) * UNITS + u + 1)
                act.copy(hid[i % 2].hi[:, u // 2, half(u % 2)], hidden[u % 2][:]).then_inc(hid_hi, 1)

            def step(turn, i, drain=False):
                e = turn * 2 + i
                for u in range(UNITS):
                    n = e * UNITS + u
                    if not drain:
                        act.wait_ge(up_done, n + 1)
                        wait(act, mult_done, n - 1)
                        act.activation(silu[u % 2][:], up_bank(u, 0), ACT.Silu).then_inc(silu_done, 1)
                    if u == 0:
                        if not before(turn, i - 1):
                            hidden_high(turn, i - 1, UNITS - 1)
                        if drain:
                            return
                    else:
                        hidden_high(turn, i, u - 1)
                    if u in (1, 2, 4) and ahead(turn, i):
                        split_weight(turn, i + 1, (1, 2, 4).index(u))
                    if u == 6:
                        act.wait_ge(spread_done, e + 1)
                        wait(act, mixed_done, e * 2)
                        act.copy(spread[:].rearrange("p (b n) -> p b n", b=2), spread_ps).then_inc(spread_out, 1)

            for n in range(3):
                split_weight(0, 0, n)
            turns(step, act)

        @block.vector
        def _(dve):
            def hidden_low(turn, i, u):
                dve.wait_ge(hid_hi, (turn * 2 + i) * UNITS + u + 1)
                dve.tensor_tensor(hid[i % 2].lo[:, u // 2, half(u % 2)], hidden[u % 2][:],
                                  f32(hid[i % 2].hi[:, u // 2, half(u % 2)]), ALU.subtract).then_inc(hid_lo, 1)

            def step(turn, i, drain=False):
                e = turn * 2 + i
                for u in range(UNITS):
                    n = e * UNITS + u
                    if not drain:
                        dve.wait_ge(silu_done, n + 1)
                        wait(dve, hid_lo, n - 1)
                        dve.tensor_tensor(hidden[u % 2][:], silu[u % 2][:], up_bank(u, 1), ALU.mult).then_inc(mult_done, 1)
                    if u > 0 and not drain:
                        hidden_low(turn, i, u - 1)
                    if u == 0 and not before(turn, i - 1):
                        hidden_low(turn, i - 1, UNITS - 1)
                    if u in (3, 5) and not before(turn, i - 1):
                        d = (u - 3) // 2
                        dve.wait_ge(down_done, (e - 1) * 2 + d + 1)
                        dve.wait_ge(spread_out, e)
                        wait(dve, sum_done, (e - 2) * 2 + d + 1)
                        dve.tensor_tensor(mixed[d][:], down_bank(d), spread[:, half(d)], ALU.mult).then_inc(mixed_done, 1)

            turns(step, dve)
            for d in range(2):
                dve.wait_ge(back_done, d + 1)
                rows = g.x[:, d * TT // 2:(d + 1) * TT // 2, :]
                dve.tensor_tensor(rows, g.psum[:, d, :].rearrange("p (t d) -> p t d", d=D), rows,
                                  ALU.add).then_inc(x_done, 1)

        @block.tensor
        def _(pe):
            def step(turn, i, drain=False):
                e = turn * 2 + i
                if not drain:
                    pe.wait_ge(up_w_lo, e + 1)
                for u in range(UNITS):
                    n = e * UNITS + u
                    if not drain:
                        wait(pe, mult_done, n - 1)
                        for which in range(2):
                            f = u // 2
                            last = matmul3(pe, up_bank(u, which), parts[i][which][:, f * P:(f + 1) * P],
                                           xnT[:, half(u % 2)])
                        last.then_inc(up_done, 1)
                    if u in (1, 3) and not before(turn, i - 1):
                        d = (u - 1) // 2
                        pe.wait_ge(hid_lo, e * UNITS)
                        pe.wait_ge(down_w_lo, e)
                        wait(pe, mixed_done, (e - 2) * 2 + d + 1)
                        for f in range(FT):
                            last = matmul3(pe, down_bank(d), parts[(i - 1) % 2][2][:, f * D:(f + 1) * D],
                                           hid[(i - 1) % 2][:, f, half(d)], start=f == 0, stop=f == FT - 1)
                        last.then_inc(down_done, 1)
                    if u == 5 and not drain:
                        pe.wait_ge(diag_done, e + 1)
                        wait(pe, spread_out, e)
                        for b in range(2):
                            tiles = slice(b * TT // 2, (b + 1) * TT // 2)
                            pe.matmul(spread_ps[:, b, :], ones[:], diagonal.hi[:, tiles, :], start=True, stop=False)
                            last = pe.matmul(spread_ps[:, b, :], ones[:], diagonal.lo[:, tiles, :],
                                             start=False, stop=True)
                        last.then_inc(spread_done, 1)

            pe.wait_ge(const_done, 2)
            turns(step, pe)
            for d in range(2):
                pe.wait_ge(sum_done, (E - 1) * 2 + d + 1)
                for t in range(TT // 2):
                    at = d * HALF + t * P
                    last = pe.transpose(g.psum[:, d, t * P:(t + 1) * P], total[:, at:at + P], g.ident[:])
                last.then_inc(back_done, 1)


def alloc(core, nc):
    class Shared:
        pass

    g = Shared()
    g.psum = core.stack.enter_context(nc.psum_tensor("ps_all", [P, 8, BANK], F32))
    g.x = core.sb("x", [P, TT, D])
    g.attended = core.sb("attended", [P, TT * D])
    g.ident = core.sb("ident", [P, P])
    g.zeros = core.sb("zeros", [P, 4 * D])
    g.minus_half = core.sb("minus_half", [P, TT])
    g.bias0 = core.sb("bias0", [P, D])
    g.bias1 = core.sb("bias1", [P, D])
    g.gates = core.sb("gates", [P, 4])
    g.expert_w = [[core.sb(f"expert_w{i}_{n}", [P, F]) for n in range(3)] for i in range(2)]
    g.expert_w_loaded = [core.sem(f"ld_expert0_{i}") for i in range(2)]
    g.expert1_w_loaded = [core.sem(f"ld_expert1_{i}") for i in range(2)]
    g.gather_at = core.sb("gather_at", [P, TOPK, TT], U32)
    g.token_weights = core.sb("token_weights", [P, TOPK, TT])
    g.ctxT = core.split("ctxT", [C, KEYS])
    g.expert_in = nc.dram_tensor("expert_in", [SLOTS, D], F32, kind="Internal").ap()
    g.expert_out = nc.dram_tensor("expert_out", [SLOTS, D], F32, kind="Internal").ap()
    g.values1 = nc.dram_tensor("values1", [B, H1 * M, D], F32, kind="Internal").ap()
    g.value_weights_loaded = core.sem("value_weights_loaded")
    g.expert_in_zeroed = core.sem("expert_in_zeroed")
    return g


def flamingo(nc, io, out, until=None):
    io = dict(io)
    io["x"] = io["x"].rearrange("b s d -> (b s) d")
    io["ctx"] = io["ctx_768"].rearrange("b m c -> (b m) c")
    with ExitStack() as stack:
        core = Core(nc, stack)
        g = alloc(core, nc)
        with ExitStack() as layer0:
            c0 = core.scope(layer0)
            g.xnT = c0.split("xnT", [D, T])
            g.keys0 = c0.split("keys0", [D, H0, KEYS])
            g.values0 = c0.split("values0", [P, KT, H0 * D])
            prepare0(core, g, io)
            attention0(core, g)
        if until == "attention0":
            dump(core, g.attended[:], out)
            return
        with ExitStack() as layer1:
            c1 = core.scope(layer1)
            g.keys1 = c1.split("keys1", [D, B, H1, M])
            g.wv1 = c1.sb("wv1", [C, H1 * DH1])
            g.wo1 = c1.sb("wo1", [P, H1 // 2, D])
            dispatch(core, g, io)
            if until == "dispatch":
                dump(core, g.expert_in, out)
                return
            experts0(core, g, io)
            combine(core, g)
            if until == "experts0":
                dump(core, g.x[:].rearrange("p t d -> p (t d)"), out)
                return
            attention1(core, g, io)
            if until == "attention1":
                dump(core, g.x[:].rearrange("p t d -> p (t d)"), out)
                return
        experts1(core, g, io, out.rearrange("b s d -> (b s) d"))


def dump(core, ap, out):
    with core.nc.semaphore("dump") as s, core.nc.Block() as block:
        @block.sync
        def _(sp):
            sp.dma_start(out, ap).then_inc(s, 16)
            sp.wait_ge(s, 16)


_INS = ["x", "ctx_768", "g_xattn", "g_ffn",
        "L0_xattn_Wq", "L0_xattn_Wk", "L0_xattn_Wv", "L0_xattn_Wout", "L0_xattn_bout",
        "L0_ffn_Wr", "L0_ffn_W1", "L0_ffn_W3", "L0_ffn_W2",
        "L1_xattn_Wq", "L1_xattn_Wk", "L1_xattn_Wv", "L1_xattn_Wo", "L1_xattn_bo",
        "L1_ffn_w_router", "L1_ffn_w_gating", "L1_ffn_w_gate", "L1_ffn_w_up", "L1_ffn_w_down"]


def kernel(**inputs):
    import concourse.bacc as _bacc
    from concourse.bass_utils import run_bass_kernel_spmd as _run

    nc = _bacc.Bacc("TRN2", target_bir_lowering=False, num_devices=1)
    arrays, io = {}, {}
    for name in _INS:
        a = np.ascontiguousarray(inputs[name])
        arrays[f"in_{name}_dram"] = a
        io[name] = nc.dram_tensor(f"in_{name}_dram", a.shape, mybir.dt.from_np(a.dtype), kind="ExternalInput").ap()
    out = nc.dram_tensor("out_dram", (B, S, D), F32, kind="ExternalOutput").ap()
    flamingo(nc, io, out)
    r = _run(nc, [arrays], core_ids=[0])
    return r.results[0]["out_dram"]
```

```python
from contextlib import ExitStack

import numpy as np

import concourse.bass as bass
from concourse import mybir

F32 = mybir.dt.float32
F32R = mybir.dt.float32r
BF16 = mybir.dt.bfloat16
U32 = mybir.dt.uint32
ALU = mybir.AluOpType
ACT = mybir.ActivationFunctionType
AX = mybir.AxisListType

P = 128
D = 128
C = 96
B, S, M = 8, 128, 77
T = B * S
TT = T // P
KEYS = B * M
KT = -(-KEYS // P)
KLAST = KEYS - (KT - 1) * P
H0, DH0 = 8, 128
H1, DH1 = 16, 64
E, F = 8, 512
FT = F // P
TOPK = 2
CAP = max(1, -(-T * TOPK * 5 // (4 * E)))
SLOTS = E * CAP
EPS = 1e-5
BANK = 512
SCALE0 = 1.5 * DH0 ** -0.5
SCALE1 = DH1 ** -0.5


def f32(ap):
    return ap.bitcast(F32)


class Split:

    def __init__(self, hi, lo):
        self.hi, self.lo = hi, lo

    def __getitem__(self, at):
        return Split(self.hi[at], self.lo[at])

    def view(self, pattern, **sizes):
        return Split(self.hi.rearrange(pattern, **sizes), self.lo.rearrange(pattern, **sizes))


def matmul3(pe, out, lhsT, rhs, start=True, stop=True):
    pe.matmul(out, lhsT.hi, rhs.hi, start=start, stop=False)
    pe.matmul(out, lhsT.hi, rhs.lo, start=False, stop=False)
    return pe.matmul(out, lhsT.lo, rhs.hi, start=False, stop=stop)


class Core:

    def __init__(self, nc, stack):
        self.nc, self.stack = nc, stack

    def scope(self, stack):
        return Core(self.nc, stack)

    def sb(self, name, shape, dt=F32):
        return self.stack.enter_context(self.nc.sbuf_tensor("sb_" + name, shape, dt))

    def split(self, name, shape):
        return Split(self.sb(name + "_hi", shape, F32R)[:], self.sb(name + "_lo", shape, F32R)[:])

    def sem(self, name):
        return self.stack.enter_context(self.nc.semaphore(name))


def wait(eng, sem, value):
    if not (isinstance(value, int) and value <= 0):
        eng.wait_ge(sem, value)


class Steps:

    def __init__(self, sem):
        self.sem, self.n = sem, 0


class Chain:

    def __init__(self, eng, steps):
        self.eng, self.steps = eng, steps

    def __call__(self, instruction):
        self.steps.n += 1
        instruction.then_inc(self.steps.sem, 1)
        self.eng.wait_ge(self.steps.sem, self.steps.n)
        return instruction


def layernorm_stats(dve, step, x, stats, moments, tiles=range(TT)):
    for t in tiles:
        last = dve.bn_stats(stats[:, t, :], x[:, t, :])
    step(last)
    for t in tiles:
        last = dve.bn_aggr(moments[:, t, :], stats[:, t, :])
    step(last)


def layernorm_variance(dve, moments, variance_eps):
    return dve.tensor_scalar(variance_eps[:], moments[:, :, 1], EPS, None, ALU.add)


def layernorm_apply(dve, x, moments, rstd, xn, done):
    for t in range(TT):
        dve.tensor_scalar(xn[:, t, :], x[:, t, :], moments[:, t, 0:1], rstd[:, t:t + 1],
                          ALU.subtract, ALU.mult).then_inc(done, 1)


def prepare0(core, g, io):
    nc = core.nc
    with ExitStack() as stack:
        c = core.scope(stack)
        wq = c.sb("wq0", [P, H0 * DH0])
        wk = c.sb("wk0", [C, H0 * DH0])
        wv = c.sb("wv0", [C, H0 * DH0])
        wout = c.sb("wout0", [P, H0, D])
        ctx_rows = c.sb("ctx_rows", [P, KT, C])
        wqT, wkT, wvT = (c.split(n, [P, H0, w]) for n, w in (("wq0T", D), ("wk0T", C), ("wv0T", C)))
        wout_s = c.split("wout0s", [P, H0, D])
        qk = c.split("qk0", [C, H0, D])
        vo = c.split("vo0", [C, H0 * D])
        xn = c.sb("xn_first", [P, TT, D])
        stats, moments = g.stats, g.moments
        var_eps = c.sb("ln_var0", [P, TT])
        rstd = c.sb("ln_rstd0", [P, TT])
        gates_raw = c.sb("gates_raw", [P, 4])

        loaded = {n: c.sem("a_ld_" + n) for n in ("x", "ctx", "wq", "wk", "wv", "wout", "small")}
        ident_done, zero_done = c.sem("a_ident"), c.sem("a_zero")
        var_done, rstd_done, xn_done = c.sem("a_var"), c.sem("a_rstd"), c.sem("a_xn")
        pe_done, hi_done, lo_done = c.sem("a_pe"), c.sem("a_hi"), c.sem("a_lo")
        wout_hi, wout_lo = c.sem("a_wouthi"), c.sem("a_woutlo")

        CTX, WQ, WK, WV, QK, VO, XN = range(7)
        K0 = 7
        V0 = K0 + H0
        JOBS = V0 + KT

        def slot(j):
            return g.psum[:, 2 * (j % 4):2 * (j % 4) + 2, :].rearrange("p b n -> p (b n)")

        def evacuation(j):
            ps = slot(j)
            if j == CTX:
                return ps[0:C, 0:KEYS], g.ctxT, 1.0
            if j == WQ:
                return ps.rearrange("p (h n) -> p h n", n=P), wqT, 1.0
            if j in (WK, WV):
                return ps.rearrange("p (h n) -> p h n", n=P)[:, :, 0:C], (wkT, wvT)[j - WK], 1.0
            if j == QK:
                return ps[0:C, :].rearrange("p (h n) -> p h n", n=P), qk, SCALE0
            if j == VO:
                return ps[0:C, :], vo, 1.0
            if j == XN:
                return ps, g.xnT, 1.0
            if j < V0:
                half = ps.rearrange("p (b n) -> p b n", b=2)[:, :, 0:KEYS // 2]
                return half, g.keys0[:, j - K0, :].view("p (b n) -> p b n", b=2), 1.0
            kt = j - V0
            rows = P if kt < KT - 1 else KLAST
            return ps[0:rows, :], g.values0[0:rows, kt, :], 1.0

        block = stack.enter_context(nc.Block())

        @block.sync
        def _(sp):
            sp.dma_start(ctx_rows[:, 0:KT - 1, :],
                         io["ctx"][0:(KT - 1) * P, :].rearrange("(t p) c -> p t c", p=P)).then_inc(loaded["ctx"], 16)
            sp.dma_start(ctx_rows[0:KLAST, KT - 1, :], io["ctx"][(KT - 1) * P:KEYS, :]).then_inc(loaded["ctx"], 16)
            sp.dma_start(wq[:], io["L0_xattn_Wq"]).then_inc(loaded["wq"], 16)
            sp.dma_start(wk[:], io["L0_xattn_Wk"]).then_inc(loaded["wk"], 16)
            sp.wait_ge(zero_done, 1)
            for e in range(E):
                sp.dma_start(g.expert_in[e * CAP:(e + 1) * CAP, :].rearrange("(p r) d -> p (r d)", r=4),
                             g.zeros[0:CAP // 4, :]).then_inc(g.expert_in_zeroed, 16)

        @block.scalar
        def _(act):
            act.dma_start(g.x[:], io["x"].rearrange("(t p) d -> p t d", p=P)).then_inc(loaded["x"], 16)
            act.dma_start(wv[:], io["L0_xattn_Wv"]).then_inc(loaded["wv"], 16)
            act.dma_start(wout[:], io["L0_xattn_Wout"].rearrange("(h p) d -> p h d", p=P)).then_inc(loaded["wout"], 16)
            act.dma_start(g.bias0[:], io["L0_xattn_bout"].partition_broadcast(P)).then_inc(loaded["small"], 16)
            act.dma_start(g.bias1[:], io["L1_xattn_bo"].partition_broadcast(P)).then_inc(loaded["small"], 16)
            act.dma_start(gates_raw[:, 0:2], io["g_xattn"].partition_broadcast(P)).then_inc(loaded["small"], 16)
            act.dma_start(gates_raw[:, 2:4], io["g_ffn"].partition_broadcast(P)).then_inc(loaded["small"], 16)
            for j in range(JOBS):
                if j == QK:
                    act.wait_ge(loaded["wout"], 16)
                    act.copy(wout_s.hi, wout[:]).then_inc(wout_hi, 1)
                ps, to, factor = evacuation(j)
                act.wait_ge(pe_done, j + 1)
                act.activation(to.hi, ps, ACT.Copy, scale=factor).then_inc(hi_done, 1)
            act.wait_ge(loaded["small"], 64)
            act.activation(g.gates[:], gates_raw[:], ACT.Tanh).then_inc(hi_done, 1)

        @block.gpsimd
        def _(pool):
            step = Chain(pool, Steps(ident_done))
            step(pool.memset(g.ident[:], 0.0))
            step(pool.affine_select(out=g.ident[:], in_=g.ident[:], compare_op=ALU.not_equal, fill=1.0,
                                    base=0, pattern=[[-1, P]], channel_multiplier=1))
            pool.memset(g.zeros[:], 0.0).then_inc(zero_done, 1)
            pool.memset(g.minus_half[:], -0.5).then_inc(zero_done, 1)
            pool.wait_ge(zero_done, 2)
            pool.wait_ge(var_done, 1)
            pool.tensor_tensor(rstd[:], var_eps[:], g.minus_half[:], ALU.pow).then_inc(rstd_done, 1)

        @block.vector
        def _(dve):
            step = Chain(dve, g.dve_steps)
            dve.wait_ge(loaded["x"], 16)
            layernorm_stats(dve, step, g.x, stats, moments)
            layernorm_variance(dve, moments, var_eps).then_inc(var_done, 1)
            for j in range(JOBS):
                if j == WV:
                    dve.wait_ge(rstd_done, 1)
                    layernorm_apply(dve, g.x, moments, rstd, xn, xn_done)
                if j == QK:
                    dve.wait_ge(wout_hi, 1)
                    dve.tensor_tensor(wout_s.lo, wout[:], f32(wout_s.hi), ALU.subtract).then_inc(wout_lo, 1)
                ps, to, factor = evacuation(j)
                dve.wait_ge(hi_done, j + 1)
                if factor == 1.0:
                    dve.tensor_tensor(to.lo, ps, f32(to.hi), ALU.subtract).then_inc(lo_done, 1)
                else:
                    dve.scalar_tensor_tensor(out=to.lo, in0=ps, scalar=factor, in1=f32(to.hi),
                                             op0=ALU.mult, op1=ALU.subtract).then_inc(lo_done, 1)

        @block.tensor
        def _(pe):
            pe.wait_ge(ident_done, 2)
            for j in range(JOBS):
                ps = slot(j)
                wait(pe, lo_done, j - 3)
                if j == CTX:
                    pe.wait_ge(loaded["ctx"], 32)
                    for kt in range(KT):
                        rows = P if kt < KT - 1 else KLAST
                        last = pe.transpose(ps[0:C, kt * P:kt * P + rows], ctx_rows[0:rows, kt, :],
                                            g.ident[0:rows, 0:rows])
                elif j in (WQ, WK, WV):
                    pe.wait_ge(loaded[("wq", "wk", "wv")[j - WQ]], 16)
                    w, rows = ((wq, D), (wk, C), (wv, C))[j - WQ]
                    for h in range(H0):
                        last = pe.transpose(ps[:, h * P:h * P + rows], w[:, h * DH0:(h + 1) * DH0],
                                            g.ident[0:rows, 0:rows])
                elif j == QK:
                    pe.wait_ge(lo_done, WK + 1)
                    for h in range(H0):
                        last = matmul3(pe, ps[0:C, h * D:(h + 1) * D], wkT[:, h, :], wqT[:, h, :])
                elif j == VO:
                    pe.wait_ge(lo_done, WV + 1)
                    pe.wait_ge(wout_lo, 1)
                    for h in range(H0):
                        last = matmul3(pe, ps[0:C, h * D:(h + 1) * D], wvT[:, h, :], wout_s[:, h, :])
                elif j == XN:
                    for t in range(TT):
                        pe.wait_ge(xn_done, t + 1)
                        last = pe.transpose(ps[:, t * P:(t + 1) * P], xn[:, t, :], g.ident[:])
                elif j < V0:
                    pe.wait_ge(lo_done, QK + 1)
                    for b in range(2):
                        n = KEYS // 2
                        last = matmul3(pe, ps[:, b * BANK:b * BANK + n], qk[:, j - K0, :],
                                       g.ctxT[:, b * n:(b + 1) * n])
                else:
                    pe.wait_ge(lo_done, VO + 1)
                    kt = j - V0
                    rows = P if kt < KT - 1 else KLAST
                    for b in range(2):
                        last = matmul3(pe, ps[0:rows, b * BANK:(b + 1) * BANK],
                                       g.ctxT[:, kt * P:kt * P + rows], vo[:, b * BANK:(b + 1) * BANK])
                last.then_inc(pe_done, 1)


def attention0(core, g, io):
    nc = core.nc
    with ExitStack() as stack:
        c = core.scope(stack)
        queries = [c.split(f"queries{i}", [D, P]) for i in range(2)]
        weights = [c.sb(f"weights{i}", [P, KT * P]) for i in range(4)]
        weightsT = [c.split(f"weights{i}T", [P, KT, 2, P]) for i in range(2)]
        neg_max = c.sb("neg_max0", [P, 2])
        den, rden = c.sb("den0", [P, 4]), c.sb("rden0", [P, 4])
        outT = c.sb("outT", [D, 2 * P])

        queries_ready, pad_done = c.sem("b_queries"), c.sem("b_pad")
        scores_done, max_done, exp_done = c.sem("b_scores"), c.sem("b_max"), c.sem("b_exp")
        recip_done, norm_done = c.sem("b_recip"), c.sem("b_norm")
        turned, hi_done, lo_done = c.sem("b_turned"), c.sem("b_hi"), c.sem("b_lo")
        pv_done, out_done, back_done, attended_done = (c.sem("b_" + n) for n in ("pv", "out", "back", "attended"))

        UNITS = 2 * H0
        TURNS = TT // 2
        CHUNKS = [(0, 3), (3, KT)]
        DRAIN = 6
        half = KEYS // 2

        def scores(u):
            return g.psum[:, 2 * (u % 2):2 * (u % 2) + 2, 0:half]

        def turned_bank(i):
            return g.psum[:, 4 + i, :]

        out_ps = g.psum[:, 6, 0:2 * P]
        back_ps = g.psum[:, 7, 0:2 * D]

        def steps(engine_step, engine):
            for s in range(UNITS):
                engine_step(0, s)
            with engine.Fori(1, TURNS) as turn:
                for s in range(UNITS):
                    engine_step(turn, s)
            for s in range(DRAIN):
                engine_step(TURNS, s)

        def unit(turn, s):
            return turn * UNITS + s

        def exists(turn, u):
            return not isinstance(turn, int) or 0 <= turn * UNITS + u < TURNS * UNITS

        block = stack.enter_context(nc.Block())

        @block.sync
        def _(sp):
            for j, name in enumerate(("L1_xattn_Wq", "L1_xattn_Wk", "L1_xattn_Wv")):
                rows = io[name].shape[0]
                for i in range(2):
                    sp.dma_start(g.weights1[j][i][0:rows, :], io[name][:, i * F:(i + 1) * F]
                                 ).then_inc(g.weights1_loaded[j], 16)

        @block.gpsimd
        def _(pool):
            for i in range(4):
                pool.memset(weights[i][:, KEYS:KT * P], 0.0).then_inc(pad_done, 1)

            def step(turn, s):
                if s < 2 and not isinstance(turn, int):
                    wait(pool, scores_done, unit(turn, s - 1))
                    at = bass.ds((turn * 2 + s) * P, P)
                    pool.tensor_copy(queries[s].hi, f32(g.xnT.hi[:, at])).then_inc(queries_ready, 1)
                    pool.tensor_copy(queries[s].lo, f32(g.xnT.lo[:, at])).then_inc(queries_ready, 1)
                if exists(turn, s - 2):
                    u = s - 2
                    w = weights[u % 4][:, 0:KEYS]
                    pool.wait_ge(recip_done, unit(turn, u + 1))
                    pool.tensor_tensor(w, w, rden[:, u % 4:u % 4 + 1].to_broadcast([P, KEYS]),
                                       ALU.mult).then_inc(norm_done, 1)

            steps(step, pool)

        @block.tensor
        def _(pe):
            def values_product(turn, u, a, b):
                h = (u // 2) % H0
                for kt in range(a, b):
                    rows = P if kt < KT - 1 else KLAST
                    last = matmul3(pe, out_ps, g.values0[0:rows, kt, h * D:(h + 1) * D],
                                   weightsT[h % 2][0:rows, kt].view("p t q -> p (t q)"),
                                   start=h == 0 and kt == 0, stop=h == H0 - 1 and kt == KT - 1)
                return last

            def step(turn, s):
                if exists(turn, s):
                    q = queries[s % 2]
                    if isinstance(turn, int):
                        q = g.xnT[:, (turn * 2 + s % 2) * P:(turn * 2 + s % 2 + 1) * P]
                    elif s < 2:
                        pe.wait_ge(queries_ready, turn * 4 + 2 * s - 2)
                    wait(pe, exp_done, unit(turn, s - 1))
                    for b in range(2):
                        last = matmul3(pe, scores(s)[:, b, :], q,
                                       g.keys0[:, s // 2, b * half:(b + 1) * half])
                    last.then_inc(scores_done, 1)
                if exists(turn, s - 2):
                    u = s - 2
                    pe.wait_ge(norm_done, unit(turn, u + 1))
                    if isinstance(turn, int) and unit(turn, u) < 4:
                        pe.wait_ge(pad_done, 4)
                    for i, (a, b) in enumerate(CHUNKS):
                        wait(pe, lo_done, unit(turn, u - 1) * 2 + i + 1)
                        for kt in range(a, b):
                            last = pe.transpose(turned_bank(i)[:, (kt - a) * P:(kt - a + 1) * P],
                                                weights[u % 4][:, kt * P:(kt + 1) * P], g.ident[:])
                        last.then_inc(turned, 1)
                if s == 4 and exists(turn, s - 5):
                    pe.wait_ge(out_done, turn)
                    for t in range(2):
                        last = pe.transpose(back_ps[:, t * D:(t + 1) * D], outT[:, t * P:(t + 1) * P], g.ident[:])
                    last.then_inc(back_done, 1)
                if s % 2 == 0 and exists(turn, s - 4):
                    pe.wait_ge(lo_done, unit(turn, s - 3) * 2 + 1)
                    if s == 4:
                        wait(pe, out_done, turn)
                    values_product(turn, s - 4, *CHUNKS[0])
                if s % 2 == 1 and exists(turn, s - 5):
                    pe.wait_ge(lo_done, unit(turn, s - 4) * 2 + 2)
                    values_product(turn, s - 5, *CHUNKS[1]).then_inc(pv_done, 1)

            steps(step, pe)

        @block.scalar
        def _(act):
            def step(turn, s):
                if s == 4 and exists(turn, s - 5):
                    act.wait_ge(pv_done, turn * H0)
                    act.copy(outT[:], out_ps).then_inc(out_done, 1)
                if exists(turn, s - 2):
                    u = s - 2
                    if u % 2 == 0:
                        wait(act, pv_done, turn * H0 + u // 2 - 1)
                    for i, (a, b) in enumerate(CHUNKS):
                        act.wait_ge(turned, unit(turn, u) * 2 + i + 1)
                        act.copy(weightsT[(u // 2) % 2].hi[:, a:b, u % 2, :],
                                 turned_bank(i)[:, 0:(b - a) * P].rearrange("p (k q) -> p k q", q=P)).then_inc(hi_done, 1)
                if exists(turn, s):
                    act.wait_ge(max_done, unit(turn, s + 1))
                    wait(act, turned, unit(turn, s - 3) * 2)
                    wait(act, recip_done, unit(turn, s - 3))
                    act.activation(weights[s % 4][:, 0:KEYS].rearrange("p (b n) -> p b n", b=2), scores(s),
                                   ACT.Exp, bias=neg_max[:, s % 2:s % 2 + 1],
                                   accum_out=den[:, s % 4:s % 4 + 1]).then_inc(exp_done, 1)

            steps(step, act)

        @block.vector
        def _(dve):
            def step(turn, s):
                if exists(turn, s):
                    dve.wait_ge(scores_done, unit(turn, s + 1))
                    wait(dve, exp_done, unit(turn, s - 1))
                    dve.tensor_reduce(neg_max[:, s % 2:s % 2 + 1], scores(s), AX.XY, ALU.max,
                                      negate=True).then_inc(max_done, 1)
                if exists(turn, s - 2):
                    u = s - 2
                    for i, (a, b) in enumerate(CHUNKS):
                        dve.wait_ge(hi_done, unit(turn, u) * 2 + i + 1)
                        dve.tensor_tensor(weightsT[(u // 2) % 2].lo[:, a:b, u % 2, :],
                                          turned_bank(i)[:, 0:(b - a) * P].rearrange("p (k q) -> p k q", q=P),
                                          f32(weightsT[(u // 2) % 2].hi[:, a:b, u % 2, :]),
                                          ALU.subtract).then_inc(lo_done, 1)
                if exists(turn, s):
                    wait(dve, norm_done, unit(turn, s - 3))
                    dve.wait_ge(exp_done, unit(turn, s + 1))
                    dve.reciprocal(rden[:, s % 4:s % 4 + 1], den[:, s % 4:s % 4 + 1]).then_inc(recip_done, 1)
                if s == 5 and exists(turn, s - 6):
                    dve.wait_ge(back_done, turn)
                    dve.tensor_tensor(g.attended[:, bass.ds((turn - 1) * 2 * D, 2 * D)].rearrange("p (t d) -> p t d", d=D),
                                      back_ps.rearrange("p (t d) -> p t d", d=D),
                                      g.bias0[:].unsqueeze(1).to_broadcast([P, 2, D]), ALU.add).then_inc(attended_done, 1)

            steps(step, dve)


LAYER0_EXPERTS = ("L0_ffn_W1", "L0_ffn_W3", "L0_ffn_W2")
LAYER1_EXPERTS = ("L1_ffn_w_gate", "L1_ffn_w_up", "L1_ffn_w_down")


def load_expert(sp, io, names, e, raw, loaded, which=(0, 1, 2)):
    for n in which:
        w = io[names[n]]
        if n < 2:
            src = w.rearrange("e d f -> (e d) f")[bass.ds(e * D, D), :]
            sp.dma_start(raw[n][:], src).then_inc(loaded, 16)
        else:
            src = w.rearrange("e f d -> (e f) d")[bass.ds(e * F, F), :]
            sp.dma_start(raw[n][:].rearrange("p (t d) -> p t d", d=D),
                         src.rearrange("(t p) d -> p t d", p=P)).then_inc(loaded, 16)


SLOT_TILES = [(0, 112), (112, 216), (216, CAP)]
NSLOT = len(SLOT_TILES)
CREDIT = 16
FIRST_SLOTS, LIKE_SLOTS = SLOT_TILES[0][1], SLOT_TILES[1][1] - SLOT_TILES[1][0]


def move_slots(queue, dram, e, tile, sem, to_dram):
    for src, dst in ((dram[bass.ds(e * CAP, FIRST_SLOTS), :], tile[0:FIRST_SLOTS, 0, :]),
                     (dram[bass.ds(e * CAP + FIRST_SLOTS, 2 * LIKE_SLOTS), :].rearrange("(s p) d -> p s d", s=2),
                      tile[0:LIKE_SLOTS, 1:NSLOT, :])):
        if to_dram:
            src, dst = dst, src
        queue.dma_start(dst, src).then_inc(sem, 16)


def dispatch(core, g, io):
    nc = core.nc
    with ExitStack() as stack:
        c = core.scope(stack)
        wr, wo = c.sb("wr0", [D, E]), c.sb("wo1", [P, H1 // 2, D])
        wqT, wkT = c.split("wq1T", [P, H1 // 2, D]), c.split("wk1T", [P, H1 // 2, C])
        wvT, wo_s = c.split("wv1T", [P, H1 // 2, C]), c.split("wo1s", [P, H1 // 2, D])
        qk = c.split("qk1", [C, 2, 2, H1 // 4, D])
        xn = c.sb("xn0", [P, TT, D])
        xnT = c.sb("xn0T", [D, T])
        stats, moments = g.stats, g.moments
        var_eps, rstd = c.sb("ln_var1", [P, TT]), c.sb("ln_rstd1", [P, TT])
        earlier = c.sb("earlier", [P, P], BF16)
        ones = c.sb("ones_bf", [P, P], BF16)
        descending = c.sb("descending", [P, TT, E])
        logits = c.sb("logits", [P, TT, E])
        masked = c.sb("masked", [P, TT, E])
        best = c.sb("best", [P, TOPK, TT])
        rank, topped = c.sb("rank", [P, TT, E]), c.sb("topped", [P, TOPK, TT])
        chosen = c.sb("chosen", [P, TOPK, TT, E])
        counted = c.sb("counted", [P, TT, E], BF16)
        places = c.sb("places", [P, TOPK, TT, E])
        pos, over = c.sb("pos", [P, TOPK, TT]), c.sb("over", [P, TOPK, TT])
        base, where_to = c.sb("slot_base", [P, TOPK, TT]), c.sb("where_to", [P, TOPK, TT])
        where_from = c.sb("where_from", [P, TOPK, TT])
        scatter_at = c.sb("scatter_at", [P, TOPK, TT], U32)
        lead, second, total = c.sb("lead", [P, TT]), c.sb("second", [P, TT]), c.sb("total", [P, TT])

        loaded = {n: c.sem("c_ld_" + n) for n in ("wr", "wo")}
        wo_hi, wo_lo = c.sem("c_wohi"), c.sem("c_wolo")
        const_done, var_done, rstd_done, xn_done = (c.sem("c_" + n) for n in ("const", "var", "rstd", "xn"))
        turned, turned_out, logits_done = c.sem("c_turned"), c.sem("c_turnedout"), c.sem("c_logits")
        counted_done, pos_done, lead_done = c.sem("c_counted"), c.sem("c_pos"), c.sem("c_lead")
        second_done, at_done, scattered = c.sem("c_second"), c.sem("c_at"), c.sem("c_scattered")
        pe_done, hi_done, lo_done = c.sem("c_pe"), c.sem("c_hi"), c.sem("c_lo")

        WQ, WK, WV, QK, K = 0, 1, 2, 3, 4
        QK_B = K + H1 // 4
        VO = K + H1 + 1
        JOBS = VO + 2
        LATE = K + 4
        RING = 3
        half = KEYS // 2

        def head(j):
            return j - K - (j > QK_B)

        def slot(j):
            return g.psum[:, 2 * (j % RING):2 * (j % RING) + 2, :]

        def evacuation(j):
            ps = slot(j)
            flat = ps.rearrange("p b n -> p (b n)").rearrange("p (h n) -> p h n", n=P)
            if j == WQ:
                return flat, wqT, 1.0
            if j in (WK, WV):
                return flat[:, :, 0:C], (wkT, wvT)[j - WK], 1.0
            if j in (QK, QK_B):
                return ps[0:C].rearrange("p o (i d) -> p o i d", d=D), qk[:, j == QK_B], SCALE1
            if j >= VO:
                i = j - VO
                return ps[0:C].rearrange("p o (h d) -> p o h d", d=D), \
                    g.vo1.view("p (o h) d -> p o h d", o=2)[:, :, 4 * i:4 * i + 4, :], 1.0
            return ps[:, :, 0:half].rearrange("p n (b k) -> p n b k", k=M), \
                g.keys1[:, :, head(j), :].view("p (n b) k -> p n b k", n=2), 1.0

        def turned_ps(d):
            return g.psum[:, 6 + d, :]

        logits_ps = g.psum[:, 6, 0:TT * E].rearrange("p (t e) -> p t e", e=E)
        pos_ps = g.psum[:, 7, 0:TT * E].rearrange("p (t e) -> p t e", e=E)

        block = stack.enter_context(nc.Block())

        @block.sync
        def _(sp):
            sp.dma_start(wr[:], io["L0_ffn_Wr"]).then_inc(loaded["wr"], 16)
            sp.dma_start(wo[:], io["L1_xattn_Wo"].rearrange("(t p) d -> p t d", p=P)).then_inc(loaded["wo"], 16)
            sp.wait_ge(pe_done, WV + 1)
            for i in range(2):
                load_expert(sp, io, LAYER0_EXPERTS, i, g.expert_w[i], g.expert_w_loaded[i], (0, 1))
                load_expert(sp, io, LAYER0_EXPERTS, i, g.expert_w[i], g.expert_w2_loaded[i], (2,))
            sp.wait_ge(scattered, 16 * TT * TOPK)
            for i in range(2):
                move_slots(sp, g.expert_in, i, g.expert_rows[i], g.expert_rows_loaded[i], False)

        @block.gpsimd
        def _(pool):
            step = Chain(pool, Steps(const_done))
            step(pool.memset(earlier[:], 1.0))
            step(pool.affine_select(out=earlier[:], in_=earlier[:], compare_op=ALU.is_gt, fill=0.0,
                                    base=0, pattern=[[1, P]], channel_multiplier=-1))
            step(pool.memset(ones[:], 1.0))
            step(pool.iota(descending[:], pattern=[[0, TT], [-1, E]], base=E, channel_multiplier=0,
                           allow_small_or_imprecise_dtypes=True))
            pool.wait_ge(var_done, 1)
            pool.tensor_tensor(rstd[:], var_eps[:], g.minus_half[:], ALU.pow).then_inc(rstd_done, 1)
            pool.wait_ge(loaded["wo"], 16)
            pool.wait_ge(wo_hi, 1)
            pool.tensor_tensor(wo_s.lo, wo[:], f32(wo_s.hi), ALU.subtract).then_inc(wo_lo, 1)
            pool.wait_ge(g.expert_in_zeroed, 16 * E)
            pool.wait_ge(at_done, 1)
            for t in range(TT):
                for k in range(TOPK):
                    pool.indirect_dma_start(
                        out=g.expert_in, out_offset=bass.IndirectOffsetOnAxis(ap=scatter_at[:, k, t:t + 1], axis=0),
                        in_=xn[:, t, :], in_offset=None, bounds_check=SLOTS - 1,
                        oob_is_err=False).then_inc(scattered, 16)
            pool.wait_ge(scattered, 16 * TT * TOPK)

        @block.scalar
        def _(act):
            def evacuate(j):
                act.wait_ge(pe_done, j + 1)
                ps, to, factor = evacuation(j)
                act.activation(to.hi, ps, ACT.Copy, scale=factor).then_inc(hi_done, 1)

            for j in (WQ, WK, WV):
                evacuate(j)
            act.wait_ge(loaded["wo"], 16)
            act.copy(wo_s.hi, wo[:]).then_inc(wo_hi, 1)
            evacuate(QK)
            for d in range(2):
                act.wait_ge(turned, d + 1)
                act.copy(xnT[:, d * T // 2:(d + 1) * T // 2], turned_ps(d)).then_inc(turned_out, 1)
            for j in range(K, K + RING):
                evacuate(j)
            act.wait_ge(lead_done, 1)
            act.activation(second[:], lead[:], ACT.Exp).then_inc(second_done, 1)
            for j in range(K + RING, JOBS):
                evacuate(j)

        @block.vector
        def _(dve):
            step = Chain(dve, g.dve_steps)

            def evacuate(j):
                ps, to, factor = evacuation(j)
                dve.wait_ge(hi_done, j + 1)
                if factor == 1.0:
                    dve.tensor_tensor(to.lo, ps, f32(to.hi), ALU.subtract).then_inc(lo_done, 1)
                else:
                    for o in range(2):
                        last = dve.scalar_tensor_tensor(out=to.lo[:, o], in0=ps[:, o], scalar=factor,
                                                        in1=f32(to.hi[:, o]), op0=ALU.mult, op1=ALU.subtract)
                    last.then_inc(lo_done, 1)

            x2d = g.x[:].rearrange("p t d -> p (t d)")
            step(dve.scalar_tensor_tensor(out=x2d, in0=g.attended[:], scalar=g.gates[:, 0:1], in1=x2d,
                                          op0=ALU.mult, op1=ALU.add))
            layernorm_stats(dve, step, g.x, stats, moments)
            layernorm_variance(dve, moments, var_eps).then_inc(var_done, 1)
            evacuate(WQ)
            evacuate(WK)
            dve.wait_ge(rstd_done, 1)
            layernorm_apply(dve, g.x, moments, rstd, xn, xn_done)
            evacuate(WV)
            evacuate(QK)
            dve.wait_ge(logits_done, 1)
            step(dve.tensor_scalar(logits[:], logits_ps, 1e4, -1e4, ALU.min, ALU.max))
            dve.wait_ge(const_done, 4)
            for k in range(TOPK):
                scores = logits if k == 0 else masked
                step(dve.tensor_reduce(best[:, k, :], scores[:], AX.X, ALU.max))
                step(dve.tensor_tensor(rank[:], scores[:], best[:, k, :].unsqueeze(2).to_broadcast([P, TT, E]),
                                       ALU.is_equal))
                step(dve.tensor_tensor(rank[:], rank[:], descending[:], ALU.mult))
                step(dve.tensor_reduce(topped[:, k, :], rank[:], AX.X, ALU.max))
                step(dve.tensor_tensor(chosen[:, k], rank[:],
                                       topped[:, k, :].unsqueeze(2).to_broadcast([P, TT, E]), ALU.is_equal))
                if k == 0:
                    step(dve.scalar_tensor_tensor(
                        out=masked[:].rearrange("p t e -> p (t e)"),
                        in0=chosen[:, 0].rearrange("p t e -> p (t e)"), scalar=-4e4,
                        in1=logits[:].rearrange("p t e -> p (t e)"), op0=ALU.mult, op1=ALU.add))
            dve.tensor_tensor(counted[:], chosen[:, 0], chosen[:, 1], ALU.add).then_inc(counted_done, 1)
            dve.tensor_tensor(lead[:], best[:, 1, :], best[:, 0, :], ALU.subtract).then_inc(lead_done, 1)
            step(dve.tensor_scalar(base[:], topped[:], float(-CAP), float(CAP * E), ALU.mult, ALU.add))
            evacuate(K)
            dve.wait_ge(pos_done, 1)
            for k in range(TOPK):
                last = dve.tensor_tensor(places[:, k], pos_ps, chosen[:, k], ALU.mult)
            step(last)
            step(dve.tensor_reduce(pos[:], places[:], AX.X, ALU.add))
            step(dve.tensor_scalar(over[:], pos[:], float(CAP), None, ALU.is_ge))
            step(dve.tensor_tensor(where_to[:], pos[:], base[:], ALU.add))
            over2, to2 = (v[:].rearrange("p k t -> p (k t)") for v in (over, where_to))
            step(dve.scalar_tensor_tensor(out=to2, in0=over2, scalar=float(1 << 16), in1=to2,
                                          op0=ALU.mult, op1=ALU.add))
            dve.tensor_copy(scatter_at[:], where_to[:]).then_inc(at_done, 1)
            for j in range(K + 1, LATE):
                evacuate(j)
            step(dve.tensor_scalar(where_from[:], pos[:], float(CAP - 1), None, ALU.min))
            step(dve.tensor_tensor(where_from[:], where_from[:], base[:], ALU.add))
            step(dve.tensor_copy(g.gather_at[:], where_from[:]))
            dve.wait_ge(second_done, 1)
            step(dve.tensor_scalar(total[:], second[:], 1.0, 1e-12, ALU.add, ALU.add))
            step(dve.reciprocal(g.token_weights[:, 0, :], total[:]))
            step(dve.tensor_tensor(g.token_weights[:, 1, :], second[:], g.token_weights[:, 0, :], ALU.mult))
            step(dve.tensor_scalar(over[:], over[:], -1.0, 1.0, ALU.mult, ALU.add))
            step(dve.tensor_tensor(g.token_weights[:], g.token_weights[:], over[:], ALU.mult))
            step(dve.tensor_scalar(g.token_weights[:], g.token_weights[:], g.gates[:, 2:3], None, ALU.mult))
            for j in range(LATE, JOBS):
                evacuate(j)

        @block.tensor
        def _(pe):
            def job(j):
                ps = slot(j)
                wait(pe, lo_done, j - RING + 1)
                if j in (WQ, WK, WV):
                    pe.wait_ge(g.weights1_loaded[j], 32)
                    rows = (D, C, C)[j]
                    flat = ps.rearrange("p b n -> p (b n)")
                    for i in range(H1 // 2):
                        w = g.weights1[j][i * P // F]
                        at = i * P % F
                        last = pe.transpose(flat[:, i * P:i * P + rows], w[0:rows, at:at + P],
                                            g.ident[0:rows, 0:rows])
                elif j in (QK, QK_B) or j >= VO:
                    if j >= VO:
                        pe.wait_ge(lo_done, WV + 1)
                        pe.wait_ge(wo_lo, 1)
                    else:
                        pe.wait_ge(lo_done, WK + 1)
                    lhs, rhs = (wkT, wqT) if j < VO else (wvT, wo_s)
                    part = j in (QK_B, VO + 1)
                    for i in range(H1 // 4):
                        for odd in range(2):
                            at, pair = slice(odd * DH1, (odd + 1) * DH1), part * (H1 // 4) + i
                            last = matmul3(pe, ps[0:C, odd, i * D:(i + 1) * D], lhs[at, pair, :], rhs[at, pair, :])
                else:
                    h = head(j)
                    pe.wait_ge(lo_done, (QK if h < H1 // 2 else QK_B) + 1)
                    for b in range(2):
                        last = matmul3(pe, ps[:, b, 0:half], qk[:, h // 8, h % 2, h % 8 // 2, :],
                                       g.ctxT[:, b * half:(b + 1) * half])
                last.then_inc(pe_done, 1)

            job(WQ)
            job(WK)
            job(WV)
            job(QK)
            for t in range(TT):
                pe.wait_ge(xn_done, t + 1)
                d, at = t // (TT // 2), t % (TT // 2) * P
                last = pe.transpose(turned_ps(d)[:, at:at + P], xn[:, t, :], g.ident[:])
                if t % (TT // 2) == TT // 2 - 1:
                    last.then_inc(turned, 1)
            pe.wait_ge(loaded["wr"], 16)
            for t in range(TT):
                if t % (TT // 2) == 0:
                    pe.wait_ge(turned_out, t // (TT // 2) + 1)
                last = pe.matmul(logits_ps[:, t, :], xnT[:, t * P:(t + 1) * P], wr[:], start=True, stop=True)
            last.then_inc(logits_done, 1)
            for j in range(K, K + RING):
                job(j)
            pe.wait_ge(counted_done, 1)
            last = pe.matmul(pos_ps, earlier[:], counted[:], start=True, stop=False)
            for t in range(TT - 1):
                last = pe.matmul(pos_ps[:, t + 1:TT, :], ones[:],
                                 counted[:, t, :].unsqueeze(1).to_broadcast([P, TT - 1 - t, E]),
                                 start=False, stop=t == TT - 2)
            last.then_inc(pos_done, 1)
            for j in range(K + RING, JOBS):
                job(j)


def experts0(core, g, io):
    nc = core.nc
    with ExitStack() as stack:
        c = core.scope(stack)
        TILES, NT, FIRST, LIKE = SLOT_TILES, NSLOT, FIRST_SLOTS, LIKE_SLOTS
        parts = [[c.split(f"ews{i}_{n}", [P, F]) for n in range(3)] for i in range(2)]
        tokensT = [c.split(f"etokT{i}", [D, CAP]) for i in range(2)]
        silu = [c.sb(f"esilu{i}", [P, CAP]) for i in range(2)]
        hidden = [c.sb(f"ehidden{i}", [P, CAP]) for i in range(2)]
        hid = [c.split(f"ehid{i}", [P, FT, CAP]) for i in range(2)]
        down_out = c.sb("edownT", [D, CAP])
        result = [c.sb(f"eresult{i}", [P, NT, D]) for i in range(2)]

        raw, w_loaded, w2_loaded = g.expert_w, g.expert_w_loaded, g.expert_w2_loaded
        rows, r_loaded = g.expert_rows, g.expert_rows_loaded
        up_w_hi, up_w_lo, down_w_hi, down_w_lo = (c.sem("d_" + n) for n in ("uwhi", "uwlo", "dwhi", "dwlo"))
        stored = g.experts_stored
        turned, turned_hi, turned_lo = c.sem("d_turned"), c.sem("d_turnedhi"), c.sem("d_turnedlo")
        up_done, silu_done, mult_done = c.sem("d_up"), c.sem("d_silu"), c.sem("d_mult")
        hid_hi, hid_lo = c.sem("d_hidhi"), c.sem("d_hidlo")
        down_done, result_done = c.sem("d_down"), c.sem("d_result")
        down_copied, back_done = c.sem("d_downout"), c.sem("d_back")

        def turns(step, engine):
            for i in range(2):
                step(0, i)
            with engine.Fori(1, E // 2 - 1) as turn:
                for i in range(2):
                    step(turn, i)
            step(E // 2 - 1, 0)
            step(E // 2 - 1, 1, ahead=False)

        def up_bank(f, which):
            return g.psum[:, 2 * (f % 2) + which, 0:CAP]

        def down_ps(i):
            return g.psum[:, 5 + i % 2, 0:CAP]

        turned_ps = g.psum[:, 4, 0:CAP]
        back_ps = g.psum[:, 7, 0:NT * D].rearrange("p (s d) -> p s d", d=D)

        def before(turn, i):
            return isinstance(turn, int) and turn * 2 + i < 0

        block = stack.enter_context(nc.Block())

        @block.sync
        def _(sp):
            def step(turn, i, ahead=True):
                e = turn * 2 + i
                if isinstance(turn, int) and turn == 0:
                    return
                sp.wait_ge(up_w_lo, e * 2 - 2)
                load_expert(sp, io, LAYER0_EXPERTS, e, raw[i], w_loaded[i], (0, 1))
                sp.wait_ge(turned, e - 1)
                move_slots(sp, g.expert_in, e, rows[i], r_loaded[i], False)
                sp.wait_ge(down_w_lo, e - 1)
                load_expert(sp, io, LAYER0_EXPERTS, e, raw[i], w2_loaded[i], (2,))

            turns(step, sp)

        @block.gpsimd
        def _(pool):
            def low(i, n):
                i = i % 2
                return pool.tensor_tensor(parts[i][n].lo, raw[i][n][:], f32(parts[i][n].hi), ALU.subtract)

            def up_low(turn, i, n):
                e = turn * 2 + i
                wait(pool, up_done, (e - 1) * FT)
                pool.wait_ge(up_w_hi, e * 2 + n + 1)
                low(i, n).then_inc(up_w_lo, 1)

            def step(turn, i, ahead=True):
                e = turn * 2 + i
                if ahead:
                    for n in range(2):
                        up_low(turn, i + 1, n)
                wait(pool, down_done, e - 1)
                pool.wait_ge(down_w_hi, e + 1)
                low(i, 2).then_inc(down_w_lo, 1)

            up_low(0, 0, 0)
            pool.wait_ge(up_w_lo, 2)
            turns(step, pool)

        @block.scalar
        def _(act):
            def split_weight(turn, i, n):
                e = turn * 2 + i
                act.wait_ge((w_loaded, w2_loaded)[n == 2][i % 2], (turn + (i // 2)) * (16 if n == 2 else 32)
                            + (16 if n == 2 else 32))
                if n == 0:
                    wait(act, up_done, (e - 1) * FT)
                if n == 2:
                    wait(act, down_done, e - 1)
                act.copy(parts[i % 2][n].hi, raw[i % 2][n][:]).then_inc(down_w_hi if n == 2 else up_w_hi, 1)

            def tokens_hi(turn, i):
                act.wait_ge(turned, turn * 2 + i + 1)
                act.copy(tokensT[i % 2].hi, turned_ps).then_inc(turned_hi, 1)

            def hidden_high(turn, i, f):
                if before(turn, i):
                    return
                e = turn * 2 + i
                if f == 0:
                    wait(act, down_done, e - 1)
                act.wait_ge(mult_done, e * FT + f + 1)
                act.copy(hid[i % 2].hi[:, f, :], hidden[f % 2][:]).then_inc(hid_hi, 1)

            def store(turn, i):
                if before(turn, i):
                    return
                act.wait_ge(result_done, turn * 2 + i + 2)
                move_slots(act, g.expert_out, turn * 2 + i, result[i % 2], stored[i % 2], True)

            def step(turn, i, ahead=True):
                e = turn * 2 + i
                for f in range(FT):
                    n = e * FT + f
                    if f == 0:
                        hidden_high(turn, i - 1, FT - 1)
                        if ahead:
                            split_weight(turn, i + 1, 0)
                    act.wait_ge(up_done, n + 1)
                    wait(act, mult_done, n - 1)
                    act.activation(silu[f % 2][:], up_bank(f, 0), ACT.Silu).then_inc(silu_done, 1)
                    if f == 0:
                        split_weight(turn, i, 2)
                    else:
                        hidden_high(turn, i, f - 1)
                    if f == 1 and ahead:
                        split_weight(turn, i + 1, 1)
                    if f == 1 and ahead:
                        tokens_hi(turn, i + 1)
                    if f == 3:
                        store(turn, i - 2)

            for n in range(2):
                split_weight(0, 0, n)
            tokens_hi(0, 0)
            turns(step, act)
            hidden_high(E // 2, -1, FT - 1)
            for i in range(2):
                store(E // 2, i - 2)

        @block.vector
        def _(dve):
            def tokens_lo(turn, i):
                dve.wait_ge(turned_hi, turn * 2 + i + 1)
                dve.tensor_tensor(tokensT[i % 2].lo, turned_ps, f32(tokensT[i % 2].hi),
                                  ALU.subtract).then_inc(turned_lo, 1)

            def copy_down(turn, i):
                if before(turn, i):
                    return
                dve.wait_ge(down_done, turn * 2 + i + 1)
                dve.tensor_copy(down_out[:], down_ps(i)).then_inc(down_copied, 1)

            def copy_result(turn, i):
                if before(turn, i):
                    return
                e = turn * 2 + i
                dve.wait_ge(back_done, e + 1)
                wait(dve, stored[i % 2], CREDIT + (turn + (i // 2)) * 32)
                dve.tensor_copy(result[i % 2][0:FIRST, 0, :], back_ps[0:FIRST, 0, :])
                dve.tensor_copy(result[i % 2][0:LIKE, 1:NT, :], back_ps[0:LIKE, 1:NT, :]).then_inc(result_done, 1)

            def hidden_low(turn, i, f):
                if before(turn, i):
                    return
                dve.wait_ge(hid_hi, (turn * 2 + i) * FT + f + 1)
                dve.tensor_tensor(hid[i % 2].lo[:, f, :], hidden[f % 2][:], f32(hid[i % 2].hi[:, f, :]),
                                  ALU.subtract).then_inc(hid_lo, 1)

            def step(turn, i, ahead=True):
                e = turn * 2 + i
                for f in range(FT):
                    n = e * FT + f
                    if f == 0:
                        copy_down(turn, i - 2)
                        hidden_low(turn, i - 1, FT - 1)
                    if f == 2:
                        copy_result(turn, i - 2)
                    dve.wait_ge(silu_done, n + 1)
                    wait(dve, hid_lo, n - 1)
                    dve.tensor_tensor(hidden[f % 2][:], silu[f % 2][:], up_bank(f, 1), ALU.mult).then_inc(mult_done, 1)
                    if f == 2 and ahead:
                        tokens_lo(turn, i + 1)
                    if f > 0:
                        hidden_low(turn, i, f - 1)

            for i in range(2):
                dve.sem_inc(stored[i], CREDIT)
            dve.sem_inc(down_copied, 1)
            dve.wait_ge(w_loaded[0], 32)
            dve.wait_ge(up_w_hi, 2)
            dve.tensor_tensor(parts[0][1].lo, raw[0][1][:], f32(parts[0][1].hi), ALU.subtract).then_inc(up_w_lo, 1)
            tokens_lo(0, 0)
            turns(step, dve)
            hidden_low(E // 2, -1, FT - 1)
            for i in range(2):
                copy_down(E // 2, i - 2)
                copy_result(E // 2, i - 2)

        @block.tensor
        def _(pe):
            def transposes(turn, i):
                e = turn * 2 + i
                pe.wait_ge(r_loaded[i % 2], (turn + i // 2) * 32 + 32)
                wait(pe, turned_lo, e)
                wait(pe, up_done, (e - 1) * FT)
                for s, (a, b) in enumerate(TILES):
                    last = pe.transpose(turned_ps[:, a:b], rows[i % 2][0:b - a, s, :], g.ident[0:b - a, 0:b - a])
                last.then_inc(turned, 1)

            def down(turn, i, f):
                if before(turn, i):
                    return
                e = turn * 2 + i
                if f == 0:
                    pe.wait_ge(down_w_lo, e + 1)
                    wait(pe, down_copied, e)
                pe.wait_ge(hid_lo, e * FT + f + 1)
                last = matmul3(pe, down_ps(i), parts[i % 2][2][:, f * D:(f + 1) * D], hid[i % 2][:, f, :],
                               start=f == 0, stop=f == FT - 1)
                if f == FT - 1:
                    last.then_inc(down_done, 1)

            def back(turn, i):
                if before(turn, i):
                    return
                e = turn * 2 + i
                pe.wait_ge(down_copied, e + 2)
                wait(pe, result_done, e + 1)
                for s, (a, b) in enumerate(TILES):
                    last = pe.transpose(back_ps[0:b - a, s, :], down_out[:, a:b], g.ident[:])
                last.then_inc(back_done, 1)

            def step(turn, i, ahead=True):
                e = turn * 2 + i
                pe.wait_ge(up_w_lo, e * 2 + 2)
                pe.wait_ge(turned_lo, e + 1)
                for f in range(FT):
                    n = e * FT + f
                    wait(pe, mult_done, n - 1)
                    for which in range(2):
                        last = matmul3(pe, up_bank(f, which), parts[i][which][:, f * P:(f + 1) * P], tokensT[i])
                    last.then_inc(up_done, 1)
                    down(turn, i - 1, f)
                    if f == 0 and ahead:
                        transposes(turn, i + 1)
                    if f == 1:
                        back(turn, i - 2)

            pe.sem_inc(result_done, 1)
            transposes(0, 0)
            turns(step, pe)
            for f in range(FT):
                down(E // 2, -1, f)
            for i in range(2):
                back(E // 2, i - 2)


def combine(core, g, io):
    nc = core.nc
    with ExitStack() as stack:
        c = core.scope(stack)
        gathered = c.sb("gathered", [P, TT, TOPK, D])
        staged = [c.sb(f"vstage{i}", [M, H1 // 2, D]) for i in range(4)]
        xn = c.sb("xn1", [P, TT, D])
        stats, moments = g.stats, g.moments
        var_eps, rstd = c.sb("ln_var2", [P, TT]), c.sb("ln_rstd2", [P, TT])
        gated_bias = c.sb("gated_bias", [P, D])

        got = [c.sem(f"v_gathered{t}") for t in range(TT)]
        pe_done, copied = c.sem("v_pe"), c.sem("v_copied")
        stored = [c.sem(f"v_stored{i}") for i in range(4)]
        var_done, rstd_done, bias_done, pad_done = (c.sem("v_" + n) for n in ("var", "rstd", "bias", "pad"))
        xn_done, turned, hi_done = c.sem("v_xn"), c.sem("v_turned"), c.sem("v_hi")

        JOBS = 2 * B
        LOAD_AFTER = (11, 13)
        RING = 3

        def slot(n):
            return g.psum[:, 2 * (n % RING):2 * (n % RING) + 2, :].rearrange("p b n -> p (b n)")

        def turned_ps(d):
            return g.psum[:, 6 + d, :]

        def half(d):
            return slice(d * T // 2, (d + 1) * T // 2)

        block = stack.enter_context(nc.Block())

        @block.gpsimd
        def _(pool):
            for i in range(2):
                pool.memset(g.raw_values[i][:, NT1 - 1, :], 0.0).then_inc(pad_done, 1)
            for i in range(2):
                pool.wait_ge(g.experts_stored[i], CREDIT + 32 * (E // 2))
            for t in range(TT):
                for k in range(TOPK):
                    pool.indirect_dma_start(
                        out=gathered[:, t, k, :], out_offset=None, in_=g.expert_out,
                        in_offset=bass.IndirectOffsetOnAxis(ap=g.gather_at[:, k, t:t + 1], axis=0)
                    ).then_inc(got[t], 16)
            pool.wait_ge(var_done, 1)
            pool.tensor_tensor(rstd[:], var_eps[:], g.minus_half[:], ALU.pow).then_inc(rstd_done, 1)
            pool.wait_ge(bias_done, 1)
            for t in range(TT):
                pool.wait_ge(xn_done, t + 1)
                pool.tensor_tensor(g.x[:, t, :], g.x[:, t, :], gated_bias[:], ALU.add)

        @block.sync
        def _(sp):
            sp.wait_ge(pad_done, 2)
            for n in range(JOBS):
                b, odd = n // 2, n % 2
                sp.wait_ge(copied, n + 1)
                sp.dma_start(g.values1[b].rearrange("(h o k) d -> o k h d", o=2, k=M)[odd],
                             staged[n % 4][:]).then_inc(stored[n % 4], 16)
                if n in LOAD_AFTER:
                    i = LOAD_AFTER.index(n)
                    for j in range(2):
                        sp.wait_ge(stored[2 * i + j], 16)
                    load_values(sp, g, i, i)
            for i in range(2):
                load_expert(sp, io, LAYER1_EXPERTS, i, g.expert_w[i], g.expert1_w_loaded[i])
            for i in range(4):
                sp.wait_ge(stored[i], 16 * JOBS // 4)

        @block.scalar
        def _(act):
            for n in range(JOBS):
                act.wait_ge(pe_done, n + 1)
                wait(act, stored[n % 4], 16 * (n // 4))
                act.copy(staged[n % 4][:], slot(n)[0:M].rearrange("p (h d) -> p h d", d=D)).then_inc(copied, 1)
            for d in range(2):
                act.wait_ge(turned, d + 1)
                act.copy(g.xn1T.hi[:, half(d)], turned_ps(d)).then_inc(hi_done, 1)

        @block.vector
        def _(dve):
            step = Chain(dve, g.dve_steps)
            dve.tensor_scalar(gated_bias[:], g.bias1[:], g.gates[:, 1:2], None, ALU.mult).then_inc(bias_done, 1)
            for t in range(TT):
                dve.wait_ge(got[t], 16 * TOPK)
                for k in range(TOPK):
                    step(dve.scalar_tensor_tensor(out=g.x[:, t, :], in0=gathered[:, t, k, :],
                                                  scalar=g.token_weights[:, k, t:t + 1], in1=g.x[:, t, :],
                                                  op0=ALU.mult, op1=ALU.add))
                step(dve.bn_stats(stats[:, t, :], g.x[:, t, :]))
                last = dve.bn_aggr(moments[:, t, :], stats[:, t, :])
            step(last)
            layernorm_variance(dve, moments, var_eps).then_inc(var_done, 1)
            dve.wait_ge(rstd_done, 1)
            layernorm_apply(dve, g.x, moments, rstd, xn, xn_done)
            for d in range(2):
                dve.wait_ge(hi_done, d + 1)
                dve.tensor_tensor(g.xn1T.lo[:, half(d)], turned_ps(d), f32(g.xn1T.hi[:, half(d)]), ALU.subtract)

        @block.tensor
        def _(pe):
            for n in range(JOBS):
                if n >= RING:
                    pe.wait_ge(copied, n - RING + 1)
                b, odd = n // 2, n % 2
                for i in range(2):
                    first = odd * (H1 // 2) + 4 * i
                    last = matmul3(pe, slot(n)[0:M, i * BANK:(i + 1) * BANK], g.ctxT[:, b * M:(b + 1) * M],
                                   g.vo1[:, first:first + 4, :].view("p h d -> p (h d)"))
                last.then_inc(pe_done, 1)
            for t in range(TT):
                pe.wait_ge(xn_done, t + 1)
                d, at = t // (TT // 2), t % (TT // 2) * P
                last = pe.transpose(turned_ps(d)[:, at:at + P], xn[:, t, :], g.ident[:])
                if t % (TT // 2) == TT // 2 - 1:
                    last.then_inc(turned, 1)


N1 = H1 * M
NT1 = -(-N1 // P)
LAST1 = N1 - (NT1 - 1) * P


def load_values(sp, g, b, i):
    rows = g.values1.rearrange("b n d -> (b n) d")[bass.ds(b * N1, N1), :]
    sp.dma_start(g.raw_values[i][:, 0:NT1 - 1, :],
                 rows[0:(NT1 - 1) * P, :].rearrange("(t p) d -> p t d", p=P)).then_inc(g.values_loaded[i], 16)
    sp.dma_start(g.raw_values[i][0:LAST1, NT1 - 1, :], rows[(NT1 - 1) * P:N1, :]).then_inc(g.values_loaded[i], 16)


def attention1(core, g, io):
    nc = core.nc
    with ExitStack() as stack:
        c = core.scope(stack)
        NT, LAST = NT1, LAST1
        CHUNKS = [(0, 4), (4, 8), (8, NT)]
        xnT, raw_values, values_loaded = g.xn1T, g.raw_values, g.values_loaded
        pad_done = c.sem("e_pad")
        queries = [c.split(f"queries1_{i}", [D, P]) for i in range(2)]
        values = [c.split(f"values1_{i}", [P, NT, D]) for i in range(2)]
        SHIFTED, BIASED = 12, 4
        maximum, neg_max = c.sb("max1", [P, SHIFTED]), c.sb("neg_max1", [P, BIASED])
        den, rden = c.sb("den1", [P, H1]), c.sb("rden1", [P, H1])
        weights = [c.sb(f"weights1_{i}", [P, NT * P]) for i in range(2)]
        by_head = [w[:, 0:N1].rearrange("p (h k) -> p h k", k=M) for w in weights]
        weightsT = c.split("turned1", [P, NT * P])

        queries_ready, v_hi, v_lo = c.sem("e_q"), c.sem("e_vhi"), c.sem("e_vlo")
        scores_done, max_done, sub_done, exp_done = (c.sem("e_" + n) for n in ("scores", "max", "sub", "exp"))
        den_done, rden_done, norm_done = c.sem("e_den"), c.sem("e_rden"), c.sem("e_norm")
        turned, hi_done, lo_done = c.sem("e_turned"), c.sem("e_hi"), c.sem("e_lo")
        pv_done, x_done = c.sem("e_pv"), c.sem("e_x")

        GROUPS = [(0, 0, 6), (1, 6, SHIFTED), (2, SHIFTED, H1)]
        NC = len(CHUNKS)

        shifted_ps = g.psum[:, 0:2, 0:6 * M].rearrange("p b (h k) -> p b h k", k=M)
        biased_ps = g.psum[:, 2, 0:BIASED * M].rearrange("p (h k) -> p h k", k=M)

        def chunk(p):
            a, z = CHUNKS[p]
            return g.psum[:, 3 + p, 0:(z - a) * P]

        def output(i):
            return g.psum[:, 6 + i, 0:D]

        def turns(step, engine):
            for i in range(2):
                step(0, i, True, False)
            with engine.Fori(1, B // 2) as turn:
                for i in range(2):
                    step(turn, i, True, True)
            for i in range(2):
                step(B // 2, i, False, True)

        def middle(turn, i, new):
            return (new or i == 0) and not (isinstance(turn, int) and turn + i == 0)

        def buffer_before(i):
            return (i - 1) % 2

        block = stack.enter_context(nc.Block())

        @block.sync
        def _(sp):
            def step(turn, i, new, old):
                if new and old:
                    b = turn * 2 + i
                    sp.wait_ge(v_lo, b - 1)
                    load_values(sp, g, b, i)

            turns(step, sp)

        @block.gpsimd
        def _(pool):
            for i in range(2):
                pool.memset(weights[i][:, N1:NT * P], 0.0).then_inc(pad_done, 1)

            def step(turn, i, new, old):
                if not middle(turn, i, new):
                    return
                b = turn * 2 + i - 1
                j = buffer_before(i)
                pool.wait_ge(rden_done, b + 1)
                pool.tensor_tensor(by_head[j], by_head[j], rden[:].unsqueeze(2).to_broadcast([P, H1, M]),
                                   ALU.mult).then_inc(norm_done, 1)
                pool.wait_ge(v_hi, b + 1)
                pool.tensor_tensor(values[j].lo, raw_values[j][:], f32(values[j].hi), ALU.subtract).then_inc(v_lo, 1)

            turns(step, pool)

        @block.scalar
        def _(act):
            def step(turn, i, new, old):
                b = turn * 2 + i
                if old:
                    wait(act, pv_done, b - 1)
                    for p, (a, z) in enumerate(CHUNKS):
                        act.wait_ge(turned, (b - 2) * NC + p + 1)
                        act.copy(weightsT.hi[:, a * P:z * P], chunk(p)).then_inc(hi_done, 1)
                if middle(turn, i, new):
                    j = buffer_before(i)
                    act.wait_ge(values_loaded[j], (turn + i) * 32)
                    act.copy(values[j].hi, raw_values[j][:]).then_inc(v_hi, 1)
                if new:
                    act.wait_ge(max_done, b + 1)
                    wait(act, turned, (b - 1) * NC)
                    for k in range(BIASED):
                        h = SHIFTED + k
                        last = act.activation(by_head[i][:, h, :], g.psum[:, 2, k * M:(k + 1) * M], ACT.Exp,
                                              bias=neg_max[:, k:k + 1], accum_out=den[:, h:h + 1])
                    last.then_inc(exp_done, 1)
                    act.wait_ge(sub_done, b + 1)
                    act.activation(by_head[i][:, 0:SHIFTED, :], by_head[i][:, 0:SHIFTED, :], ACT.Exp).then_inc(exp_done, 1)

            act.sem_inc(pv_done, 1)
            turns(step, act)

        @block.vector
        def _(dve):
            def normalise(b, i):
                dve.wait_ge(exp_done, b * 2 + 2)
                dve.tensor_reduce(den[:, 0:SHIFTED], by_head[i % 2][:, 0:SHIFTED, :], AX.X, ALU.add).then_inc(den_done, 1)
                dve.wait_ge(den_done, b + 1)
                wait(dve, norm_done, b)
                dve.reciprocal(rden[:], den[:]).then_inc(rden_done, 1)

            def step(turn, i, new, old):
                b = turn * 2 + i
                if new and not isinstance(turn, int):
                    wait(dve, scores_done, b - 1)
                    at = bass.ds(b * P, P)
                    dve.tensor_copy(queries[i].hi, f32(xnT.hi[:, at])).then_inc(queries_ready, 1)
                    dve.tensor_copy(queries[i].lo, f32(xnT.lo[:, at])).then_inc(queries_ready, 1)
                if middle(turn, i, new):
                    normalise(b - 1, i - 1)
                if old:
                    for p, (a, z) in enumerate(CHUNKS):
                        dve.wait_ge(hi_done, (b - 2) * NC + p + 1)
                        dve.tensor_tensor(weightsT.lo[:, a * P:z * P], chunk(p), f32(weightsT.hi[:, a * P:z * P]),
                                          ALU.subtract).then_inc(lo_done, 1)
                if new:
                    dve.wait_ge(scores_done, b + 1)
                    dve.tensor_reduce(maximum[:].rearrange("p (b h) -> p b h", b=2), shifted_ps, AX.X, ALU.max)
                    dve.tensor_reduce(neg_max[:], biased_ps, AX.X, ALU.max, negate=True).then_inc(max_done, 1)
                    dve.wait_ge(max_done, b + 1)
                    wait(dve, turned, (b - 1) * NC)
                    dve.tensor_tensor(
                        by_head[i][:, 0:SHIFTED, :].rearrange("p (b h) k -> p b h k", b=2), shifted_ps,
                        maximum[:].rearrange("p (b h) -> p b h", b=2).unsqueeze(3)
                        .to_broadcast([P, 2, SHIFTED // 2, M]), ALU.subtract).then_inc(sub_done, 1)
                if old and not new:
                    dve.wait_ge(x_done, b)
                    layernorm_stats(dve, Chain(dve, g.dve_steps), g.x, g.stats, g.moments,
                                    range(B - 2) if i == 0 else (B - 2,))
                if old:
                    dve.wait_ge(pv_done, b)
                    rows = g.x[:, bass.ds(b - 2, 1), :].rearrange("p o d -> p (o d)")
                    dve.scalar_tensor_tensor(out=rows, in0=output(i), scalar=g.gates[:, 1:2], in1=rows,
                                             op0=ALU.mult, op1=ALU.add).then_inc(x_done, 1)

            turns(step, dve)

        @block.tensor
        def _(pe):
            def step(turn, i, new, old):
                b = turn * 2 + i
                if old:
                    pe.wait_ge(norm_done, b - 1)
                    for p, (a, z) in enumerate(CHUNKS):
                        for t in range(a, z):
                            last = pe.transpose(chunk(p)[:, (t - a) * P:(t - a + 1) * P],
                                                weights[i][:, t * P:(t + 1) * P], g.ident[:])
                        last.then_inc(turned, 1)
                if new:
                    q = queries[i]
                    if isinstance(turn, int):
                        q = xnT[:, b * P:(b + 1) * P]
                    else:
                        pe.wait_ge(queries_ready, b * 2 - 2)
                    wait(pe, sub_done, b)
                    for bank, a, z in GROUPS:
                        if bank == 2:
                            wait(pe, exp_done, b * 2 - 1)
                        last = matmul3(pe, g.psum[:, bank, 0:(z - a) * M], q,
                                       g.keys1[:, bass.ds(b, 1), a:z, :].view("p o h k -> p (o h k)"))
                    last.then_inc(scores_done, 1)
                if old:
                    pe.wait_ge(v_lo, b - 1)
                    wait(pe, x_done, b - 1)
                    for p, (a, z) in enumerate(CHUNKS):
                        pe.wait_ge(lo_done, (b - 2) * NC + p + 1)
                        for t in range(a, z):
                            rows = P if t < NT - 1 else LAST
                            last = matmul3(pe, output(i), weightsT[0:rows, t * P:(t + 1) * P],
                                           values[i][0:rows, t, :], start=t == 0, stop=t == NT - 1)
                    last.then_inc(pv_done, 1)

            pe.sem_inc(x_done, 2)
            pe.wait_ge(pad_done, 2)
            turns(step, pe)


def experts1(core, g, io, out):
    nc = core.nc
    with ExitStack() as stack:
        c = core.scope(stack)
        HALF = T // 2
        HT = TT // 2
        UNITS = FT * 2
        raw, w_loaded = g.expert_w, g.expert1_w_loaded
        xnT = c.split("xn2T", [D, T])
        routers_raw, routers = c.sb("routers", [D, P]), c.split("routers_s", [D, P])
        logitsT = c.sb("logitsT", [2 * E, T])
        top, probs = c.sb("top", [P, TT, 2]), c.sb("probs", [P, TT, 2, E])
        sums, rsums = c.sb("sums", [P, TT, 2]), c.sb("rsums", [P, TT, 2])
        both, bsum, rbsum = c.sb("both", [P, TT, E]), c.sb("bsum", [P, TT]), c.sb("rbsum", [P, TT])
        mix = c.sb("mix", [P, E, TT])
        mixT = c.sb("mixT", [E * TT, P])
        parts = [[c.split(f"fws{i}_{n}", [P, F]) for n in range(3)] for i in range(2)]
        silu = [c.sb(f"fsilu{i}", [P, HALF]) for i in range(2)]
        hidden = [c.sb(f"fhidden{i}", [P, HALF]) for i in range(2)]
        hid = [c.split(f"fhid{i}", [P, FT, T]) for i in range(2)]
        spread = [c.sb(f"spread{i}", [P, T]) for i in range(2)]
        mixed = [c.sb(f"mixed{i}", [D, HALF]) for i in range(2)]
        total = c.sb("total_out", [D, T])

        up_w_hi, up_w_lo, down_w_hi, down_w_lo = (c.sem("f_" + n) for n in ("uwhi", "uwlo", "dwhi", "dwlo"))
        zeroed, logitsT_done, logitsT_out = c.sem("f_zero"), c.sem("f_logitsT"), c.sem("f_logitsTout")
        logits_done, shifted, exp_done = (c.sem("f_" + n) for n in ("logits", "shifted", "exp"))
        mix_done, mix_turned, mixT_done, mix_stored = (c.sem("f_" + n) for n in ("mix", "mixturned", "mixT", "mixst"))
        spread_loaded = [c.sem(f"f_spread{i}") for i in range(2)]
        up_done, silu_done, mult_done = c.sem("f_up"), c.sem("f_silu"), c.sem("f_mult")
        hid_hi, hid_lo = c.sem("f_hidhi"), c.sem("f_hidlo")
        down_done, mixed_done, sum_done = c.sem("f_down"), c.sem("f_mixed"), c.sem("f_sum")
        back_done, x_done, stored = c.sem("f_back"), c.sem("f_x"), c.sem("f_stored")

        def up_bank(u, which):
            return g.psum[:, 2 * ((u + (u > 1)) % 3) + which, :]

        def down_bank(d):
            return g.psum[:, 6 + d, :]

        def half(d):
            return slice(d * HALF, (d + 1) * HALF)

        logits_ps = g.psum[:, 7, 0:TT * 2 * E].rearrange("p (t r e) -> p t r e", r=2, e=E)
        mixT_ps = g.psum[0:E * TT, 6, 0:P]

        def logitsT_ps(d):
            return g.psum[0:2 * E, 6 + d, :]

        def weight_high(act, i, n):
            return act.copy(parts[i % 2][n].hi, raw[i % 2][n][:])

        def weight_low(eng, i, n):
            return eng.tensor_tensor(parts[i % 2][n].lo, raw[i % 2][n][:], f32(parts[i % 2][n].hi),
                                      ALU.subtract)

        xn, stats, moments = c.sb("xn2", [P, TT, D]), g.stats, g.moments
        var_eps, rstd = c.sb("ln_var3", [P, TT]), c.sb("ln_rstd3", [P, TT])
        r_loaded, var_done, rstd_done, r_hi, r_lo = (c.sem("f_" + n) for n in ("rld", "var", "rstd", "rhi", "rlo"))
        xn_done, turned, x_hi, x_lo = (c.sem("f_" + n) for n in ("xn", "turned", "xhi", "xlo"))

        def turned_ps(d):
            return g.psum[:, d, :]

        def turns(step, engine):
            for i in range(2):
                step(0, i)
            with engine.Fori(1, E // 2 - 1) as turn:
                for i in range(2):
                    step(turn, i)
            for i in range(2):
                step(E // 2 - 1, i)
            step(E // 2, 0, drain=True)

        def first(turn, i):
            return isinstance(turn, int) and turn == 0 and i == 0

        def ahead(turn, i):
            return not (isinstance(turn, int) and turn * 2 + i + 1 >= E)

        block = stack.enter_context(nc.Block())

        @block.sync
        def _(sp):
            def load_spread(e, i):
                row = g.mix[bass.ds(e, 1), :].rearrange("o t -> (o t)")
                sp.dma_start(spread[i][:], row.partition_broadcast(P)).then_inc(spread_loaded[i], 16)

            def step(turn, i, drain=False):
                if drain:
                    return
                e = turn * 2 + i
                if isinstance(turn, int) and turn == 0:
                    if i == 0:
                        sp.wait_ge(mixT_done, 1)
                        sp.dma_start(g.mix.rearrange("e (t p) -> (e t) p", p=P), mixT[:]).then_inc(mix_stored, 16)
                        sp.wait_ge(mix_stored, 16)
                    load_spread(e, i)
                    return
                sp.wait_ge(up_w_lo, e - 1)
                sp.wait_ge(down_w_lo, e - 1)
                load_expert(sp, io, LAYER1_EXPERTS, e, raw[i], w_loaded[i])
                sp.wait_ge(mixed_done, (e - 1) * 2)
                load_spread(e, i)

            sp.dma_start(routers_raw[:, 0:E], io["L1_ffn_w_router"]).then_inc(r_loaded, 16)
            sp.dma_start(routers_raw[:, E:2 * E], io["L1_ffn_w_gating"]).then_inc(r_loaded, 16)
            turns(step, sp)
            for d in range(2):
                sp.wait_ge(x_done, 3 + d)
                sp.dma_start(out[d * HALF:(d + 1) * HALF, :].rearrange("(t p) d -> p t d", p=P),
                             g.x[:, d * HT:(d + 1) * HT, :]).then_inc(stored, 16)
            sp.wait_ge(stored, 32)

        @block.gpsimd
        def _(pool):
            def step(turn, i, drain=False):
                e = turn * 2 + i
                if not drain and ahead(turn, i):
                    wait(pool, up_done, e * UNITS)
                    for n in range(2):
                        pool.wait_ge(up_w_hi, (e + 1) * 2 + n + 1)
                        last = weight_low(pool, i + 1, n)
                    last.then_inc(up_w_lo, 1)
                if not first(turn, i) and not drain:
                    for d in range(2):
                        pool.wait_ge(mixed_done, (e - 1) * 2 + d + 1)
                        wait(pool, sum_done, (e - 2) * 2 + d + 1)
                        pool.tensor_tensor(total[:, half(d)], total[:, half(d)], mixed[d][:],
                                           ALU.add).then_inc(sum_done, 1)
                if not drain and ahead(turn, i):
                    wait(pool, down_done, e * 2)
                    pool.wait_ge(down_w_hi, e + 2)
                    weight_low(pool, i + 1, 2).then_inc(down_w_lo, 1)

            pool.memset(routers_raw[:, 2 * E:P], 0.0).then_inc(zeroed, 1)
            pool.wait_ge(var_done, 1)
            pool.tensor_tensor(rstd[:], var_eps[:], g.minus_half[:], ALU.pow).then_inc(rstd_done, 1)
            pool.wait_ge(down_w_hi, 1)
            weight_low(pool, 0, 2).then_inc(down_w_lo, 1)
            pool.memset(total[:], 0.0).then_inc(zeroed, 1)
            pool.wait_ge(zeroed, 2)
            turns(step, pool)

        @block.scalar
        def _(act):
            def split_weight(turn, i, n):
                e = turn * 2 + i
                if n == 0:
                    act.wait_ge(w_loaded[i % 2], (turn + i // 2) * 48 + 48)
                    wait(act, up_done, (e - 1) * UNITS)
                if n == 2:
                    wait(act, down_done, (e - 1) * 2)
                weight_high(act, i, n).then_inc(down_w_hi if n == 2 else up_w_hi, 1)

            def hidden_high(turn, i, u):
                act.wait_ge(mult_done, (turn * 2 + i) * UNITS + u + 1)
                act.copy(hid[i % 2].hi[:, u // 2, half(u % 2)], hidden[u % 2][:]).then_inc(hid_hi, 1)

            def step(turn, i, drain=False):
                e = turn * 2 + i
                for u in range(UNITS):
                    n = e * UNITS + u
                    early = u == UNITS - 1 and not drain and not ahead(turn, i)
                    if early:
                        hidden_high(turn, i, u - 1)
                    if not drain:
                        act.wait_ge(up_done, n + 1)
                        wait(act, mult_done, n - 1)
                        act.activation(silu[u % 2][:], up_bank(u, 0), ACT.Silu).then_inc(silu_done, 1)
                    if u == 0:
                        if not first(turn, i):
                            hidden_high(turn, i - 1, UNITS - 1)
                        if drain:
                            return
                    elif not early:
                        hidden_high(turn, i, u - 1)
                    if u in (2, 3, 4) and ahead(turn, i):
                        split_weight(turn, i + 1, (2, 3, 4).index(u))

            act.wait_ge(w_loaded[0], 48)
            for n in range(3):
                weight_high(act, 0, n).then_inc(down_w_hi if n == 2 else up_w_hi, 1)
            act.wait_ge(r_loaded, 32)
            act.wait_ge(zeroed, 1)
            act.copy(routers.hi, routers_raw[:]).then_inc(r_hi, 1)
            for d in range(2):
                act.wait_ge(turned, d + 1)
                act.copy(xnT.hi[:, half(d)], turned_ps(d)).then_inc(x_hi, 1)
            for d in range(2):
                act.wait_ge(logitsT_done, d + 1)
                act.copy(logitsT[:, half(d)], logitsT_ps(d)).then_inc(logitsT_out, 1)
            act.wait_ge(shifted, 1)
            act.activation(probs[:, :, 0, :], probs[:, :, 0, :], ACT.Exp)
            act.activation(probs[:, :, 1, :], probs[:, :, 1, :], ACT.Exp, scale=10.0).then_inc(exp_done, 1)
            turns(step, act)

        @block.vector
        def _(dve):
            chain = Chain(dve, g.dve_steps)

            def softmaxes(stage):
                if stage == 0:
                    dve.wait_ge(exp_done, 1)
                    chain(dve.tensor_reduce(sums[:], probs[:], AX.X, ALU.add))
                    chain(dve.reciprocal(rsums[:], sums[:]))
                if stage == 1:
                    chain(dve.tensor_tensor(probs[:], probs[:], rsums[:].unsqueeze(3).to_broadcast([P, TT, 2, E]), ALU.mult))
                    chain(dve.tensor_tensor(both[:], probs[:, :, 0, :], probs[:, :, 1, :], ALU.mult))
                    chain(dve.tensor_reduce(bsum[:], both[:], AX.X, ALU.add))
                if stage == 2:
                    chain(dve.tensor_scalar(bsum[:], bsum[:], 1e-9, None, ALU.add))
                    chain(dve.reciprocal(rbsum[:], bsum[:]))
                    chain(dve.tensor_scalar(rbsum[:], rbsum[:], g.gates[:, 3:4], None, ALU.mult))
                    dve.tensor_tensor(mix[:].rearrange("p e t -> p t e"), both[:],
                                      rbsum[:].unsqueeze(2).to_broadcast([P, TT, E]), ALU.mult).then_inc(mix_done, 1)
                if stage == 5:
                    dve.wait_ge(mix_turned, 1)
                    dve.tensor_copy(mixT[:], mixT_ps).then_inc(mixT_done, 1)

            def hidden_low(turn, i, u):
                dve.wait_ge(hid_hi, (turn * 2 + i) * UNITS + u + 1)
                dve.tensor_tensor(hid[i % 2].lo[:, u // 2, half(u % 2)], hidden[u % 2][:],
                                  f32(hid[i % 2].hi[:, u // 2, half(u % 2)]), ALU.subtract).then_inc(hid_lo, 1)

            def step(turn, i, drain=False):
                e = turn * 2 + i
                for u in range(UNITS):
                    n = e * UNITS + u
                    early = u == UNITS - 1 and not drain and not ahead(turn, i)
                    if early:
                        hidden_low(turn, i, u - 1)
                    if not drain:
                        dve.wait_ge(silu_done, n + 1)
                        wait(dve, hid_lo, n - 1)
                        dve.tensor_tensor(hidden[u % 2][:], silu[u % 2][:], up_bank(u, 1), ALU.mult).then_inc(mult_done, 1)
                    if u > 0 and not drain and not early:
                        hidden_low(turn, i, u - 1)
                    if u == 0 and not first(turn, i):
                        hidden_low(turn, i - 1, UNITS - 1)
                    if first(turn, i):
                        softmaxes(u)
                    if u in (2, 4) and not first(turn, i):
                        d = (u - 2) // 2
                        dve.wait_ge(down_done, (e - 1) * 2 + d + 1)
                        dve.wait_ge(spread_loaded[(i - 1) % 2], (turn + i) * 16)
                        wait(dve, sum_done, (e - 2) * 2 + d + 1)
                        dve.tensor_tensor(mixed[d][:], down_bank(d), spread[(i - 1) % 2][:, half(d)],
                                          ALU.mult).then_inc(mixed_done, 1)

            layernorm_stats(dve, chain, g.x, stats, moments, (TT - 1,))
            layernorm_variance(dve, moments, var_eps).then_inc(var_done, 1)
            dve.wait_ge(w_loaded[0], 48)
            for n in range(2):
                dve.wait_ge(up_w_hi, n + 1)
                last = weight_low(dve, 0, n)
            last.then_inc(up_w_lo, 1)
            dve.wait_ge(r_loaded, 32)
            dve.wait_ge(r_hi, 1)
            dve.tensor_tensor(routers.lo, routers_raw[:], f32(routers.hi), ALU.subtract).then_inc(r_lo, 1)
            dve.wait_ge(rstd_done, 1)
            layernorm_apply(dve, g.x, moments, rstd, xn, xn_done)
            for d in range(2):
                dve.wait_ge(x_hi, d + 1)
                dve.tensor_tensor(xnT.lo[:, half(d)], turned_ps(d), f32(xnT.hi[:, half(d)]),
                                  ALU.subtract).then_inc(x_lo, 1)
            dve.wait_ge(logits_done, 1)
            chain(dve.tensor_reduce(top[:], logits_ps, AX.X, ALU.max))
            dve.tensor_tensor(probs[:], logits_ps, top[:].unsqueeze(3).to_broadcast([P, TT, 2, E]),
                              ALU.subtract).then_inc(shifted, 1)
            turns(step, dve)
            for n in range(4):
                dve.wait_ge(back_done, n + 1)
                wait(dve, x_done, n - 1)
                rows = g.x[:, n % 2 * HT:(n % 2 + 1) * HT, :]
                dve.tensor_tensor(rows, g.psum[:, n, :].rearrange("p (t d) -> p t d", d=D), rows,
                                  ALU.add).then_inc(x_done, 1)

        @block.tensor
        def _(pe):
            def step(turn, i, drain=False):
                e = turn * 2 + i
                if not drain:
                    pe.wait_ge(up_w_lo, e + 1)
                for u in range(UNITS):
                    n = e * UNITS + u
                    if not drain:
                        wait(pe, mult_done, n - 1 if u in (2, 3) else n - 2)
                        for which in range(2):
                            f = u // 2
                            last = matmul3(pe, up_bank(u, which), parts[i][which][:, f * P:(f + 1) * P],
                                           xnT[:, half(u % 2)])
                        last.then_inc(up_done, 1)
                    if first(turn, i) and u == 0:
                        pe.wait_ge(logitsT_out, 2)
                        for t in range(TT):
                            last = pe.transpose(logits_ps[:, t].rearrange("p r e -> p (r e)"),
                                                logitsT[:, t * P:(t + 1) * P], g.ident[0:2 * E, 0:2 * E])
                        last.then_inc(logits_done, 1)
                    if first(turn, i) and u == 4:
                        pe.wait_ge(mix_done, 1)
                        pe.transpose(mixT_ps, mix[:].rearrange("p e t -> p (e t)"), g.ident[:]).then_inc(mix_turned, 1)
                    if u in (1, 3) and not first(turn, i):
                        d = (u - 1) // 2
                        pe.wait_ge(down_w_lo, e)
                        if first(turn, i - 1):
                            pe.wait_ge(mixT_done, 1)
                        wait(pe, mixed_done, (e - 2) * 2 + d + 1)
                        for f in range(FT):
                            pe.wait_ge(hid_lo, (e - 1) * UNITS + 2 * f + d + 1)
                            last = matmul3(pe, down_bank(d), parts[(i - 1) % 2][2][:, f * D:(f + 1) * D],
                                           hid[(i - 1) % 2][:, f, half(d)], start=f == 0, stop=f == FT - 1)
                        last.then_inc(down_done, 1)

            for t in range(TT):
                pe.wait_ge(xn_done, t + 1)
                last = pe.transpose(turned_ps(t // HT)[:, t % HT * P:(t % HT + 1) * P], xn[:, t, :], g.ident[:])
                if t % HT == HT - 1:
                    last.then_inc(turned, 1)
            pe.wait_ge(r_lo, 1)
            for d in range(2):
                pe.wait_ge(x_lo, d + 1)
                matmul3(pe, g.psum[:, 6 + d, :], routers, xnT[:, half(d)]).then_inc(logitsT_done, 1)
            turns(step, pe)
            pe.wait_ge(mult_done, E * UNITS)
            for d in range(2):
                pe.wait_ge(sum_done, (E - 2) * 2 + d + 1)
                for t in range(HT):
                    at = d * HALF + t * P
                    last = pe.transpose(g.psum[:, d, t * P:(t + 1) * P], total[:, at:at + P], g.ident[:])
                last.then_inc(back_done, 1)
            for d in range(2):
                pe.wait_ge(mixed_done, (E - 1) * 2 + d + 1)
                for t in range(HT):
                    last = pe.transpose(g.psum[:, 2 + d, t * P:(t + 1) * P], mixed[d][:, t * P:(t + 1) * P], g.ident[:])
                last.then_inc(back_done, 1)


def alloc(core, nc):
    class Shared:
        pass

    g = Shared()
    g.psum = core.stack.enter_context(nc.psum_tensor("ps_all", [P, 8, BANK], F32))
    g.x = core.sb("x", [P, TT, D])
    g.attended = core.sb("attended", [P, TT * D])
    g.stats, g.moments = core.sb("ln_stats", [P, TT, 6]), core.sb("ln_moments", [P, TT, 2])
    g.ident = core.sb("ident", [P, P])
    g.zeros = core.sb("zeros", [P, 4 * D])
    g.minus_half = core.sb("minus_half", [P, TT])
    g.bias0 = core.sb("bias0", [P, D])
    g.bias1 = core.sb("bias1", [P, D])
    g.gates = core.sb("gates", [P, 4])
    g.expert_w = [[core.sb(f"expert_w{i}_{n}", [P, F]) for n in range(3)] for i in range(2)]
    flat = [w for pair in g.expert_w for w in pair]
    g.weights1 = [flat[0:2], flat[2:4], flat[4:6]]
    g.weights1_loaded = [core.sem(f"ld_weights1_{j}") for j in range(3)]
    g.expert_rows = [core.sb(f"expert_rows{i}", [P, NSLOT, D]) for i in range(2)]
    g.expert_rows_loaded = [core.sem(f"ld_expert_rows{i}") for i in range(2)]
    g.expert_w_loaded = [core.sem(f"ld_expert0_{i}") for i in range(2)]
    g.expert_w2_loaded = [core.sem(f"ld_expert0_down{i}") for i in range(2)]
    g.expert1_w_loaded = [core.sem(f"ld_expert1_{i}") for i in range(2)]
    g.gather_at = core.sb("gather_at", [P, TOPK, TT], U32)
    g.token_weights = core.sb("token_weights", [P, TOPK, TT])
    g.ctxT = core.split("ctxT", [C, KEYS])
    g.expert_in = nc.dram_tensor("expert_in", [SLOTS, D], F32, kind="Internal").ap()
    g.expert_out = nc.dram_tensor("expert_out", [SLOTS, D], F32, kind="Internal").ap()
    g.values1 = nc.dram_tensor("values1", [B, H1 * M, D], F32, kind="Internal").ap()
    g.mix = nc.dram_tensor("mix", [E, T], F32, kind="Internal").ap()
    g.experts_stored = [core.sem(f"experts_stored{i}") for i in range(2)]
    g.dve_steps = Steps(core.sem("dve_steps"))
    g.values_loaded = [core.sem(f"values_loaded{i}") for i in range(2)]
    g.expert_in_zeroed = core.sem("expert_in_zeroed")
    return g


def flamingo(nc, io, out):
    io = dict(io)
    io["x"] = io["x"].rearrange("b s d -> (b s) d")
    io["ctx"] = io["ctx_768"].rearrange("b m c -> (b m) c")
    with ExitStack() as stack:
        core = Core(nc, stack)
        g = alloc(core, nc)
        with ExitStack() as layer0:
            c0 = core.scope(layer0)
            g.xnT = c0.split("xnT", [D, T])
            g.keys0 = c0.split("keys0", [D, H0, KEYS])
            g.values0 = c0.split("values0", [P, KT, H0 * D])
            prepare0(core, g, io)
            attention0(core, g, io)
        with ExitStack() as layer1:
            c1 = core.scope(layer1)
            g.keys1 = c1.split("keys1", [D, B, H1, M])
            g.vo1 = c1.split("vo1", [C, H1, D])
            dispatch(core, g, io)
            experts0(core, g, io)
            g.xn1T = c1.split("xn1T", [D, T])
            g.raw_values = [c1.sb(f"vraw{i}", [P, NT1, D]) for i in range(2)]
            combine(core, g, io)
            attention1(core, g, io)
        experts1(core, g, io, out.rearrange("b s d -> (b s) d"))


_INS = ["x", "ctx_768", "g_xattn", "g_ffn",
        "L0_xattn_Wq", "L0_xattn_Wk", "L0_xattn_Wv", "L0_xattn_Wout", "L0_xattn_bout",
        "L0_ffn_Wr", "L0_ffn_W1", "L0_ffn_W3", "L0_ffn_W2",
        "L1_xattn_Wq", "L1_xattn_Wk", "L1_xattn_Wv", "L1_xattn_Wo", "L1_xattn_bo",
        "L1_ffn_w_router", "L1_ffn_w_gating", "L1_ffn_w_gate", "L1_ffn_w_up", "L1_ffn_w_down"]


def kernel(**inputs):
    import concourse.bacc as _bacc
    from concourse.bass_utils import run_bass_kernel_spmd as _run

    nc = _bacc.Bacc("TRN2", target_bir_lowering=False, num_devices=1)
    arrays, io = {}, {}
    for name in _INS:
        a = np.ascontiguousarray(inputs[name])
        arrays[f"in_{name}_dram"] = a
        io[name] = nc.dram_tensor(f"in_{name}_dram", a.shape, mybir.dt.from_np(a.dtype), kind="ExternalInput").ap()
    out = nc.dram_tensor("out_dram", (B, S, D), F32, kind="ExternalOutput").ap()
    flamingo(nc, io, out)
    r = _run(nc, [arrays], core_ids=[0])
    return r.results[0]["out_dram"]
```
